# Optimizing a Trainium2 kernel written in Bass

```python
import numpy as np
import jax
import jax.numpy as jnp

def _softmax(x, axis=-1):
    return jax.nn.softmax(x, axis=axis)

def _gelu(x):
    return jax.nn.gelu(x, approximate=True)

def _silu(x):
    return jax.nn.silu(x)

def _sigmoid(x):
    return jax.nn.sigmoid(x)

def _layernorm(x, axis=-1, eps=1e-05):
    m = jnp.mean(x, axis=axis, keepdims=True)
    v = jnp.var(x, axis=axis, keepdims=True)
    return (x - m) / jnp.sqrt(v + eps)

def _scatter_add(tgt, idx, src, axis=0):
    return tgt.at[idx].add(src)

def _segment_sum(src, seg, n):
    return jax.ops.segment_sum(src, seg, n)
kernel_name = 'mk_gnn_ffn_d1_gnn_r8_c32a12'

def setup_inputs(seed: int=0):
    np.random.seed(seed)
    _w = jnp.asarray

    def _rec_inputs():
        import jax
        import jax.numpy as jnp
        _gk = jax.random.key(seed)
        x = -0.0001126 + 1 * jax.random.normal(jax.random.fold_in(_gk, 1), (3750, 256), jnp.float32)
        src = jax.random.randint(jax.random.fold_in(_gk, 2), (60000,), 0, 3750, jnp.int32)
        dst = jnp.minimum((3750 * jax.random.uniform(jax.random.fold_in(_gk, 3), (60000,)) ** 2.0).astype(jnp.int32), 29999)
        _o = jnp.argsort(dst, stable=True)
        src = src[_o]
        dst = dst[_o]
        edge_type_8 = jax.random.randint(jax.random.fold_in(_gk, 12), (60000,), 0, 8, jnp.int32)
        return (x, src, dst, edge_type_8)
    x, src, dst, edge_type_8 = _rec_inputs()

    def _L0_gnn_setup():
        import jax, jax.numpy as jnp
        import numpy as np
        N_NODES = 3750
        N_EDGES = 60000
        IN_FEAT = 256
        OUT_FEAT = 256
        N_RELS = 8
        N_HEADS = 4
        HEAD_DIM = OUT_FEAT // N_HEADS
        LEAKY_SLOPE = 0.2
        key = jax.random.key(seed)
        ks = jax.random.split(key, 8)
        inputs = jax.random.normal(ks[0], (N_NODES, IN_FEAT), dtype=jnp.float32)
        conv_weights = jax.random.normal(ks[1], (N_RELS, N_HEADS, IN_FEAT, HEAD_DIM), dtype=jnp.float32) * (1.0 / np.sqrt(IN_FEAT))
        attn_l = jax.random.normal(ks[2], (N_RELS, N_HEADS, HEAD_DIM), dtype=jnp.float32) * 0.1
        attn_r = jax.random.normal(ks[3], (N_RELS, N_HEADS, HEAD_DIM), dtype=jnp.float32) * 0.1
        h_bias = jax.random.normal(ks[4], (OUT_FEAT,), dtype=jnp.float32) * 0.02
        edge_src = jax.random.randint(ks[5], (N_EDGES,), 0, N_NODES, dtype=jnp.int32)
        edge_dst = jax.random.randint(ks[6], (N_EDGES,), 0, N_NODES, dtype=jnp.int32)
        edge_type = jax.random.randint(ks[7], (N_EDGES,), 0, N_RELS, dtype=jnp.int32)
        return {'inputs': inputs, 'conv_weights': conv_weights, 'attn_l': attn_l, 'attn_r': attn_r, 'h_bias': h_bias, 'edge_src': edge_src, 'edge_dst': edge_dst, 'edge_type': edge_type}
    _L0_gnn_all = _L0_gnn_setup()
    _L0_gnn_in = {k: v for k, v in _L0_gnn_all.items() if k in ('conv_weights', 'attn_l', 'attn_r', 'h_bias')}
    del _L0_gnn_all

    def _L0_ffn_setup():
        import jax, jax.numpy as jnp
        import numpy as np
        NUM_EXPERTS = 8
        TOP_K = 2
        B, S, D = (8, 1024, 256)

        def _moe(tokens, router_w, w1, b1, w2, b2):
            N = tokens.shape[0]
            E = router_w.shape[0]
            logits = tokens.astype(jnp.float32) @ router_w.astype(jnp.float32).T
            probs = jax.nn.softmax(logits, axis=-1)
            rw, re = jax.lax.top_k(probs, TOP_K)
            if TOP_K > 1:
                rw = rw / jnp.maximum(rw.sum(-1, keepdims=True), 1e-12)
            rw = rw.astype(tokens.dtype)
            combine = jnp.zeros((N, E), tokens.dtype).at[jnp.arange(N)[:, None], re].set(rw)
            out = tokens
            for e in range(E):
                h = jax.nn.gelu(tokens @ w1[e] + b1[e], approximate=False)
                y = h @ w2[e] + b2[e]
                out = out + combine[:, e:e + 1] * y
            return out
        key = jax.random.key(seed)
        ks = jax.random.split(key, 4)
        scale = 1.0 / np.sqrt(D).astype(np.float32)
        return {'input_embeddings': jax.random.normal(ks[0], (B, S, D), jnp.float32), 'router_w': jax.random.normal(ks[1], (NUM_EXPERTS, D), jnp.float32) * scale, 'w1': jax.random.normal(ks[2], (NUM_EXPERTS, D, D), jnp.float32) * scale, 'b1': jnp.zeros((NUM_EXPERTS, D), jnp.float32), 'w2': jax.random.normal(ks[3], (NUM_EXPERTS, D, D), jnp.float32) * scale, 'b2': jnp.zeros((NUM_EXPERTS, D), jnp.float32)}
    _L0_ffn_all = _L0_ffn_setup()
    _L0_ffn_in = {k: v for k, v in _L0_ffn_all.items() if k in ('router_w', 'w1', 'b1', 'w2', 'b2')}
    del _L0_ffn_all
    return {'x': x, 'src': src, 'dst': dst, 'edge_type_8': edge_type_8, 'L0_gnn_conv_weights': _L0_gnn_in['conv_weights'], 'L0_gnn_attn_l': _L0_gnn_in['attn_l'], 'L0_gnn_attn_r': _L0_gnn_in['attn_r'], 'L0_gnn_h_bias': _L0_gnn_in['h_bias'], 'L0_ffn_router_w': _L0_ffn_in['router_w'], 'L0_ffn_w1': _L0_ffn_in['w1'], 'L0_ffn_b1': _L0_ffn_in['b1'], 'L0_ffn_w2': _L0_ffn_in['w2'], 'L0_ffn_b2': _L0_ffn_in['b2']}

def reference(x, src, dst, edge_type_8, L0_gnn_conv_weights, L0_gnn_attn_l, L0_gnn_attn_r, L0_gnn_h_bias, L0_ffn_router_w, L0_ffn_w1, L0_ffn_b1, L0_ffn_w2, L0_ffn_b2):
    import jax
    import jax.numpy as jnp

    def _L0_gnn_ref(inputs, conv_weights, attn_l, attn_r, h_bias, edge_src, edge_dst, edge_type):
        import jax, jax.numpy as jnp
        import numpy as np
        N_NODES = 3750
        N_EDGES = 60000
        IN_FEAT = 256
        OUT_FEAT = 256
        N_RELS = 8
        N_HEADS = 4
        HEAD_DIM = OUT_FEAT // N_HEADS
        LEAKY_SLOPE = 0.2
        feat_all = jnp.einsum('ni,rhid->rnhd', inputs, conv_weights)
        feat_src_e = feat_all[edge_type, edge_src]
        feat_dst_e = feat_all[edge_type, edge_dst]
        el = jnp.sum(feat_src_e * attn_l[edge_type], axis=-1)
        er = jnp.sum(feat_dst_e * attn_r[edge_type], axis=-1)
        e = jax.nn.leaky_relu(el + er, negative_slope=LEAKY_SLOPE)
        m = jax.ops.segment_max(e, edge_dst, num_segments=N_NODES)
        ex = jnp.exp(e - m[edge_dst])
        denom = jax.ops.segment_sum(ex, edge_dst, num_segments=N_NODES)
        alpha = ex / denom[edge_dst]
        h = jax.ops.segment_sum(alpha[..., None] * feat_src_e, edge_dst, num_segments=N_NODES)
        h = h.reshape(N_NODES, OUT_FEAT) + h_bias
        return h

    def _L0_ffn_ref(input_embeddings, router_w, w1, b1, w2, b2):
        import jax, jax.numpy as jnp
        import numpy as np
        NUM_EXPERTS = 8
        TOP_K = 2
        B, S, D = (8, 1024, 256)

        def _moe(tokens, router_w, w1, b1, w2, b2):
            N = tokens.shape[0]
            E = router_w.shape[0]
            logits = tokens.astype(jnp.float32) @ router_w.astype(jnp.float32).T
            probs = jax.nn.softmax(logits, axis=-1)
            rw, re = jax.lax.top_k(probs, TOP_K)
            if TOP_K > 1:
                rw = rw / jnp.maximum(rw.sum(-1, keepdims=True), 1e-12)
            rw = rw.astype(tokens.dtype)
            combine = jnp.zeros((N, E), tokens.dtype).at[jnp.arange(N)[:, None], re].set(rw)
            out = tokens
            for e in range(E):
                h = jax.nn.gelu(tokens @ w1[e] + b1[e], approximate=False)
                y = h @ w2[e] + b2[e]
                out = out + combine[:, e:e + 1] * y
            return out
        b, s, d = input_embeddings.shape
        tokens = input_embeddings.reshape(b * s, d)
        return _moe(tokens, router_w, w1, b1, w2, b2).reshape(b, s, d)
    x = x + _L0_gnn_ref(_layernorm(x, axis=-1), L0_gnn_conv_weights, L0_gnn_attn_l, L0_gnn_attn_r, L0_gnn_h_bias, src, dst, edge_type_8)
    x = x + _L0_ffn_ref(_layernorm(x, axis=-1)[None], L0_ffn_router_w, L0_ffn_w1, L0_ffn_b1, L0_ffn_w2, L0_ffn_b2)[0]
    return x

_drawn_inputs = setup_inputs


def setup_inputs(seed=0):
    import zlib

    import numpy as np

    out = dict(_drawn_inputs(seed))
    spreads = {'L0_ffn_b1': (0.0, 0.336), 'L0_ffn_b2': (0.0, 0.1)}
    factors = {}
    for name, (base, spread) in spreads.items():
        noise = np.random.default_rng([zlib.crc32(name.encode()), seed]).standard_normal(out[name].shape)
        drawn = base * np.exp(spread * noise) if base else spread * noise
        out[name] = jnp.asarray(drawn.astype(out[name].dtype))
    for name, factor in factors.items():
        out[name] = (out[name] * factor).astype(out[name].dtype)
    return out
```

```python
from contextlib import ExitStack

import numpy as np

import concourse.bass as bass
from concourse import mybir

F32, BF16, I32, U32 = mybir.dt.float32, mybir.dt.bfloat16, mybir.dt.int32, mybir.dt.uint32
ALU = mybir.AluOpType
ACT = mybir.ActivationFunctionType
AX = mybir.AxisListType.X

P = 128
BIG = 1.0e30


class Chain:

    def __init__(self, eng, sem):
        self.eng, self.sem, self.n = eng, sem, 0

    def __call__(self, ins):
        ins.then_inc(self.sem, 1)
        self.n += 1
        self.eng.wait_ge(self.sem, self.n)

    def put(self, ins):
        ins.then_inc(self.sem, 1)
        self.n += 1

    def sync(self):
        self.eng.wait_ge(self.sem, self.n)


def gnn_moe(nc, x, src, dst, etype, conv_w, attn_l, attn_r, h_bias, router_w, w1, b1, w2, b2, out, dbg=None):
    N, D = x.shape
    E = src.shape[0]
    R, H, _, HD = conv_w.shape
    RH = R * H
    X = router_w.shape[0]
    KD = D // P
    NW = -(-N // P)
    NP = NW * P
    FULL = N // P
    REST = N - FULL * P
    T = -(-E // P)
    TF = E // P
    TREST = E - TF * P
    PAD_TILE = T
    PAIRS = (T + NW - 1 + NW) // 2
    HALF = 12
    RING = 2 * HALF
    QUADS = 4
    SLOTS = -(-2 * PAIRS // (QUADS * HALF)) * QUADS * HALF
    PAIRS = SLOTS // 2
    ITERS = SLOTS // RING
    QITERS = SLOTS // (QUADS * HALF)
    SB = -(-SLOTS // P)
    ROW = D + H
    CP = 120
    assert E % CP == 0 and D == 2 * P and NW % 6 == 0
    EPS = 1e-5

    edges = nc.dram_tensor("edge_tiles", [T + 1, 3 * P], I32, kind="Internal").ap()
    feat = nc.dram_tensor("node_features", [NP, R * D], F32, kind="Internal").ap()
    eltab = nc.dram_tensor("source_logits", [NP, RH], F32, kind="Internal").ap()
    ertab = nc.dram_tensor("target_logits", [NP, RH], F32, kind="Internal").ap()
    feat_rows = feat.rearrange("n (r d) -> (n r) d", r=R)
    el_rows = eltab.rearrange("n (r h) -> (n r) h", r=R)
    er_rows = ertab.rearrange("n (r h) -> (n r) h", r=R)
    col = lambda a: a.rearrange("(a d) -> a d", a=1)

    with ExitStack() as ctx:
        def sb(name, shape, dt, c=ctx):
            return c.enter_context(nc.sbuf_tensor(name, shape, dt))

        def pb(name, c, shape=(P, 512), dt=F32):
            return c.enter_context(nc.psum_tensor(name, list(shape), dt))

        def sem(name):
            return ctx.enter_context(nc.semaphore(name))

        ident = sb("ident", [P, P], F32)
        iota_f = sb("iota_f", [P, P], F32)
        xb = sb("xb", [P, NW, D], F32)
        el_idx = sb("el_idx", [P, SB * P], I32)
        er_idx = sb("er_idx", [P, SB * P], I32)
        dloc = sb("dloc", [P, SB * P], F32)
        e_all = sb("e_all", [P, SB * P, H], F32)
        keys = sb("keys", [P, SB, P], F32)
        pair0 = sb("pair0", [1, NW + 2], I32)
        zero_i = sb("zero_i", [P, HALF], I32)
        zero16 = sb("zero16", [1, ROW], BF16)
        zrow = sb("zrow", [P, 1], F32)
        epsv = sb("epsv", [P, 1], F32)

        st1 = ExitStack()
        with st1:
            xt = xb
            xn = sb("xn", [P, NW, D], F32, st1)
            xnT = sb("xnT", [P, KD, NP], F32, st1)
            wsb = sb("wsb", [P, KD, R, D], F32, st1)
            wa = sb("wa", [P, KD, 2, RH], F32, st1)
            with ExitStack() as c1:
                dst_i = sb("dst_i", [CP, E // CP], I32, c1)
                dst_f = sb("dst_f", [CP, E // CP], F32, c1)
                cmp = sb("cmp", [CP, E // CP], F32, c1)
                cnt = sb("cnt", [CP, NW - 1], F32, c1)
                ones = sb("ones", [P, P], F32, c1)
                sti = sb("sti", [P, 4, NW + 1], I32, c1)
                stf = sb("stf", [P, 6, NW + 1], F32, c1)
                slot_id = sb("slot_id", [P, SB, 1], F32, c1)
                ge = sb("ge", [P, SB, NW - 1], F32, c1)
                ged = sb("ged", [P, SB, NW - 1], F32, c1)
                win = sb("win", [P, SB], F32, c1)
                tile_f = sb("tile_f", [P, SB], F32, c1)
                tile_i = sb("tile_i", [P, SB], I32, c1)
                wtmp = sb("wtmp", [P, R * D], F32, c1)
                att = sb("att", [P, 2, R * D], F32, c1)
                padr = sb("padr", [2, 3 * P], I32, c1)
                eg = sb("eg", [P, SB, 3 * P], I32, c1)
                ef = sb("ef", [P, SB, 3, P], F32, c1)
                ix = sb("ix", [P, SB, 3, P], F32, c1)
                stat = sb("stat", [P, NW, 6], F32, c1)
                mv = sb("mv", [P, NW, 2], F32, c1)
                rstd = sb("rstd", [P, NW], F32, c1)
                std = sb("std", [P, NW], F32, c1)
                hb = sb("hb", [P, D], F32, c1)
                lts = sb("lts", [P, NW, 2 * RH], F32, c1)

                psc = pb("psc", c1)
                pst = [pb(f"pst{i}", c1) for i in range(4)]
                psl = [pb(f"psl{i}", c1) for i in range(2)]

                s_const = sem("constants_ready")
                s_ident = sem("identity_ready")
                s_dst = sem("dst_loaded")
                s_x = sem("x_loaded")
                s_w = sem("weights_loaded")
                s_att = sem("attention_loaded")
                s_pad = sem("pad_rows_ready")
                s_et = sem("edge_tiles_stored")
                s_dv = sem("vector_steps_1")
                s_cnt = sem("counts_ready")
                s_cntp = sem("counts_summed")
                s_tile = sem("slot_tiles_ready")
                s_eg = sem("slot_edges_gathered")
                s_ix = sem("slot_indices_ready")
                s_tp = sem("transposes_done_1")
                s_te = sem("transposes_copied_1")
                s_var = sem("variance_ready")
                s_std = sem("std_ready")
                s_xn = sem("xn_ready")
                s_wa = sem("attention_folded")
                s_lt = sem("logits_done")
                s_le = sem("logits_copied")
                s_ls = sem("logit_tables_stored")
                s_p0 = sem("pair_bounds_ready")

                with nc.Block() as block:
                    @block.sync
                    def _(eng):
                        eng.dma_start(dst_i[:, :], dst.rearrange("(p f) -> p f", p=CP)).then_inc(s_dst, 16)
                        eng.wait_ge(s_const, 1)
                        eng.dma_start(xt[:, 0:FULL, :],
                                      x[0:FULL * P, :].rearrange("(t p) f -> p t f", p=P)).then_inc(s_x, 16)
                        eng.dma_start(xt[0:REST, FULL, :], x[FULL * P:N, :]).then_inc(s_x, 16)
                        for n, a in enumerate((attn_l, attn_r)):
                            eng.dma_start(att[:, n, :], a.rearrange("r h d -> (r h d)").partition_broadcast(P))\
                               .then_inc(s_att, 16)
                        eng.dma_start(hb[:, :], h_bias.partition_broadcast(P)).then_inc(s_att, 16)
                        eng.wait_ge(s_le, NW)
                        for n, tab in enumerate((eltab, ertab)):
                            eng.dma_start(tab.rearrange("(t p) c -> p t c", p=P),
                                          lts[:, :, n * RH:(n + 1) * RH]).then_inc(s_ls, 16)
                        eng.wait_ge(s_ls, 32)

                    @block.gpsimd
                    def _(eng):
                        eng.memset(xt[:, FULL, :], 0.0).then_inc(s_const, 1)
                        eng.memset(ident[:, :], 0.0).then_inc(s_const, 1)
                        eng.memset(zero16[:, :], 0.0).then_inc(s_const, 1)
                        eng.memset(zero_i[:, :], 0).then_inc(s_const, 1)
                        eng.memset(zrow[:, :], 0.0).then_inc(s_const, 1)
                        eng.memset(epsv[:, :], EPS).then_inc(s_const, 1)
                        eng.memset(ones[:, :], 1.0).then_inc(s_const, 1)
                        eng.iota(iota_f[:, :], pattern=[[1, P]], base=0, channel_multiplier=0,
                                 allow_small_or_imprecise_dtypes=True).then_inc(s_const, 1)
                        eng.iota(slot_id[:, :, :], pattern=[[P, SB], [1, 1]], base=0, channel_multiplier=1,
                                 allow_small_or_imprecise_dtypes=True).then_inc(s_const, 1)
                        eng.memset(padr[:, 0:2 * P], 0).then_inc(s_pad, 1)
                        eng.memset(padr[:, 2 * P:3 * P], -1).then_inc(s_pad, 1)
                        eng.wait_ge(s_const, 9)
                        eng.affine_select(out=ident[:, :], in_=ident[:, :], compare_op=ALU.not_equal, fill=1.0,
                                          base=0, pattern=[[-1, P]], channel_multiplier=1).then_inc(s_ident, 1)
                        eng.wait_ge(s_tile, 1)
                        eng.wait_ge(s_et, 8 * 16)
                        for k in range(SB):
                            eng.indirect_dma_start(eg[:, k, :], None, edges[:, :],
                                                   bass.IndirectOffsetOnAxis(ap=tile_i[:, k:k + 1], axis=0))\
                               .then_inc(s_eg, 16)
                        eng.wait_ge(s_eg, 16 * SB)

                    @block.scalar
                    def _(eng):
                        for n, a in enumerate((src, etype, dst)):
                            eng.dma_start(edges[0:TF, n * P:(n + 1) * P],
                                          a[0:TF * P].rearrange("(t e) -> t e", e=P)).then_inc(s_et, 16)
                            eng.dma_start(edges[TF:TF + 1, n * P:n * P + TREST],
                                          col(a[TF * P:E])).then_inc(s_et, 16)
                        eng.wait_ge(s_pad, 2)
                        eng.dma_start(edges[TF:TF + 1, :].rearrange("a (n e) -> a n e", e=P)[:, :, TREST:P],
                                      padr[0:1, :].rearrange("a (n e) -> a n e", e=P)[:, :, TREST:P])\
                           .then_inc(s_et, 16)
                        eng.dma_start(edges[T:T + 1, :], padr[1:2, :]).then_inc(s_et, 16)
                        for kh in range(KD):
                            for r in range(R):
                                eng.dma_start(wsb[:, kh, r, :].rearrange("p (h d) -> p h d", h=H),
                                              conv_w[r, :, kh * P:(kh + 1) * P, :].rearrange("h k d -> k h d"))\
                                   .then_inc(s_w, 16)
                        eng.wait_ge(s_var, 1)
                        eng.activation(std[:, :], mv[:, :, 1], ACT.Sqrt, bias=epsv[:, 0:1]).then_inc(s_std, 1)
                        for t in range(NW):
                            eng.wait_ge(s_tp, t + 1)
                            eng.copy(xnT[:, :, t * P:(t + 1) * P],
                                     pst[t % 4][:, 0:2 * P].rearrange("p (k n) -> p k n", k=KD)).then_inc(s_te, 1)
                        for t in range(NW):
                            eng.wait_ge(s_lt, t + 1)
                            eng.copy(lts[:, t, :], psl[t % 2][:, 0:2 * RH]).then_inc(s_le, 1)
                        for k in range(SB):
                            eng.wait_ge(s_tp, NW + k + 1)
                            b = pst[(NW + k) % 4]
                            eng.copy(el_idx[:, k * P:(k + 1) * P], b[:, 0:P])
                            eng.copy(er_idx[:, k * P:(k + 1) * P], b[:, P:2 * P])
                            eng.copy(dloc[:, k * P:(k + 1) * P], b[:, 2 * P:3 * P]).then_inc(s_te, 1)
                        eng.wait_ge(s_et, 8 * 16)
                        eng.wait_ge(s_w, 16 * KD * R)
                        eng.wait_ge(s_te, NW + SB)

                    @block.tensor
                    def _(eng):
                        eng.wait_ge(s_const, 9)
                        eng.wait_ge(s_cnt, 1)
                        eng.matmul(psc[:, 0:NW - 1], ones[0:CP, :], cnt[:, :], start=True, stop=True)\
                           .then_inc(s_cntp, 1)
                        eng.wait_ge(s_ident, 1)
                        for t in range(NW):
                            eng.wait_ge(s_xn, t + 1)
                            if t >= 4:
                                eng.wait_ge(s_te, t - 3)
                            for k in range(KD):
                                tr = eng.transpose(pst[t % 4][:, k * P:(k + 1) * P],
                                                   xn[:, t, k * P:(k + 1) * P], ident[:, :])
                            tr.then_inc(s_tp, 1)
                        eng.wait_ge(s_wa, 1)
                        for t in range(NW):
                            eng.wait_ge(s_te, t + 1)
                            if t >= 2:
                                eng.wait_ge(s_le, t - 1)
                            for k in range(KD):
                                mm = eng.matmul(psl[t % 2][:, 0:2 * RH], xnT[:, k, t * P:(t + 1) * P],
                                                wa[:, k, :, :].rearrange("p a c -> p (a c)"),
                                                start=(k == 0), stop=(k == KD - 1))
                            mm.then_inc(s_lt, 1)
                        eng.wait_ge(s_ix, 1)
                        for k in range(SB):
                            eng.wait_ge(s_te, NW + k - 3)
                            for n in range(3):
                                tr = eng.transpose(pst[(NW + k) % 4][:, n * P:(n + 1) * P], ix[:, k, n, :],
                                                   ident[:, :])
                            tr.then_inc(s_tp, 1)

                    @block.vector
                    def _(eng):
                        do = Chain(eng, s_dv)
                        eng.wait_ge(s_dst, 16)
                        do(eng.tensor_copy(dst_f[:, :], dst_i[:, :]))
                        for w in range(1, NW):
                            do.put(eng.tensor_scalar(cmp[:, :], dst_f[:, :], float(w * P), 0.0, ALU.is_lt, ALU.add,
                                                     accum_out=cnt[:, w - 1:w]))
                            do.sync()
                        eng.engine_nop().then_inc(s_cnt, 1)
                        eng.wait_ge(s_x, 32)
                        for t in range(NW):
                            do.put(eng.bn_stats(stat[:, t, :], xt[:, t, :]))
                        do.sync()
                        for t in range(NW):
                            do.put(eng.bn_aggr(mv[:, t, :], stat[:, t, :]))
                        do.sync()
                        eng.engine_nop().then_inc(s_var, 1)
                        eng.wait_ge(s_cntp, 1)
                        do.put(eng.memset(stf[:, 0, 0:1], 0.0))
                        do.put(eng.memset(stf[:, 0, NW:NW + 1], float(E)))
                        do(eng.tensor_copy(stf[:, 0, 1:NW], psc[:, 0:NW - 1]))
                        do(eng.tensor_scalar(stf[:, 1, :], stf[:, 0, :], 1.0, None, ALU.subtract))
                        do.put(eng.tensor_copy(sti[:, 0, :], stf[:, 0, :]))
                        do(eng.tensor_copy(sti[:, 1, :], stf[:, 1, :]))
                        do(eng.tensor_scalar(sti[:, 2:4, :], sti[:, 0:2, :], 7, None, ALU.arith_shift_right))
                        do(eng.tensor_copy(stf[:, 2:4, :], sti[:, 2:4, :]))
                        do(eng.tensor_tensor(stf[:, 4, 0:NW], stf[:, 3, 1:NW + 1], stf[:, 2, 0:NW], ALU.subtract))
                        do(eng.tensor_scalar(stf[:, 4, 0:NW], stf[:, 4, 0:NW], 0.0, 2.0, ALU.max, ALU.add))
                        do(eng.tensor_copy(sti[:, 0, 0:NW], stf[:, 4, 0:NW]))
                        do(eng.tensor_scalar(sti[:, 0, 0:NW], sti[:, 0, 0:NW], 1, None, ALU.arith_shift_right))
                        do(eng.tensor_copy(stf[:, 4, 0:NW], sti[:, 0, 0:NW]))
                        do(eng.memset(stf[:, 5, :], 0.0))
                        do(eng.tensor_tensor_scan(stf[:, 1, 0:NW], stf[:, 4, 0:NW], stf[:, 5, 0:NW], 0.0,
                                                  ALU.add, ALU.add))
                        do(eng.tensor_copy(stf[:, 5, 1:NW], stf[:, 1, 0:NW - 1]))
                        do(eng.memset(stf[:, 5, NW:NW + 1], float(PAIRS)))
                        do(eng.tensor_copy(pair0[0:1, 0:NW + 1], stf[0:1, 5, :]))
                        do(eng.tensor_scalar(stf[:, 5, :], stf[:, 5, :], 2.0, None, ALU.mult))
                        do(eng.tensor_tensor(stf[:, 4, :], stf[:, 2, :], stf[:, 5, :], ALU.subtract))
                        do(eng.tensor_tensor(stf[:, 3, 1:NW], stf[:, 4, 1:NW], stf[:, 4, 0:NW - 1], ALU.subtract))
                        do(eng.tensor_tensor(ge[:, :, :], slot_id[:, :, :].to_broadcast([P, SB, NW - 1]),
                                             stf[:, 5:6, 1:NW].to_broadcast([P, SB, NW - 1]), ALU.is_ge))
                        do.put(eng.tensor_reduce(win[:, :], ge[:, :, :], AX, ALU.add))
                        do(eng.tensor_tensor(ged[:, :, :], ge[:, :, :],
                                             stf[:, 3:4, 1:NW].to_broadcast([P, SB, NW - 1]), ALU.mult))
                        do(eng.tensor_reduce(tile_f[:, :], ged[:, :, :], AX, ALU.add))
                        do(eng.tensor_tensor(tile_f[:, :], tile_f[:, :], slot_id[:, :, 0], ALU.add))
                        do.put(eng.tensor_scalar(tile_f[:, :], tile_f[:, :], float(PAD_TILE), 0.0, ALU.min, ALU.max))
                        do(eng.tensor_scalar(win[:, :], win[:, :], float(P), None, ALU.mult))
                        do(eng.tensor_copy(tile_i[:, :], tile_f[:, :]))
                        eng.engine_nop().then_inc(s_tile, 1)
                        eng.wait_ge(s_std, 1)
                        do(eng.reciprocal(rstd[:, :], std[:, :]))
                        for t in range(NW):
                            eng.tensor_scalar(xn[:, t, :], xt[:, t, :], mv[:, t, 0:1], rstd[:, t:t + 1],
                                              ALU.subtract, ALU.mult).then_inc(s_xn, 1)
                        eng.wait_ge(s_w, 16 * KD * R)
                        eng.wait_ge(s_att, 48)
                        for k in range(KD):
                            for n in range(2):
                                do(eng.tensor_tensor(wtmp[:, :], wsb[:, k, :, :].rearrange("p r d -> p (r d)"),
                                                     att[:, n, :], ALU.mult))
                                do(eng.tensor_reduce(wa[:, k, n, :], wtmp[:, :].rearrange("p (c d) -> p c d", d=HD),
                                                     AX, ALU.add))
                        eng.engine_nop().then_inc(s_wa, 1)
                        eng.wait_ge(s_eg, 16 * SB)
                        do(eng.tensor_copy(ef[:, :, :, :], eg[:, :, :].rearrange("p k (n e) -> p k n e", n=3)))
                        do.put(eng.scalar_tensor_tensor(ix[:, :, 0, :], ef[:, :, 0, :], float(R), ef[:, :, 1, :],
                                                        ALU.mult, ALU.add))
                        do(eng.scalar_tensor_tensor(ix[:, :, 1, :], ef[:, :, 2, :], float(R), ef[:, :, 1, :],
                                                    ALU.mult, ALU.add))
                        do.put(eng.tensor_scalar(ix[:, :, 1, :], ix[:, :, 1, :], 0.0, None, ALU.max))
                        do(eng.tensor_tensor(ix[:, :, 2, :], ef[:, :, 2, :],
                                             win[:, :].unsqueeze(2).to_broadcast([P, SB, P]), ALU.subtract))
                        eng.engine_nop().then_inc(s_ix, 1)
                        do.put(eng.tensor_scalar(ef[:, :, 0, :], ix[:, :, 2, :], 0.0, None, ALU.is_ge))
                        do(eng.tensor_scalar(ef[:, :, 1, :], ix[:, :, 2, :], float(P), None, ALU.is_lt))
                        do(eng.tensor_tensor(ef[:, :, 0, :], ef[:, :, 0, :], ef[:, :, 1, :], ALU.mult))
                        do(eng.scalar_tensor_tensor(keys[:, :, :], ef[:, :, 2, :], 1.0, ef[:, :, 0, :],
                                                    ALU.add, ALU.mult))
                        eng.wait_ge(s_xn, NW)
                        do(eng.tensor_tensor(xb[:, :, :], xt[:, :, :],
                                             hb[:, :].unsqueeze(1).to_broadcast([P, NW, D]), ALU.add))

            el_g = sb("el_g", [P, RING, H], F32, st1)
            er_g = sb("er_g", [P, RING, H], F32, st1)
            ir1 = sb("ir1", [P, 2, QUADS, HALF], I32, st1)
            fsb = sb("fsb", [P, 2, R * D], F32, st1)
            with ExitStack() as c2:
                psf = [pb(f"psf{i}", c2) for i in range(8)]
                s_ir = sem("index_ring_1")
                s_g1 = [sem(f"logits_gathered{i}") for i in range(2)]
                s_u1 = sem("logits_added")
                s_f = sem("features_done")
                s_fa = sem("features_copied_scalar")
                s_fv = sem("features_copied_vector")
                s_fs = [sem(f"features_stored{i}") for i in range(2)]
                s_e0 = sem("unused_logits_cleared")

                with nc.Block() as block:
                    @block.gpsimd
                    def _(eng):
                        eng.memset(e_all[:, SLOTS:SB * P, :], 0.0).then_inc(s_e0, 1)
                        for n, tab in enumerate((el_idx, er_idx)):
                            eng.tensor_copy(ir1[:, n, 0, :], tab[:, 0:HALF]).then_inc(s_ir, 1)
                        with eng.Fori(0, QITERS) as i:
                            for q in range(QUADS):
                                b = q % 2
                                m = i * QUADS + q
                                eng.wait_ge(s_ir, (m + 1) * 2)
                                eng.wait_ge(s_u1, m + 1)
                                for n, tab in enumerate((el_idx, er_idx)):
                                    eng.tensor_tensor(ir1[:, n, (q + 1) % QUADS, :], tab[:, bass.ds((m + 1) * HALF, HALF)],
                                                      zero_i[:, :], ALU.add).then_inc(s_ir, 1)
                                for j in range(HALF):
                                    for n, (ring, rows) in enumerate(((el_g, el_rows), (er_g, er_rows))):
                                        eng.indirect_dma_start(
                                            ring[:, b * HALF + j, :], None, rows,
                                            bass.IndirectOffsetOnAxis(ap=ir1[:, n, q, j:j + 1], axis=0))\
                                            .then_inc(s_g1[b], 16)
                        eng.wait_ge(s_g1[0], ITERS * 2 * HALF * 16)
                        eng.wait_ge(s_g1[1], ITERS * 2 * HALF * 16)

                    @block.vector
                    def _(eng):
                        eng.engine_nop().then_inc(s_u1, 2)
                        with eng.Fori(0, ITERS) as i:
                            for b in range(2):
                                eng.wait_ge(s_g1[b], (i + 1) * (2 * HALF * 16))
                                eng.tensor_tensor(e_all[:, bass.ds(i * RING + b * HALF, HALF), :],
                                                  el_g[:, b * HALF:(b + 1) * HALF, :],
                                                  er_g[:, b * HALF:(b + 1) * HALF, :], ALU.add).then_inc(s_u1, 1)

                    @block.tensor
                    def _(eng):
                        for t in range(NW):
                            for c in range(4):
                                q = t * 4 + c
                                if t >= 2:
                                    eng.wait_ge(s_fa, q - 7)
                                for k in range(KD):
                                    mm = eng.matmul(psf[q % 8][:, :], xnT[:, k, t * P:(t + 1) * P],
                                                    wsb[:, k, 2 * c:2 * c + 2, :].rearrange("p r d -> p (r d)"),
                                                    start=(k == 0), stop=(k == KD - 1))
                                mm.then_inc(s_f, 1)

                    @block.scalar
                    def _(eng):
                        for t in range(NW):
                            if t >= 2:
                                eng.wait_ge(s_fs[t % 2], 16 * (t // 2))
                            for c in range(4):
                                q = t * 4 + c
                                eng.wait_ge(s_f, q + 1)
                                eng.copy(fsb[:, t % 2, c * 512:(c + 1) * 512], psf[q % 8][:, :]).then_inc(s_fa, 1)

                    @block.sync
                    def _(eng):
                        for t in range(NW):
                            eng.wait_ge(s_fa, 4 * (t + 1))
                            eng.dma_start(feat[t * P:(t + 1) * P, :], fsb[:, t % 2, :]).then_inc(s_fs[t % 2], 16)
                        for b in range(2):
                            eng.wait_ge(s_fs[b], 16 * (NW // 2))

        with ExitStack() as c3:
            es = sb("es", [P, SB, H, P], F32, c3)
            fw = sb("fw", [P, SB, H, P], F32, c3)
            bw = sb("bw", [P, SB, H, P], F32, c3)
            brk = sb("brk", [P, SB, P + 1], F32, c3)
            summ = sb("summ", [P, SB, 5, H], F32, c3)
            rows = sb("rows", [H, 5, SB * P], F32, c3)
            rt = sb("rt", [H, 6, SB * P], F32, c3)
            inc = sb("inc", [P, SB, 2, H], F32, c3)
            pse = [pb(f"pse{i}", c3) for i in range(4)]
            psr = [pb(f"psr{i}", c3) for i in range(2)]
            s_d3 = sem("vector_steps_3")
            s_lr = sem("edge_logits_ready")
            s_t3 = sem("transposes_done_3")
            s_c3 = sem("transposes_copied_3")
            s_sm = sem("row_summaries_ready")
            s_rt = sem("summaries_turned")
            s_rc = sem("carries_ready")
            s_it = sem("carries_turned")
            s_mx = sem("segment_max_ready")
            s_ex = sem("exp_ready")
            NB3 = SB

            with nc.Block() as block:
                @block.tensor
                def _(eng):
                    eng.wait_ge(s_lr, 1)
                    for k in range(SB):
                        if k >= 4:
                            eng.wait_ge(s_c3, k - 3)
                        for h in range(H):
                            tr = eng.transpose(pse[k % 4][:, h * P:(h + 1) * P], e_all[:, k * P:(k + 1) * P, h],
                                               ident[:, :])
                        tr.then_inc(s_t3, 1)
                    eng.wait_ge(s_sm, 1)
                    for k in range(SB):
                        if k >= 1:
                            eng.wait_ge(s_c3, SB + k)
                        for n in range(5):
                            tr = eng.transpose(psr[n // 4][0:H, (n % 4) * P:(n % 4 + 1) * P], summ[:, k, n, :],
                                               ident[:, :])
                        tr.then_inc(s_t3, 1)
                    eng.wait_ge(s_rc, 1)
                    eng.wait_ge(s_c3, 2 * SB)
                    for k in range(SB):
                        for n in range(2):
                            tr = eng.transpose(psr[0][:, (2 * k + n) * H:(2 * k + n + 1) * H],
                                               rt[:, 4 + n, k * P:(k + 1) * P], ident[0:H, 0:H])
                    tr.then_inc(s_t3, 1)
                    for k in range(SB):
                        eng.wait_ge(s_ex, k + 1)
                        eng.wait_ge(s_c3, 2 * SB + 1)
                        if k >= 4:
                            eng.wait_ge(s_c3, 2 * SB + 1 + k - 3)
                        for h in range(H):
                            tr = eng.transpose(pse[k % 4][:, h * P:(h + 1) * P], es[:, k, h, :], ident[:, :])
                        tr.then_inc(s_t3, 1)

                @block.scalar
                def _(eng):
                    for k in range(SB):
                        eng.wait_ge(s_t3, k + 1)
                        eng.copy(es[:, k, :, :].rearrange("p h e -> p (h e)"), pse[k % 4][:, :]).then_inc(s_c3, 1)
                    for k in range(SB):
                        eng.wait_ge(s_t3, SB + k + 1)
                        eng.copy(rows[:, 0:4, k * P:(k + 1) * P],
                                 psr[0][0:H, :].rearrange("p (n s) -> p n s", n=4))
                        eng.copy(rows[:, 4, k * P:(k + 1) * P], psr[1][0:H, 0:P]).then_inc(s_c3, 1)
                    eng.wait_ge(s_t3, 2 * SB + 1)
                    eng.copy(inc[:, :, :, :].rearrange("p k n h -> p (k n h)"), psr[0][:, 0:SB * 2 * H])\
                       .then_inc(s_c3, 1)
                    for k in range(SB):
                        eng.wait_ge(s_mx, k + 1)
                        eng.activation(es[:, k, :, :], es[:, k, :, :], ACT.Exp, bias=zrow[:, 0:1]).then_inc(s_ex, 1)
                    for k in range(SB):
                        eng.wait_ge(s_t3, 2 * SB + 2 + k)
                        eng.copy(e_all[:, k * P:(k + 1) * P, :].rearrange("p s h -> p h s"),
                                 pse[k % 4][:, :].rearrange("p (h s) -> p h s", h=H)).then_inc(s_c3, 1)
                    eng.wait_ge(s_c3, 3 * SB + 1)

                @block.vector
                def _(eng):
                    do = Chain(eng, s_d3)
                    do(eng.scalar_tensor_tensor(e_all[:, :, :], e_all[:, :, :], 0.2, e_all[:, :, :],
                                                ALU.mult, ALU.max))
                    eng.engine_nop().then_inc(s_lr, 1)
                    do.put(eng.memset(brk[:, :, 0:1], 0.0))
                    do.put(eng.memset(brk[:, :, P:P + 1], 0.0))
                    do(eng.tensor_tensor(brk[:, :, 1:P], keys[:, :, 1:P], keys[:, :, 0:P - 1], ALU.not_equal))
                    do(eng.tensor_scalar(brk[:, :, 1:P], brk[:, :, 1:P], -BIG, None, ALU.mult))
                    do.put(eng.tensor_reduce(summ[:, :, 2, 0:1], keys[:, :, :], AX, ALU.min))
                    do(eng.tensor_reduce(summ[:, :, 2, 1:2], keys[:, :, :], AX, ALU.max))
                    do(eng.tensor_tensor(summ[:, :, 2, 2:3], summ[:, :, 2, 0:1], summ[:, :, 2, 1:2], ALU.is_equal))
                    do.put(eng.tensor_copy(summ[:, :, 3, :], keys[:, :, 0:1].to_broadcast([P, SB, H])))
                    do.put(eng.tensor_copy(summ[:, :, 4, :], keys[:, :, P - 1:P].to_broadcast([P, SB, H])))
                    do.put(eng.tensor_copy(summ[:, :, 2, 0:2], summ[:, :, 2, 2:3].to_broadcast([P, SB, 2])))
                    do(eng.tensor_copy(summ[:, :, 2, 3:4], summ[:, :, 2, 2:3]))

                    def scans(first):
                        for k in range(SB):
                            for h in range(H):
                                a = -BIG if first else inc[:, k, 0, h:h + 1]
                                b = -BIG if first else inc[:, k, 1, h:h + 1]
                                do.put(eng.tensor_tensor_scan(fw[:, k, h, :], brk[:, k, 0:P], es[:, k, h, :],
                                                              a, ALU.add, ALU.max))
                                do.put(eng.tensor_tensor_scan(bw[:, k, h, ::-1], brk[:, k, P:0:-1],
                                                              es[:, k, h, ::-1], b, ALU.add, ALU.max))
                        do.sync()

                    eng.wait_ge(s_c3, SB)
                    scans(True)
                    do.put(eng.tensor_copy(summ[:, :, 0, :], fw[:, :, :, P - 1]))
                    do(eng.tensor_copy(summ[:, :, 1, :], bw[:, :, :, 0]))
                    eng.engine_nop().then_inc(s_sm, 1)
                    eng.wait_ge(s_c3, 2 * SB)
                    S = SB * P
                    do.put(eng.memset(rt[:, :, :], 0.0))
                    do.sync()
                    do.put(eng.tensor_tensor(rt[:, 0, 1:S], rows[:, 3, 1:S], rows[:, 4, 0:S - 1], ALU.is_equal))
                    do.sync()
                    do.put(eng.tensor_tensor(rt[:, 1, :], rt[:, 0, :], rows[:, 2, :], ALU.mult))
                    do(eng.tensor_tensor(rt[:, 2, 0:S - 1], rt[:, 0, 1:S], rows[:, 2, 0:S - 1], ALU.mult))
                    do(eng.tensor_scalar(rt[:, 0:3, :], rt[:, 0:3, :], 1.0, BIG, ALU.subtract, ALU.mult))
                    do.put(eng.tensor_tensor_scan(rt[:, 1, :], rt[:, 1, :], rows[:, 0, :], -BIG, ALU.add, ALU.max))
                    do(eng.tensor_tensor_scan(rt[:, 2, ::-1], rt[:, 2, ::-1], rows[:, 1, ::-1], -BIG,
                                              ALU.add, ALU.max))
                    do.put(eng.memset(rt[:, 4, 0:1], -BIG))
                    do.put(eng.memset(rt[:, 5, S - 1:S], -BIG))
                    do.put(eng.tensor_tensor(rt[:, 4, 1:S], rt[:, 1, 0:S - 1], rt[:, 0, 1:S], ALU.add))
                    do(eng.tensor_tensor(rt[:, 5, 0:S - 1], rt[:, 2, 1:S], rt[:, 0, 1:S], ALU.add))
                    eng.engine_nop().then_inc(s_rc, 1)
                    eng.wait_ge(s_c3, 2 * SB + 1)
                    scans(False)
                    do(eng.tensor_tensor(fw[:, :, :, :], fw[:, :, :, :], bw[:, :, :, :], ALU.max))
                    for k in range(SB):
                        eng.tensor_tensor(es[:, k, :, :], es[:, k, :, :], fw[:, k, :, :],
                                          ALU.subtract).then_inc(s_mx, 1)
        if dbg is not None and "e_all" in dbg:
            s_dbg = sem("dbg")
            with nc.Block() as block:
                @block.sync
                def _(eng):
                    eng.dma_start(dbg["e_all"], e_all[:, :, :]).then_inc(s_dbg, 16)
                    eng.wait_ge(s_dbg, 16)

        hacc = sb("hacc", [P, NW, ROW], F32)
        w1s = sb("w1s", [P, KD, X, D], F32)
        w2s = sb("w2s", [P, KD, X, D], F32)
        b1s = sb("b1s", [P, X, KD], F32)
        b2s = sb("b2s", [X, D], F32)
        rws = sb("rws", [P, KD, X], F32)
        s_fw = sem("expert_weights_loaded")
        with ExitStack() as c4:
            G = sb("G", [P, RING, ROW], F32, c4)
            OH = sb("OH", [P, 2, P], F32, c4)
            ir2 = sb("ir2", [P, QUADS, HALF], I32, c4)
            psh = [pb(f"psh{i}", c4) for i in range(2)]
            s_gs = [sem(f"rows_gathered{j}") for j in range(2)]
            s_ir2 = sem("index_ring_2")
            s_use = sem("slots_summed")
            s_bank = sem("window_banks_free")
            s_exc = sem("weights_copied")
            s_wt = sem("slots_weighted")
            s_g = sem("rows_weighted")
            s_win = sem("windows_summed")

            with nc.Block() as block:
                @block.gpsimd
                def _(eng):
                    eng.tensor_copy(ir2[:, 0, :], el_idx[:, 0:HALF]).then_inc(s_ir2, 1)
                    with eng.Fori(0, QITERS) as i:
                        for q in range(QUADS):
                            b = q % 2
                            m = i * QUADS + q
                            eng.wait_ge(s_ir2, m + 1)
                            eng.wait_ge(s_use, m * HALF + HALF)
                            eng.tensor_tensor(ir2[:, (q + 1) % QUADS, :], el_idx[:, bass.ds((m + 1) * HALF, HALF)],
                                              zero_i[:, :], ALU.add).then_inc(s_ir2, 1)
                            for j in range(HALF):
                                eng.indirect_dma_start(G[:, b * HALF + j, 0:D], None, feat_rows,
                                                       bass.IndirectOffsetOnAxis(ap=ir2[:, q, j:j + 1], axis=0))\
                                   .then_inc(s_gs[b], 16)
                    for b in range(2):
                        eng.wait_ge(s_gs[b], ITERS * HALF * 16)

                @block.scalar
                def _(eng):
                    with eng.Fori(0, NW // 2) as v:
                        for b in range(2):
                            eng.wait_ge(s_win, v * 2 + b + 1)
                            eng.copy(hacc[:, bass.ds(v * 2 + b, 1), :].rearrange("p a d -> p (a d)"),
                                     psh[b][:, 0:ROW]).then_inc(s_bank, 1)
                    eng.wait_ge(s_bank, NW + 2)

                @block.vector
                def _(eng):
                    eng.engine_nop().then_inc(s_use, RING)
                    eng.engine_nop().then_inc(s_bank, 2)
                    with eng.Fori(0, ITERS) as i:
                        for b in range(2):
                            s0 = i * RING + b * HALF
                            eng.wait_ge(s_gs[b], (i + 1) * (HALF * 16))
                            eng.tensor_copy(G[:, b * HALF:(b + 1) * HALF, D:ROW],
                                            e_all[:, bass.ds(s0, HALF), :]).then_inc(s_exc, 1)
                            eng.wait_ge(s_exc, i * 2 + b + 1)
                            for j in range(b * HALF, (b + 1) * HALF):
                                s = i * RING + j
                                g = G[:, j, 0:D].rearrange("p (h d) -> p h d", h=H)
                                eng.tensor_tensor(g, g, G[:, j, D:ROW].unsqueeze(2).to_broadcast([P, H, HD]),
                                                  ALU.mult).then_inc(s_g, 1)
                                eng.wait_ge(s_use, s + RING - 1)
                                eng.tensor_scalar(OH[:, j % 2, :], iota_f[:, :], dloc[:, bass.ds(s, 1)], None,
                                                  ALU.is_equal).then_inc(s_wt, 1)
                    eng.wait_ge(s_g, SLOTS)

                @block.tensor
                def _(eng):
                    with eng.Fori(0, NW // 2) as v:
                        for b in range(2):
                            lo = eng.value_load(pair0[0:1, bass.ds(v * 2 + b, 1)], min_val=0, max_val=PAIRS - 1)
                            hi = eng.value_load(pair0[0:1, bass.ds(v * 2 + b + 1, 1)], min_val=1, max_val=PAIRS)
                            eng.wait_ge(s_bank, v * 2 + b + 1)
                            eng.matmul(psh[b][:, 0:ROW], zero16[0:1, 0:P], zero16[0:1, :], start=True, stop=False)
                            with eng.Fori(lo, hi) as p:
                                for j in range(2):
                                    eng.wait_ge(s_g, p * 2 + j + 1)
                                    eng.wait_ge(s_wt, p * 2 + j + 1)
                                    eng.matmul(psh[b][:, 0:ROW], OH[:, j, :],
                                               G[:, bass.ds((p * 2 + j) % RING, 1), :]
                                               .rearrange("p a d -> p (a d)"),
                                               start=False, stop=False).then_inc(s_use, 1)
                            eng.matmul(psh[b][:, 0:ROW], zero16[0:1, 0:P], zero16[0:1, :], start=False, stop=True)\
                               .then_inc(s_win, 1)

                @block.sync
                def _(eng):
                    with nc.allow_non_contiguous_dma(reason="small transposed loads"):
                        eng.dma_start(b1s[:, :, :], b1.rearrange("e (k p) -> p e k", p=P)).then_inc(s_fw, 16)
                        for k in range(KD):
                            eng.dma_start(rws[:, k, :], router_w[:, k * P:(k + 1) * P].rearrange("e p -> p e"))\
                               .then_inc(s_fw, 16)
                    eng.dma_start(b2s[:, :], b2).then_inc(s_fw, 16)
                    for k in range(KD):
                        eng.dma_start(w1s[:, k, :, :], w1[:, k * P:(k + 1) * P, :].rearrange("e p d -> p e d"))\
                           .then_inc(s_fw, 16)
                        eng.dma_start(w2s[:, k, :, :], w2[:, k * P:(k + 1) * P, :].rearrange("e p d -> p e d"))\
                           .then_inc(s_fw, 16)
                    eng.wait_ge(s_fw, 16 * (2 + 3 * KD))

        if dbg is not None and "hacc" in dbg:
            s_dbg = sem("dbg2")
            with nc.Block() as block:
                @block.sync
                def _(eng):
                    eng.dma_start(dbg["hacc"], hacc[:, :, :]).then_inc(s_dbg, 16)
                    eng.wait_ge(s_dbg, 16)

        TG = 3
        GN = TG * P
        xt2 = sb("xt2", [P, KD, NP], F32)
        comb = sb("comb", [P, NW, X], F32)
        acc = xb
        with ExitStack() as c5:
            prob = sb("prob", [P, NW, X], F32, c5)
            mk = sb("mk", [P, NW, X], F32, c5)
            mk2 = sb("mk2", [P, NW, X], F32, c5)
            top = sb("top", [P, NW, 8], F32, c5)
            topi = sb("topi", [P, NW, 8], U32, c5)
            topf = sb("topf", [P, NW, 8], F32, c5)
            r1 = sb("r1", [P, NW], F32, c5)
            r2 = sb("r2", [P, NW], F32, c5)
            stat = sb("stat5", [P, NW, 6], F32, c5)
            mv = sb("mv5", [P, NW, 2], F32, c5)
            cT = sb("cT", [X, 2, P], F32, c5)
            pst = [pb(f"pt5{i}", c5) for i in range(4)]
            psl = pb("pl5", c5)
            psc = [pb(f"pc5{i}", c5) for i in range(2)]
            s_d5 = sem("vector_steps_5")
            s_var5 = sem("variance_ready_5")
            s_std5 = sem("std_ready_5")
            s_xn5 = sem("xn_ready_5")
            s_t5 = sem("transposes_done_5")
            s_c5 = sem("transposes_copied_5")
            s_lg = sem("router_logits_done")
            s_sh = sem("router_shifted")
            s_ex5 = sem("router_exp_done")
            s_cm = sem("combine_ready")
            s_ct = sem("combine_turned")
            s_cc = sem("combine_copied")
            s_b2 = sem("bias_rows_done")
            s_ba = sem("bias_rows_added")

            with nc.Block() as block:
                @block.vector
                def _(eng):
                    do = Chain(eng, s_d5)
                    dn = hacc[:, :, D:ROW]
                    do(eng.tensor_scalar(dn, dn, 0.5, None, ALU.max))
                    do(eng.reciprocal(dn, dn))
                    for t in range(NW):
                        g = hacc[:, t, 0:D].rearrange("p (h d) -> p h d", h=H)
                        do.put(eng.tensor_tensor(g, g, hacc[:, t, D:ROW].unsqueeze(2).to_broadcast([P, H, HD]),
                                                 ALU.mult))
                    do.sync()
                    do(eng.tensor_tensor(xb[:, :, :], xb[:, :, :], hacc[:, :, 0:D], ALU.add))
                    for t in range(NW):
                        do.put(eng.bn_stats(stat[:, t, :], xb[:, t, :]))
                    do.sync()
                    for t in range(NW):
                        do.put(eng.bn_aggr(mv[:, t, :], stat[:, t, :]))
                    do.sync()
                    eng.engine_nop().then_inc(s_var5, 1)
                    eng.wait_ge(s_std5, 1)
                    do(eng.reciprocal(r2[:, :], r1[:, :]))
                    for t in range(NW):
                        eng.tensor_scalar(hacc[:, t, 0:D], xb[:, t, :], mv[:, t, 0:1], r2[:, t:t + 1],
                                          ALU.subtract, ALU.mult).then_inc(s_xn5, 1)
                    eng.wait_ge(s_xn5, NW)
                    do(eng.tensor_tensor(acc[:, :, :], xb[:, :, :], hacc[:, :, 0:D], ALU.add))
                    eng.wait_ge(s_lg, 1)
                    do(eng.tensor_copy(prob[:, :, :].rearrange("p t e -> p (t e)"), psl[:, 0:NW * X]))
                    do(eng.tensor_reduce(r2[:, :], prob[:, :, :], AX, ALU.max))
                    do(eng.tensor_tensor(prob[:, :, :], prob[:, :, :],
                                         r2[:, :].unsqueeze(2).to_broadcast([P, NW, X]), ALU.subtract))
                    eng.engine_nop().then_inc(s_sh, 1)
                    eng.wait_ge(s_ex5, 1)
                    do(eng.tensor_reduce(r2[:, :], prob[:, :, :], AX, ALU.add))
                    do(eng.reciprocal(r2[:, :], r2[:, :]))
                    do(eng.tensor_tensor(prob[:, :, :], prob[:, :, :],
                                         r2[:, :].unsqueeze(2).to_broadcast([P, NW, X]), ALU.mult))
                    for t in range(NW):
                        do.put(eng.max(top[:, t, :], prob[:, t, :]))
                    do.sync()
                    for t in range(NW):
                        do.put(eng.max_index(topi[:, t, :], top[:, t, :], prob[:, t, :]))
                    do.sync()
                    do(eng.tensor_copy(topf[:, :, :], topi[:, :, :]))
                    lane = iota_f[:, 0:X].unsqueeze(1).to_broadcast([P, NW, X])
                    do.put(eng.tensor_tensor(mk[:, :, :], lane, topf[:, :, 0:1].to_broadcast([P, NW, X]),
                                             ALU.is_equal))
                    do.put(eng.tensor_tensor(mk2[:, :, :], lane, topf[:, :, 1:2].to_broadcast([P, NW, X]),
                                             ALU.is_equal))
                    do(eng.tensor_tensor(r2[:, :], top[:, :, 0], top[:, :, 1], ALU.add))
                    do.put(eng.tensor_tensor(mk[:, :, :], mk[:, :, :], mk2[:, :, :], ALU.add))
                    do(eng.tensor_scalar(r2[:, :], r2[:, :], 1e-12, None, ALU.max))
                    do.put(eng.reciprocal(r1[:, :], r2[:, :]))
                    do(eng.tensor_tensor(mk[:, :, :], mk[:, :, :], prob[:, :, :], ALU.mult))
                    do(eng.tensor_tensor(comb[:, :, :], mk[:, :, :],
                                         r1[:, :].unsqueeze(2).to_broadcast([P, NW, X]), ALU.mult))
                    eng.engine_nop().then_inc(s_cm, 1)
                    for t in range(NW):
                        eng.wait_ge(s_b2, t + 1)
                        eng.tensor_tensor(acc[:, t, :], acc[:, t, :], psc[t % 2][:, 0:D], ALU.add).then_inc(s_ba, 1)
                    eng.wait_ge(s_ba, NW)

                @block.scalar
                def _(eng):
                    eng.wait_ge(s_var5, 1)
                    eng.activation(r1[:, :], mv[:, :, 1], ACT.Sqrt, bias=epsv[:, 0:1]).then_inc(s_std5, 1)
                    for t in range(NW):
                        eng.wait_ge(s_t5, t + 1)
                        eng.copy(xt2[:, :, t * P:(t + 1) * P],
                                 pst[t % 4][:, 0:2 * P].rearrange("p (k n) -> p k n", k=KD)).then_inc(s_c5, 1)
                    eng.wait_ge(s_sh, 1)
                    eng.activation(prob[:, :, :], prob[:, :, :], ACT.Exp, bias=zrow[:, 0:1]).then_inc(s_ex5, 1)
                    for t in range(NW):
                        eng.wait_ge(s_ct, t + 1)
                        if t >= 2:
                            eng.wait_ge(s_b2, t - 1)
                        eng.copy(cT[:, t % 2, :], pst[t % 4][0:X, 0:P]).then_inc(s_cc, 1)

                @block.tensor
                def _(eng):
                    for t in range(NW):
                        eng.wait_ge(s_xn5, t + 1)
                        if t >= 4:
                            eng.wait_ge(s_c5, t - 3)
                        for k in range(KD):
                            tr = eng.transpose(pst[t % 4][:, k * P:(k + 1) * P], hacc[:, t, k * P:(k + 1) * P],
                                               ident[:, :])
                        tr.then_inc(s_t5, 1)
                    eng.wait_ge(s_c5, NW)
                    for t in range(NW):
                        for k in range(KD):
                            mm = eng.matmul(psl[:, t * X:(t + 1) * X], xt2[:, k, t * P:(t + 1) * P], rws[:, k, :],
                                            start=(k == 0), stop=(k == KD - 1))
                    mm.then_inc(s_lg, 1)
                    eng.wait_ge(s_cm, 1)
                    for t in range(NW + 1):
                        if t < NW:
                            if t >= 4:
                                eng.wait_ge(s_cc, t - 3)
                            eng.transpose(pst[t % 4][0:X, 0:P], comb[:, t, :], ident[:, :]).then_inc(s_ct, 1)
                        if t >= 1:
                            eng.wait_ge(s_cc, t)
                            if t >= 3:
                                eng.wait_ge(s_ba, t - 2)
                            eng.matmul(psc[(t - 1) % 2][:, 0:D], cT[:, (t - 1) % 2, :], b2s[:, :],
                                       start=True, stop=True).then_inc(s_b2, 1)

        with ExitStack() as c6:
            hT = sb("hT", [P, 2, KD, GN], F32, c6)
            ph = [[pb(f"ph{i}{j}", c6) for j in range(KD)] for i in range(2)]
            py = [pb(f"py{i}", c6) for i in range(4)]
            s_h = sem("hidden_done")
            s_ge = sem("hidden_activated")
            s_y = sem("expert_rows_done")
            s_ya = sem("expert_rows_added")
            s_out = sem("output_stored")
            NG = NW // TG
            HP = KD * X
            YP = TG * X

            with nc.Block() as block:
                @block.tensor
                def _(eng):
                    with eng.Fori(0, NG) as g:
                        def up(e):
                            for hh in range(KD):
                                eng.wait_ge(s_ge, g * HP + e * KD + hh + 1)
                                for k in range(KD):
                                    mm = eng.matmul(ph[e % 2][hh][:, 0:GN], w1s[:, k, e, hh * P:(hh + 1) * P],
                                                    xt2[:, k, bass.ds(g * GN, GN)],
                                                    start=(k == 0), stop=(k == KD - 1))
                                mm.then_inc(s_h, 1)

                        def down(e):
                            eng.wait_ge(s_ge, g * HP + (e + 1) * KD + 2 * KD)
                            for m in range(TG):
                                n = e * TG + m
                                eng.wait_ge(s_ya, g * YP + n + 1)
                                for hh in range(KD):
                                    mm = eng.matmul(py[n % 4][:, 0:D], hT[:, e % 2, hh, m * P:(m + 1) * P],
                                                    w2s[:, hh, e, :], start=(hh == 0), stop=(hh == KD - 1))
                                mm.then_inc(s_y, 1)

                        up(0)
                        for e in range(X):
                            if e + 1 < X:
                                up(e + 1)
                            down(e)

                @block.scalar
                def _(eng):
                    with eng.Fori(0, NG) as g:
                        for e in range(X):
                            eng.wait_ge(s_y, g * YP + e * TG + TG)
                            for hh in range(KD):
                                eng.wait_ge(s_h, g * HP + e * KD + hh + 1)
                                eng.activation(hT[:, e % 2, hh, :], ph[e % 2][hh][:, 0:GN], ACT.Gelu,
                                               bias=b1s[:, e, hh:hh + 1]).then_inc(s_ge, 1)

                @block.vector
                def _(eng):
                    eng.engine_nop().then_inc(s_ge, 2 * KD)
                    eng.engine_nop().then_inc(s_y, 2 * TG)
                    eng.engine_nop().then_inc(s_ya, 4)
                    with eng.Fori(0, NG) as g:
                        for e in range(X):
                            for m in range(TG):
                                n = e * TG + m
                                eng.wait_ge(s_y, g * YP + n + 1 + 2 * TG)
                                if e:
                                    eng.wait_ge(s_ya, g * YP + n - TG + 1 + 4)
                                a = acc[:, bass.ds(g * TG + m, 1), :].rearrange("p a d -> p (a d)")
                                eng.scalar_tensor_tensor(a, py[n % 4][:, 0:D],
                                                         comb[:, bass.ds(g * TG + m, 1), e], a,
                                                         ALU.mult, ALU.add).then_inc(s_ya, 1)

                @block.sync
                def _(eng):
                    for g in range(NG):
                        eng.wait_ge(s_ya, (g + 1) * YP + 4)
                        for t in range(g * TG, (g + 1) * TG):
                            if t < FULL:
                                eng.dma_start(out[t * P:(t + 1) * P, :], acc[:, t, :]).then_inc(s_out, 16)
                            else:
                                eng.dma_start(out[t * P:N, :], acc[0:REST, t, :]).then_inc(s_out, 16)
                    eng.wait_ge(s_out, 16 * NW)


_INS = ['x', 'src', 'dst', 'edge_type_8', 'L0_gnn_conv_weights', 'L0_gnn_attn_l', 'L0_gnn_attn_r', 'L0_gnn_h_bias',
        'L0_ffn_router_w', 'L0_ffn_w1', 'L0_ffn_b1', 'L0_ffn_w2', 'L0_ffn_b2']
_OUTS = [((3750, 256), 'float32')]


def kernel(**inputs):
    import numpy as _np
    import concourse.bacc as _bacc
    from concourse import mybir as _mybir
    from concourse.bass_utils import run_bass_kernel_spmd as _run

    nc = _bacc.Bacc("TRN2", target_bir_lowering=False, num_devices=1)
    arrays, args = {}, []
    for name in _INS:
        a = _np.ascontiguousarray(inputs[name])
        arrays[f"in_{name}_dram"] = a
        args.append(nc.dram_tensor(f"in_{name}_dram", a.shape, _mybir.dt.from_np(a.dtype), kind="ExternalInput").ap())
    for i, (shape, dtype) in enumerate(_OUTS):
        dt = _mybir.dt.from_np(_np.dtype(dtype))
        args.append(nc.dram_tensor(f"out_{i}_dram", shape, dt, kind="ExternalOutput").ap())
    gnn_moe(nc, *args)
    r = _run(nc, [arrays], core_ids=[0])
    got = tuple(r.results[0][f"out_{i}_dram"] for i in range(len(_OUTS)))
    return got[0]
```

```python
from contextlib import ExitStack

import numpy as np

import concourse.bass as bass
from concourse import mybir

F32, BF16, I32, U32 = mybir.dt.float32, mybir.dt.bfloat16, mybir.dt.int32, mybir.dt.uint32
ALU = mybir.AluOpType
ACT = mybir.ActivationFunctionType
AX = mybir.AxisListType.X

P = 128
BIG = 1.0e30


class Chain:

    def __init__(self, eng, sem):
        self.eng, self.sem, self.n = eng, sem, 0

    def __call__(self, ins):
        ins.then_inc(self.sem, 1)
        self.n += 1
        self.eng.wait_ge(self.sem, self.n)

    def put(self, ins):
        ins.then_inc(self.sem, 1)
        self.n += 1

    def sync(self):
        self.eng.wait_ge(self.sem, self.n)


def gnn_moe(nc, x, src, dst, etype, conv_w, attn_l, attn_r, h_bias, router_w, w1, b1, w2, b2, out):
    N, D = x.shape
    E = src.shape[0]
    R, H, _, HD = conv_w.shape
    RH = R * H
    X = router_w.shape[0]
    KD = D // P
    NW = -(-N // P)
    NP = NW * P
    FULL = N // P
    REST = N - FULL * P
    T = -(-E // P)
    TF = E // P
    TREST = E - TF * P
    PAD_TILE = T
    PAIRS = (T + NW - 1 + NW) // 2
    HALF = 12
    QUADS = 4
    C = 2 * HALF
    RING = 2 * C
    SLOTS = -(-2 * PAIRS // RING) * RING
    PAIRS = SLOTS // 2
    NC = SLOTS // C
    CP2 = C // 2
    EG = 16
    NEG = SLOTS // EG
    HC = H * C
    SB = -(-SLOTS // P)
    ROW = D + H
    CP = 120
    assert E % CP == 0 and D == 2 * P and NW % 6 == 0 and SLOTS % (3 * EG) == 0
    EPS = 1e-5
    NCONST = 11 + CP2
    CELLS = 16
    assert CELLS > CP2 + 1

    edges = nc.dram_tensor("edge_tiles", [T + 1, 3 * P], I32, kind="Internal").ap()
    feat = nc.dram_tensor("node_rows", [NP, R * ROW], F32, kind="Internal").ap()
    feat_rows = feat.rearrange("n (r d) -> (n r) d", r=R)
    dloc_rows = nc.dram_tensor("slot_targets", [SB * P, P], BF16, kind="Internal").ap()
    brk_rows = nc.dram_tensor("segment_breaks", [SB * P, P + 1], F32, kind="Internal").ap()
    col = lambda a: a.rearrange("(a d) -> a d", a=1)

    with ExitStack() as ctx:
        def sb(name, shape, dt, c=ctx):
            return c.enter_context(nc.sbuf_tensor(name, shape, dt))

        def pb(name, c, shape=(P, 512), dt=F32):
            return c.enter_context(nc.psum_tensor(name, list(shape), dt))

        def sem(name):
            return ctx.enter_context(nc.semaphore(name))

        ident = sb("ident", [P, P], F32)
        iota_f = sb("iota_f", [P, P], F32)
        xb = sb("xb", [P, NW, D], F32)
        el_idx = sb("el_idx", [P, SB * P], I32)
        etyp = sb("etyp", [P, SB * P], F32)
        dloc = sb("dloc", [P, SB * P], F32)
        er_all = sb("er_all", [P, SLOTS, H], F32)
        brkt = sb("brkt", [HC, NC, P + 1], F32)
        flag = sb("flag", [1, 4, SB * P], F32)
        cross = sb("cross", [P, NC], F32)
        new_in_group = sb("new_in_group", [1, NEG], I32)
        new_in_chunk = sb("new_in_chunk", [1, NC], I32)
        chunk_info = sb("chunk_info", [1, NC], I32)
        iota_p = sb("iota_p", [P, 1], F32)
        pair0 = sb("pair0", [1, NW + 2], I32)
        zero_i = sb("zero_i", [P, HALF], I32)
        zero16 = sb("zero16", [1, ROW], BF16)
        zrow = sb("zrow", [P, 1], F32)
        epsv = sb("epsv", [P, 1], F32)

        st1 = ExitStack()
        with st1:
            xt = xb
            xn = sb("xn", [P, 6, D], F32, st1)
            xnT = sb("xnT", [P, KD, NP + P], F32, st1)
            wsb = sb("wsb", [P, KD, R, D], F32, st1)
            wa = sb("wa", [P, KD, 2, RH], F32, st1)
            lts = sb("lts", [P, NW, 2, RH], F32, st1)
            er3 = sb("er3", [P, 3, NW, RH], BF16, st1)
            with ExitStack() as c1:
                keys = sb("keys", [P, SB, P], F32, c1)
                brk = sb("brk", [P, SB, P + 1], F32, c1)
                summ = sb("summ", [P, SB, 4], F32, c1)
                rows = sb("rows", [1, 4, SB * P], F32, c1)
                dlb16 = sb("dlb16", [P, SB, P], BF16, c1)
                crow = sb("crow", [1, 4, NC], F32, c1)
                winrow = sb("winrow", [1, SB * P], F32, c1)
                newp = sb("newp", [1, PAIRS], F32, c1)
                nprod = sb("nprod", [1, PAIRS], F32, c1)
                pow2 = sb("pow2", [1, CP2], F32, c1)
                dst_i = sb("dst_i", [CP, E // CP], I32, c1)
                dst_f = sb("dst_f", [CP, E // CP], F32, c1)
                cmp = sb("cmp", [CP, E // CP], F32, c1)
                cnt = sb("cnt", [CP, NW - 1], F32, c1)
                ones = sb("ones", [P, P], F32, c1)
                sti = sb("sti", [P, 4, NW + 1], I32, c1)
                stf = sb("stf", [P, 6, NW + 1], F32, c1)
                slot_id = sb("slot_id", [P, SB, 1], F32, c1)
                ge = sb("ge", [P, SB, NW - 1], F32, c1)
                ged = sb("ged", [P, SB, NW - 1], F32, c1)
                win = sb("win", [P, SB], F32, c1)
                tile_f = sb("tile_f", [P, SB], F32, c1)
                tile_i = sb("tile_i", [P, SB], I32, c1)
                wtmp = er_all[:, :, :].rearrange("p s h -> p (s h)")[:, 0:R * D]
                att = sb("att", [P, R * D], F32, c1)
                padr = sb("padr", [2, 3 * P], I32, c1)
                eg = sb("eg", [P, SB, 3 * P], I32, c1)
                ert = eg[:, :, :].rearrange("p k e -> p (k e)").bitcast(F32).rearrange("p (n t c) -> p n t c", n=2, t=NW)
                ef = sb("ef", [P, SB, 3, P], F32, c1)
                ix = sb("ix", [P, SB, 3, P], F32, c1)
                stat = sb("stat", [P, NW, 6], F32, c1)
                mv = sb("mv", [P, NW, 2], F32, c1)
                rstd = sb("rstd", [P, NW], F32, c1)
                std = sb("std", [P, NW], F32, c1)
                hb = sb("hb", [P, D], F32, c1)
                psc = pb("psc", c1)
                pst = [pb(f"pst{i}", c1) for i in range(4)]
                psl = [pb(f"psl{i}", c1) for i in range(2)]
                psx = pb("psx", c1)

                s_const = sem("constants_ready")
                s_ident = sem("identity_ready")
                s_dst = sem("dst_loaded")
                s_x = sem("x_loaded")
                s_w = sem("weights_loaded")
                s_att = sem("attention_loaded")
                s_pad = sem("pad_rows_ready")
                s_et = sem("edge_tiles_stored")
                s_dv = sem("vector_steps_1")
                s_cnt = sem("counts_ready")
                s_cntp = sem("counts_summed")
                s_tile = sem("slot_tiles_ready")
                s_eg = sem("slot_edges_gathered")
                s_ix = sem("slot_indices_ready")
                s_tp = sem("transposes_done_1")
                s_te = sem("transposes_copied_1")
                s_var = sem("variance_ready")
                s_std = sem("std_ready")
                s_xn = sem("xn_ready")
                s_wa = sem("attention_folded")
                s_lt = sem("logits_done")
                s_le = sem("logits_copied")
                s_ls = sem("logit_tables_stored")
                s_wl = sem("source_vectors_folded")
                s_hb = sem("bias_loaded")
                s_wr = sem("slot_windows_turned")
                s_br = sem("segment_breaks_ready")
                s_sm = sem("row_summaries_ready")
                s_cr = sem("crossing_rows_ready")

                with nc.Block() as block:
                    @block.sync
                    def _(eng):
                        eng.dma_start(dst_i[:, :], dst.rearrange("(p f) -> p f", p=CP)).then_inc(s_dst, 16)
                        eng.wait_ge(s_const, 1)
                        eng.dma_start(xt[:, 0:FULL, :],
                                      x[0:FULL * P, :].rearrange("(t p) f -> p t f", p=P)).then_inc(s_x, 16)
                        eng.dma_start(xt[0:REST, FULL, :], x[FULL * P:N, :]).then_inc(s_x, 16)
                        eng.dma_start(hb[:, :], h_bias.partition_broadcast(P)).then_inc(s_hb, 16)
                        for n, a in enumerate((attn_l, attn_r)):
                            if n:
                                eng.wait_ge(s_wl, 1)
                            eng.dma_start(att[:, :], a.rearrange("r h d -> (r h d)").partition_broadcast(P))\
                               .then_inc(s_att, 16)
                        eng.wait_ge(s_br, 1)
                        eng.dma_start(dloc_rows.rearrange("(k s) e -> s k e", s=P), dlb16[:, :, :]).then_inc(s_ls, 16)
                        eng.dma_start(brk_rows.rearrange("(k s) e -> s k e", s=P), brk[:, :, :]).then_inc(s_ls, 16)
                        eng.wait_ge(s_ls, 32)
                        for h in range(H):
                            eng.dma_start(brkt[h * C:(h + 1) * C, :, :],
                                          brk_rows[0:SLOTS, :].rearrange("(c s) e -> s c e", s=C)).then_inc(s_ls, 16)
                        eng.wait_ge(s_ls, 16 * (2 + H))

                    @block.gpsimd
                    def _(eng):
                        eng.memset(xt[:, FULL, :], 0.0).then_inc(s_const, 1)
                        eng.memset(ident[:, :], 0.0).then_inc(s_const, 1)
                        eng.memset(zero16[:, :], 0.0).then_inc(s_const, 1)
                        eng.memset(zero_i[:, :], 0).then_inc(s_const, 1)
                        eng.memset(zrow[:, :], 0.0).then_inc(s_const, 1)
                        eng.memset(epsv[:, :], EPS).then_inc(s_const, 1)
                        eng.memset(ones[:, :], 1.0).then_inc(s_const, 1)
                        eng.iota(iota_f[:, :], pattern=[[1, P]], base=0, channel_multiplier=0,
                                 allow_small_or_imprecise_dtypes=True).then_inc(s_const, 1)
                        eng.iota(iota_p[:, :], pattern=[[0, 1]], base=0, channel_multiplier=1,
                                 allow_small_or_imprecise_dtypes=True).then_inc(s_const, 1)
                        eng.memset(xnT[:, :, NP:NP + P], 0.0).then_inc(s_const, 1)
                        eng.iota(slot_id[:, :, :], pattern=[[P, SB], [1, 1]], base=0, channel_multiplier=1,
                                 allow_small_or_imprecise_dtypes=True).then_inc(s_const, 1)
                        for n in range(CP2):
                            eng.memset(pow2[:, n:n + 1], float(2 ** n)).then_inc(s_const, 1)
                        eng.memset(padr[:, 0:2 * P], 0).then_inc(s_pad, 1)
                        eng.memset(padr[:, 2 * P:3 * P], -1).then_inc(s_pad, 1)
                        eng.wait_ge(s_const, NCONST)
                        eng.affine_select(out=ident[:, :], in_=ident[:, :], compare_op=ALU.not_equal, fill=1.0,
                                          base=0, pattern=[[-1, P]], channel_multiplier=1).then_inc(s_ident, 1)
                        eng.wait_ge(s_tile, 1)
                        eng.wait_ge(s_et, 8 * 16)
                        for k in range(SB):
                            eng.indirect_dma_start(eg[:, k, :], None, edges[:, :],
                                                   bass.IndirectOffsetOnAxis(ap=tile_i[:, k:k + 1], axis=0))\
                               .then_inc(s_eg, 16)
                        eng.wait_ge(s_eg, 16 * SB)

                    @block.scalar
                    def _(eng):
                        for n, a in enumerate((src, etype, dst)):
                            eng.dma_start(edges[0:TF, n * P:(n + 1) * P],
                                          a[0:TF * P].rearrange("(t e) -> t e", e=P)).then_inc(s_et, 16)
                            eng.dma_start(edges[TF:TF + 1, n * P:n * P + TREST],
                                          col(a[TF * P:E])).then_inc(s_et, 16)
                        eng.wait_ge(s_pad, 2)
                        eng.dma_start(edges[TF:TF + 1, :].rearrange("a (n e) -> a n e", e=P)[:, :, TREST:P],
                                      padr[0:1, :].rearrange("a (n e) -> a n e", e=P)[:, :, TREST:P])\
                           .then_inc(s_et, 16)
                        eng.dma_start(edges[T:T + 1, :], padr[1:2, :]).then_inc(s_et, 16)
                        for kh in range(KD):
                            for r in range(R):
                                eng.dma_start(wsb[:, kh, r, :].rearrange("p (h d) -> p h d", h=H),
                                              conv_w[r, :, kh * P:(kh + 1) * P, :].rearrange("h k d -> k h d"))\
                                   .then_inc(s_w, 16)
                        eng.wait_ge(s_var, 1)
                        eng.activation(std[:, :], mv[:, :, 1], ACT.Sqrt, bias=epsv[:, 0:1]).then_inc(s_std, 1)
                        for t in range(NW):
                            eng.wait_ge(s_tp, t + 1)
                            eng.copy(xnT[:, :, t * P:(t + 1) * P],
                                     pst[t % 4][:, 0:2 * P].rearrange("p (k n) -> p k n", k=KD)).then_inc(s_te, 1)
                        for t in range(NW):
                            eng.wait_ge(s_lt, t + 1)
                            eng.copy(lts[:, t, :, :].rearrange("p n c -> p (n c)"),
                                     psl[t % 2][:, 0:2 * RH]).then_inc(s_le, 1)
                        for k in range(SB):
                            eng.wait_ge(s_tp, NW + k + 1)
                            b = pst[(NW + k) % 4]
                            eng.copy(el_idx[:, k * P:(k + 1) * P], b[:, 0:P])
                            eng.copy(etyp[:, k * P:(k + 1) * P], b[:, P:2 * P])
                            eng.copy(dloc[:, k * P:(k + 1) * P], b[:, 2 * P:3 * P]).then_inc(s_te, 1)
                        for k in range(SB):
                            eng.wait_ge(s_tp, NW + SB + k + 1)
                            eng.copy(rows[:, :, k * P:(k + 1) * P],
                                     pst[(NW + SB + k) % 4][0:1, :].rearrange("p (n s) -> p n s", n=4)).then_inc(s_te, 1)
                        eng.wait_ge(s_et, 8 * 16)
                        eng.wait_ge(s_w, 16 * KD * R)
                        eng.wait_ge(s_te, NW + 2 * SB)

                    @block.tensor
                    def _(eng):
                        eng.wait_ge(s_const, NCONST)
                        eng.wait_ge(s_cnt, 1)
                        eng.matmul(psc[:, 0:NW - 1], ones[0:CP, :], cnt[:, :], start=True, stop=True)\
                           .then_inc(s_cntp, 1)
                        eng.wait_ge(s_ident, 1)
                        eng.wait_ge(s_tile, 1)
                        for k in range(SB):
                            tr = eng.transpose((psx if k < 4 else psc)[0:1, (k % 4) * P:(k % 4 + 1) * P], win[:, k:k + 1],
                                               ident[:, :])
                        tr.then_inc(s_wr, 1)
                        for t in range(NW):
                            eng.wait_ge(s_xn, t + 1)
                            if t >= 4:
                                eng.wait_ge(s_te, t - 3)
                            for k in range(KD):
                                tr = eng.transpose(pst[t % 4][:, k * P:(k + 1) * P],
                                                   xn[:, t % 6, k * P:(k + 1) * P], ident[:, :])
                            tr.then_inc(s_tp, 1)
                        eng.wait_ge(s_wa, 1)
                        for t in range(NW):
                            eng.wait_ge(s_te, t + 1)
                            if t >= 2:
                                eng.wait_ge(s_le, t - 1)
                            for k in range(KD):
                                mm = eng.matmul(psl[t % 2][:, 0:2 * RH], xnT[:, k, t * P:(t + 1) * P],
                                                wa[:, k, :, :].rearrange("p a c -> p (a c)"),
                                                start=(k == 0), stop=(k == KD - 1))
                            mm.then_inc(s_lt, 1)
                        eng.wait_ge(s_ix, 1)
                        for k in range(SB):
                            eng.wait_ge(s_te, NW + k - 3)
                            for n in range(3):
                                tr = eng.transpose(pst[(NW + k) % 4][:, n * P:(n + 1) * P], ix[:, k, n, :],
                                                   ident[:, :])
                            tr.then_inc(s_tp, 1)
                        eng.wait_ge(s_sm, 1)
                        for k in range(SB):
                            eng.wait_ge(s_te, NW + SB + k - 3)
                            for n in range(4):
                                tr = eng.transpose(pst[(NW + SB + k) % 4][0:1, n * P:(n + 1) * P], summ[:, k, n:n + 1],
                                                   ident[:, :])
                            tr.then_inc(s_tp, 1)
                        eng.wait_ge(s_cr, 1)
                        eng.matmul(psx[:, 0:NC], ones[0:1, :], crow[:, 0, :], start=True, stop=True)\
                           .then_inc(s_cntp, 1)

                    @block.vector
                    def _(eng):
                        do = Chain(eng, s_dv)
                        eng.wait_ge(s_dst, 16)
                        do(eng.tensor_copy(dst_f[:, :], dst_i[:, :]))
                        for w in range(1, NW):
                            do.put(eng.tensor_scalar(cmp[:, :], dst_f[:, :], float(w * P), 0.0, ALU.is_lt, ALU.add,
                                                     accum_out=cnt[:, w - 1:w]))
                            do.sync()
                        eng.engine_nop().then_inc(s_cnt, 1)
                        eng.wait_ge(s_x, 32)
                        for t in range(NW):
                            do.put(eng.bn_stats(stat[:, t, :], xt[:, t, :]))
                        do.sync()
                        for t in range(NW):
                            do.put(eng.bn_aggr(mv[:, t, :], stat[:, t, :]))
                        do.sync()
                        eng.engine_nop().then_inc(s_var, 1)
                        eng.wait_ge(s_cntp, 1)
                        do.put(eng.memset(stf[:, 0, 0:1], 0.0))
                        do.put(eng.memset(stf[:, 0, NW:NW + 1], float(E)))
                        do(eng.tensor_copy(stf[:, 0, 1:NW], psc[:, 0:NW - 1]))
                        do(eng.tensor_scalar(stf[:, 1, :], stf[:, 0, :], 1.0, None, ALU.subtract))
                        do.put(eng.tensor_copy(sti[:, 0, :], stf[:, 0, :]))
                        do(eng.tensor_copy(sti[:, 1, :], stf[:, 1, :]))
                        do(eng.tensor_scalar(sti[:, 2:4, :], sti[:, 0:2, :], 7, None, ALU.arith_shift_right))
                        do(eng.tensor_copy(stf[:, 2:4, :], sti[:, 2:4, :]))
                        do(eng.tensor_tensor(stf[:, 4, 0:NW], stf[:, 3, 1:NW + 1], stf[:, 2, 0:NW], ALU.subtract))
                        do(eng.tensor_scalar(stf[:, 4, 0:NW], stf[:, 4, 0:NW], 0.0, 2.0, ALU.max, ALU.add))
                        do(eng.tensor_copy(sti[:, 0, 0:NW], stf[:, 4, 0:NW]))
                        do(eng.tensor_scalar(sti[:, 0, 0:NW], sti[:, 0, 0:NW], 1, None, ALU.arith_shift_right))
                        do(eng.tensor_copy(stf[:, 4, 0:NW], sti[:, 0, 0:NW]))
                        do(eng.memset(stf[:, 5, :], 0.0))
                        do(eng.tensor_tensor_scan(stf[:, 1, 0:NW], stf[:, 4, 0:NW], stf[:, 5, 0:NW], 0.0,
                                                  ALU.add, ALU.add))
                        do(eng.tensor_copy(stf[:, 5, 1:NW], stf[:, 1, 0:NW - 1]))
                        do(eng.memset(stf[:, 5, NW:NW + 1], float(PAIRS)))
                        do(eng.tensor_copy(pair0[0:1, 0:NW + 1], stf[0:1, 5, :]))
                        do(eng.tensor_scalar(stf[:, 5, :], stf[:, 5, :], 2.0, None, ALU.mult))
                        do(eng.tensor_tensor(stf[:, 4, :], stf[:, 2, :], stf[:, 5, :], ALU.subtract))
                        do(eng.tensor_tensor(stf[:, 3, 1:NW], stf[:, 4, 1:NW], stf[:, 4, 0:NW - 1], ALU.subtract))
                        do(eng.tensor_tensor(ge[:, :, :], slot_id[:, :, :].to_broadcast([P, SB, NW - 1]),
                                             stf[:, 5:6, 1:NW].to_broadcast([P, SB, NW - 1]), ALU.is_ge))
                        do.put(eng.tensor_reduce(win[:, :], ge[:, :, :], AX, ALU.add))
                        do(eng.tensor_tensor(ged[:, :, :], ge[:, :, :],
                                             stf[:, 3:4, 1:NW].to_broadcast([P, SB, NW - 1]), ALU.mult))
                        do(eng.tensor_reduce(tile_f[:, :], ged[:, :, :], AX, ALU.add))
                        do(eng.tensor_tensor(tile_f[:, :], tile_f[:, :], slot_id[:, :, 0], ALU.add))
                        do.put(eng.tensor_scalar(tile_f[:, :], tile_f[:, :], float(PAD_TILE), 0.0, ALU.min, ALU.max))
                        do(eng.tensor_scalar(win[:, :], win[:, :], float(P), None, ALU.mult))
                        do(eng.tensor_copy(tile_i[:, :], tile_f[:, :]))
                        eng.engine_nop().then_inc(s_tile, 1)
                        eng.wait_ge(s_wr, 1)
                        do.put(eng.tensor_copy(winrow[:, 0:4 * P], psx[0:1, :]))
                        do(eng.tensor_copy(winrow[:, 4 * P:5 * P], psc[0:1, 0:P]))
                        do(eng.tensor_scalar(winrow[:, :], winrow[:, :], 1.0 / P, None, ALU.mult))
                        do.put(eng.memset(newp[:, 0:1], 0.0))
                        do(eng.tensor_tensor(newp[:, 1:PAIRS], winrow[:, 2:2 * PAIRS:2], winrow[:, 0:2 * PAIRS - 2:2],
                                             ALU.subtract))
                        do(eng.tensor_tensor(nprod[:, :].rearrange("p (g n) -> p g n", n=EG // 2),
                                             newp[:, :].rearrange("p (g n) -> p g n", n=EG // 2),
                                             pow2[:, 0:EG // 2].unsqueeze(1).to_broadcast([1, NEG, EG // 2]), ALU.mult))
                        do(eng.tensor_reduce(nprod[:, 0:NEG],
                                             nprod[:, :].rearrange("p (g n) -> p g n", n=EG // 2), AX, ALU.add))
                        do(eng.tensor_copy(new_in_group[:, :], nprod[:, 0:NEG]))
                        do(eng.memset(crow[:, 1, :], 0.0))
                        do(eng.tensor_tensor_scan(crow[:, 2, :], newp[:, 0:PAIRS:CP2], crow[:, 1, :], 0.0,
                                                  ALU.add, ALU.add))
                        do(eng.tensor_tensor(crow[:, 2, :], iota_f[0:1, 0:NC], crow[:, 2, :], ALU.subtract))
                        do(eng.scalar_tensor_tensor(crow[:, 3, :], crow[:, 2, :], 32.0, winrow[:, C - 2:SLOTS:C],
                                                    ALU.mult, ALU.add))
                        do(eng.scalar_tensor_tensor(crow[:, 3, :], crow[:, 3, :], 32.0, winrow[:, 0:SLOTS:C],
                                                    ALU.mult, ALU.add))
                        do(eng.tensor_copy(chunk_info[:, :], crow[:, 3, :]))
                        do(eng.tensor_tensor(nprod[:, :].rearrange("p (g n) -> p g n", n=CP2),
                                             newp[:, :].rearrange("p (g n) -> p g n", n=CP2),
                                             pow2[:, :].unsqueeze(1).to_broadcast([1, NC, CP2]), ALU.mult))
                        do(eng.tensor_reduce(nprod[:, 0:NC],
                                             nprod[:, :].rearrange("p (g n) -> p g n", n=CP2), AX, ALU.add))
                        do(eng.tensor_copy(new_in_chunk[:, :], nprod[:, 0:NC]))
                        eng.wait_ge(s_std, 1)
                        do(eng.reciprocal(rstd[:, :], std[:, :]))
                        for t in range(NW):
                            if t >= 6:
                                eng.wait_ge(s_tp, t - 5)
                            eng.tensor_scalar(xn[:, t % 6, :], xt[:, t, :], mv[:, t, 0:1], rstd[:, t:t + 1],
                                              ALU.subtract, ALU.mult).then_inc(s_xn, 1)
                        eng.wait_ge(s_w, 16 * KD * R)
                        for n in range(2):
                            eng.wait_ge(s_att, 16 * (n + 1))
                            for k in range(KD):
                                do(eng.tensor_tensor(wtmp, wsb[:, k, :, :].rearrange("p r d -> p (r d)"),
                                                     att[:, :], ALU.mult))
                                do(eng.tensor_reduce(wa[:, k, n, :], wtmp.rearrange("p (c d) -> p c d", d=HD),
                                                     AX, ALU.add))
                            if n == 0:
                                eng.engine_nop().then_inc(s_wl, 1)
                        eng.engine_nop().then_inc(s_wa, 1)
                        eng.wait_ge(s_eg, 16 * SB)
                        do(eng.tensor_copy(ef[:, :, :, :], eg[:, :, :].rearrange("p k (n e) -> p k n e", n=3)))
                        do.put(eng.scalar_tensor_tensor(ix[:, :, 0, :], ef[:, :, 0, :], float(R), ef[:, :, 1, :],
                                                        ALU.mult, ALU.add))
                        do.put(eng.tensor_copy(ix[:, :, 1, :], ef[:, :, 1, :]))
                        do(eng.tensor_tensor(ix[:, :, 2, :], ef[:, :, 2, :],
                                             win[:, :].unsqueeze(2).to_broadcast([P, SB, P]), ALU.subtract))
                        eng.engine_nop().then_inc(s_ix, 1)
                        do.put(eng.tensor_copy(dlb16[:, :, :], ix[:, :, 2, :]))
                        do.put(eng.tensor_scalar(ef[:, :, 0, :], ix[:, :, 2, :], 0.0, None, ALU.is_ge))
                        do(eng.tensor_scalar(ef[:, :, 1, :], ix[:, :, 2, :], float(P), None, ALU.is_lt))
                        do(eng.tensor_tensor(ef[:, :, 0, :], ef[:, :, 0, :], ef[:, :, 1, :], ALU.mult))
                        do(eng.scalar_tensor_tensor(keys[:, :, :], ef[:, :, 2, :], 1.0, ef[:, :, 0, :],
                                                    ALU.add, ALU.mult))
                        do.put(eng.memset(brk[:, :, 0:1], 0.0))
                        do.put(eng.memset(brk[:, :, P:P + 1], 0.0))
                        do(eng.tensor_tensor(brk[:, :, 1:P], keys[:, :, 1:P], keys[:, :, 0:P - 1], ALU.not_equal))
                        do(eng.tensor_scalar(brk[:, :, 1:P], brk[:, :, 1:P], -BIG, None, ALU.mult))
                        eng.engine_nop().then_inc(s_br, 1)
                        do.put(eng.tensor_reduce(summ[:, :, 1], keys[:, :, :], AX, ALU.min))
                        do(eng.tensor_reduce(summ[:, :, 2], keys[:, :, :], AX, ALU.max))
                        do(eng.tensor_tensor(summ[:, :, 0], summ[:, :, 1], summ[:, :, 2], ALU.is_equal))
                        do.put(eng.tensor_copy(summ[:, :, 1], keys[:, :, 0]))
                        do.put(eng.tensor_copy(summ[:, :, 2], keys[:, :, P - 1]))
                        do(eng.tensor_copy(summ[:, :, 3], ix[:, :, 2, 0]))
                        eng.engine_nop().then_inc(s_sm, 1)
                        eng.wait_ge(s_le, NW)
                        do(eng.tensor_copy(er3[:, 0, :, :], lts[:, :, 1, :]))
                        do(eng.tensor_copy(ert[:, 0, :, :], er3[:, 0, :, :]))
                        do(eng.tensor_tensor(ert[:, 1, :, :], lts[:, :, 1, :], ert[:, 0, :, :], ALU.subtract))
                        do(eng.tensor_copy(er3[:, 1, :, :], ert[:, 1, :, :]))
                        do(eng.tensor_copy(ert[:, 0, :, :], er3[:, 1, :, :]))
                        do(eng.tensor_tensor(er3[:, 2, :, :], ert[:, 1, :, :], ert[:, 0, :, :], ALU.subtract))
                        eng.wait_ge(s_te, NW + 2 * SB)
                        S = SB * P
                        do(eng.memset(flag[:, :, :], 0.0))
                        do(eng.tensor_tensor(flag[:, 0, 1:S], rows[:, 1, 1:S], rows[:, 2, 0:S - 1], ALU.is_equal))
                        do.put(eng.tensor_tensor(flag[:, 1, :], flag[:, 0, :], rows[:, 0, :], ALU.mult))
                        do.put(eng.tensor_tensor(flag[:, 2, 0:S - 1], flag[:, 0, 1:S], rows[:, 0, 0:S - 1], ALU.mult))
                        do(eng.tensor_copy(flag[:, 3, 0:S - 1], flag[:, 0, 1:S]))
                        do(eng.tensor_scalar(rows[:, 1, :], rows[:, 1, :], 0.0, None, ALU.is_gt))
                        do(eng.tensor_tensor(rows[:, 1, :], rows[:, 1, :], flag[:, 0, :], ALU.mult))
                        do(eng.scalar_tensor_tensor(rows[:, 3, :], rows[:, 3, :], 1.0, rows[:, 1, :],
                                                    ALU.add, ALU.mult))
                        do(eng.tensor_scalar(crow[:, 0, :], rows[:, 3, 0:SLOTS:C], 1.0, None, ALU.subtract))
                        eng.engine_nop().then_inc(s_cr, 1)
                        do(eng.tensor_scalar(flag[:, :, :], flag[:, :, :], 1.0, BIG, ALU.subtract, ALU.mult))
                        eng.wait_ge(s_cntp, 2)
                        do(eng.tensor_scalar(cross[:, :], psx[:, 0:NC], iota_p[:, 0:1], None, ALU.is_equal))
                        eng.wait_ge(s_xn, NW)
                        eng.wait_ge(s_hb, 16)
                        do(eng.tensor_tensor(xb[:, :, :], xt[:, :, :],
                                             hb[:, :].unsqueeze(1).to_broadcast([P, NW, D]), ALU.add))

            fsb = sb("fsb", [P, 2, R, ROW], F32, st1)
            stg = sb("stg", [P, 2, KD, P], F32, st1)
            dlb = sb("dlb", [P, 3, EG * P], BF16, st1)
            sel = sb("sel", [P, 3 * EG * P], BF16, st1)
            tmask = sb("tmask", [P, EG, R], F32, st1)
            tprod = sb("tprod", [P, EG, R, H], F32, st1)
            with ExitStack() as c2:
                psf = [pb(f"psf{i}", c2) for i in range(4)]
                pse = pb("pse2", c2, (P, 1024))
                s_stg = sem("node_tile_staged")
                s_f = sem("features_done")
                s_fa = sem("features_copied")
                s_fl = sem("source_logits_copied")
                s_fs = [sem(f"features_stored{i}") for i in range(2)]
                s_dl = [sem(f"targets_spread{i}") for i in range(3)]
                s_st = sem("selectors_ready")
                s_eu = sem("slots_looked_up")
                s_ev = sem("lookups_copied")
                s_tm = sem("lookup_steps")

                with nc.Block() as block:
                    @block.tensor
                    def _(eng):
                        wreg = eng.alloc_register("lookup_window")
                        eng.reg_mov(wreg, 0)

                        def tile(w, b):
                            eng.wait_ge(s_stg, w + 1)
                            for c in range(4):
                                eng.wait_ge(s_fa, w * 4 + c + 1)
                                for k in range(KD):
                                    mm = eng.matmul(psf[c][:, :], stg[:, b, k, :],
                                                    wsb[:, k, 2 * c:2 * c + 2, :].rearrange("p r d -> p (r d)"),
                                                    start=(k == 0), stop=(k == KD - 1))
                                mm.then_inc(s_f, 1)

                        def lookups(n, u, half):
                            fresh = eng.value_load(new_in_group[0:1, bass.ds(n, 1)], min_val=0, max_val=255)
                            eng.wait_ge(s_st, n + 3)
                            eng.wait_ge(s_ev, n + 1)
                            for q in range(EG // 2):
                                eng.reg_add(wreg, wreg, (fresh >> q) & 1)
                                w = eng.snap(wreg, min_val=0, max_val=NW - 1)
                                for j in range(2):
                                    s = 2 * q + j
                                    for m in range(3):
                                        mm = eng.matmul(pse[:, half * 512 + s * RH:half * 512 + (s + 1) * RH],
                                                        sel[:, (u * EG + s) * P:(u * EG + s + 1) * P],
                                                        er3[:, m, bass.ds(w, 1), :].rearrange("p a c -> p (a c)"),
                                                        start=(m == 0), stop=(m == 2))
                            mm.then_inc(s_eu, EG)

                        with eng.Fori(0, NEG // 6) as i:
                            for u in range(6):
                                tile(i * 6 + u, u % 2)
                                lookups(i * 6 + u, u % 3, u % 2)
                        for n in range(NEG // 6 * 6, NEG):
                            lookups(n, n % 3, n % 2)

                    @block.scalar
                    def _(eng):
                        eng.copy(stg[:, 0, :, :], xnT[:, :, 0:P]).then_inc(s_stg, 1)
                        with eng.Fori(0, NW // 2) as v:
                            for b in range(2):
                                w = v * 2 + b
                                eng.copy(stg[:, 1 - b, :, :], xnT[:, :, bass.ds(w * P + P, P)]).then_inc(s_stg, 1)
                                eng.copy(fsb[:, b, :, D:ROW], lts[:, bass.ds(w, 1), 0, :]
                                         .rearrange("p a (r h) -> p (a r) h", r=R)).then_inc(s_fl, 1)
                                for c in range(4):
                                    eng.wait_ge(s_f, w * 4 + c + 1)
                                    eng.copy(fsb[:, b, 2 * c:2 * c + 2, 0:D],
                                             psf[c][:, :].rearrange("p (r d) -> p r d", r=2)).then_inc(s_fa, 1)
                                eng.wait_ge(s_fl, w + 1)
                                eng.wait_ge(s_fa, w * 4 + 8)
                                eng.dma_start(feat[bass.ds(w * P, P), :],
                                              fsb[:, b, :, :].rearrange("p r d -> p (r d)")).then_inc(s_fs[b], 16)
                            for b in range(2):
                                eng.wait_ge(s_fs[b], v * 16 + 16)

                    @block.sync
                    def _(eng):
                        def load(rows_ap, u):
                            eng.dma_start(dlb[:, u, :], rows_ap.rearrange("s e -> (s e)").partition_broadcast(P))\
                               .then_inc(s_dl[u], 16)

                        load(dloc_rows[0:EG, :], 0)
                        with eng.Fori(0, NEG // 3) as i:
                            for u in range(3):
                                n = i * 3 + u
                                eng.wait_ge(s_st, n + 1)
                                load(dloc_rows[bass.ds(n * EG + EG, EG), :], (u + 1) % 3)
                        for u in range(3):
                            eng.wait_ge(s_dl[u], 16 * (NEG // 3) + (16 if u == 0 else 0))

                    @block.vector
                    def _(eng):
                        eng.engine_nop().then_inc(s_fa, 4)
                        eng.engine_nop().then_inc(s_st, 2)
                        eng.engine_nop().then_inc(s_ev, 2)
                        eng.engine_nop().then_inc(s_eu, 3 * EG)

                        def selectors(u):
                            eng.tensor_scalar(sel[:, u * EG * P:(u + 1) * EG * P], dlb[:, u, :], iota_p[:, 0:1], None,
                                              ALU.is_equal).then_inc(s_st, 1)

                        eng.wait_ge(s_dl[0], 16)
                        selectors(0)
                        with eng.Fori(0, NEG // 3) as i:
                            for u in range(3):
                                n = i * 3 + u
                                eng.wait_ge(s_dl[(u + 1) % 3], i * 16 + (32 if u == 2 else 16))
                                eng.wait_ge(s_eu, n * EG + EG)
                                selectors((u + 1) % 3)
                                eng.tensor_tensor(tmask[:, :, :], iota_f[:, 0:R].unsqueeze(1).to_broadcast([P, EG, R]),
                                                  etyp[:, bass.ds(n * EG, EG)].unsqueeze(2).to_broadcast([P, EG, R]),
                                                  ALU.is_equal).then_inc(s_tm, 1)
                                eng.wait_ge(s_tm, n * 2 + 1)
                                eng.wait_ge(s_eu, n * EG + 4 * EG)
                                eng.tensor_tensor(tprod[:, :, :, :],
                                                  pse[:, bass.ds((n % 2) * 512, 512)]
                                                  .rearrange("p (s r h) -> p s r h", s=EG, r=R),
                                                  tmask[:, :, :].unsqueeze(3).to_broadcast([P, EG, R, H]),
                                                  ALU.mult).then_inc(s_tm, 1)
                                eng.wait_ge(s_tm, n * 2 + 2)
                                eng.tensor_reduce(er_all[:, bass.ds(n * EG, EG), :],
                                                  tprod[:, :, :, :].rearrange("p s r h -> p s h r"),
                                                  AX, ALU.add).then_inc(s_ev, 1)
                        eng.wait_ge(s_ev, NEG + 2)

        hacc = sb("hacc", [P, NW, ROW], F32)
        with ExitStack() as c4:
            hcell = sb("hcell", [P, CELLS, ROW], F32, c4)
            G = sb("G", [P, RING, ROW], F32, c4)
            OH = sb("OH", [P, C, P], F32, c4)
            ir2 = sb("ir2", [P, QUADS, HALF], I32, c4)
            onesr = sb("onesr", [1, P], F32, c4)
            eraw = sb("eraw", [P, C, H], F32, c4)
            elog = sb("elog", [P, H, C], F32, c4)
            bkc = sb("bkc", [HC, P + 1], F32, c4)
            flc = sb("flc", [1, 4, C], F32, c4)
            fw = sb("fw", [HC, P], F32, c4)
            bw = sb("bw", [HC, P], F32, c4)
            ends = sb("ends", [1, H, C + 1], F32, c4)
            begs = sb("begs", [1, H, C + 1], F32, c4)
            incr = sb("incr", [1, 2, H, C], F32, c4)
            inc = sb("inc", [HC, 2], F32, c4)
            down = sb("down", [1, H], F32, c4)
            downe = sb("downe", [1, H], F32, c4)
            resc = sb("resc", [P, H], F32, c4)
            wrow = sb("wrow", [HC, P], F32, c4)
            psh = pb("psh", c4, (P, 1024))
            psE = pb("psE", c4)
            psR = pb("psR", c4)
            psI = pb("psI", c4)
            psX = pb("psX", c4)
            s_gs = [sem(f"rows_gathered{j}") for j in range(2)]
            s_ir2 = sem("index_ring")
            s_use = sem("slots_summed")
            s_bank = sem("cell_banks_free")
            s_wt = sem("slots_selected")
            s_g = sem("rows_weighted")
            s_win = sem("cells_summed")
            s_z = sem("window_sums_cleared")
            s_st3 = sem("chunk_steps")
            s_t1 = sem("logits_turned")
            s_t2 = sem("segment_ends_turned")
            s_t3 = sem("carries_turned")
            s_t4 = sem("weights_turned")
            s_e1 = sem("logits_ready")
            s_e2 = sem("segment_ends_ready")
            s_e3 = sem("carries_ready")
            s_e4 = sem("maxima_subtracted")
            s_x1 = sem("rescale_exp_done")
            s_x2 = sem("weights_exp_done")
            s_x3 = sem("weights_placed")
            s_bf = sem("breaks_and_flags_ready")
            s_sv = sem("rescale_column_ready")
            s_mg = sem("cell_merge_steps")

            with nc.Block() as block:
                @block.gpsimd
                def _(eng):
                    eng.memset(hacc[:, :, :], 0.0).then_inc(s_z, 1)
                    eng.memset(onesr[:, :], 1.0).then_inc(s_z, 1)
                    eng.tensor_copy(ir2[:, 0, :], el_idx[:, 0:HALF]).then_inc(s_ir2, 1)
                    with eng.Fori(0, NC // 2) as i:
                        for q in range(QUADS):
                            m = i * QUADS + q
                            eng.wait_ge(s_ir2, m + 1)
                            eng.wait_ge(s_use, m * HALF + HALF)
                            eng.wait_ge(s_e1, i * 2 + q // 2 + q % 2 + 1)
                            eng.tensor_tensor(ir2[:, (q + 1) % QUADS, :], el_idx[:, bass.ds((m + 1) * HALF, HALF)],
                                              zero_i[:, :], ALU.add).then_inc(s_ir2, 1)
                            for j in range(HALF):
                                eng.indirect_dma_start(G[:, q * HALF + j, :], None, feat_rows,
                                                       bass.IndirectOffsetOnAxis(ap=ir2[:, q, j:j + 1], axis=0))\
                                   .then_inc(s_gs[q // 2], 16)
                    for b in range(2):
                        eng.wait_ge(s_gs[b], (NC // 2) * C * 16)

                @block.tensor
                def _(eng):
                    eng.wait_ge(s_z, 2)
                    cell = eng.alloc_register("open_cell")
                    eng.reg_mov(cell, 0)

                    def bank_of(at):
                        return psh[:, bass.ds((at & 1) * 512, ROW)]

                    def open_cell():
                        at = eng.snap(cell, min_val=0, max_val=NW + NC)
                        eng.wait_ge(s_bank, at + 1)
                        eng.matmul(bank_of(at), zero16[0:1, 0:P], zero16[0:1, :], start=True, stop=False)

                    def close_cell():
                        at = eng.snap(cell, min_val=0, max_val=NW + NC)
                        eng.matmul(bank_of(at), zero16[0:1, 0:P], zero16[0:1, :], start=False, stop=True)\
                           .then_inc(s_win, 1)
                        eng.reg_add(cell, cell, 1)

                    def chunk(i, b):
                        c = i * 2 + b
                        fresh = eng.value_load(new_in_chunk[0:1, bass.ds(c, 1)], min_val=0, max_val=2 ** CP2 - 1)
                        eng.wait_ge(s_e1, c + 3)
                        eng.transpose(psE[0:HC, 0:P], elog[:, :, :].rearrange("p h s -> p (h s)"), ident[:, :])\
                           .then_inc(s_t1, 1)
                        eng.wait_ge(s_e2, c + 1)
                        eng.transpose(psR[0:1, 0:HC], fw[:, P - 1:P], ident[0:HC, 0:HC])
                        eng.transpose(psR[0:1, P:P + HC], bw[:, 0:1], ident[0:HC, 0:HC]).then_inc(s_t2, 1)
                        eng.wait_ge(s_e3, c + 1)
                        eng.wait_ge(s_x1, c + 1)
                        eng.matmul(psI[:, 2:2 + H], onesr[:, :], downe[:, :], start=True, stop=True)
                        for n in range(2):
                            tr = eng.transpose(psI[0:HC, n:n + 1], incr[:, n, :, :].rearrange("p h s -> p (h s)"),
                                               ident[0:1, 0:1])
                        tr.then_inc(s_t3, 1)
                        eng.wait_ge(s_x2, c + 1)
                        eng.transpose(psX[:, 0:HC], wrow[:, :], ident[0:HC, 0:HC]).then_inc(s_t4, 1)
                        open_cell()
                        for q in range(CP2):
                            if q > 0:
                                with eng.If((fresh >> q) & 1):
                                    close_cell()
                                    open_cell()
                            at = eng.snap(cell, min_val=0, max_val=NW + NC)
                            if q % 2 == 0:
                                eng.wait_ge(s_wt, c * (CP2 // 2) + q // 2 + 1)
                            for u in range(2):
                                j = 2 * q + u
                                eng.matmul(bank_of(at), OH[:, j, :], G[:, b * C + j, :], start=False, stop=False)\
                                   .then_inc(s_use, 1)
                        close_cell()

                    with eng.Fori(0, NC // 2) as i:
                        for b in range(2):
                            chunk(i, b)

                @block.scalar
                def _(eng):
                    with eng.Fori(0, NC // 2) as i:
                        for b in range(2):
                            c = i * 2 + b
                            info = eng.value_load(chunk_info[0:1, bass.ds(c, 1)], min_val=0, max_val=32767)
                            wl, wh, off = info & 31, (info >> 5) & 31, info >> 10
                            eng.wait_ge(s_sv, c * 5 + 5)
                            eng.copy(bkc[:, :], brkt[:, bass.ds(c, 1), :].rearrange("p a e -> p (a e)"))\
                               .then_inc(s_bf, 1)
                            eng.copy(flc[:, :, :], flag[:, :, bass.ds(c * C, C)]).then_inc(s_bf, 1)
                            eng.wait_ge(s_e3, c + 1)
                            eng.activation(downe[:, :], down[:, :], ACT.Exp, bias=zrow[0:1, 0:1]).then_inc(s_x1, 1)
                            eng.wait_ge(s_e4, c + 1)
                            eng.activation(wrow[:, :], wrow[:, :], ACT.Exp, bias=zrow[0:HC, 0:1]).then_inc(s_x2, 1)
                            eng.wait_ge(s_t4, c + 1)
                            eng.copy(G[:, b * C:(b + 1) * C, D:ROW].rearrange("p s h -> p h s"),
                                     psX[:, 0:HC].rearrange("p (h s) -> p h s", h=H)).then_inc(s_x3, 1)
                            with eng.Fori(wl, wh + 1) as wv:
                                w = nc.s_assert_within(wv, 0, NW - 1,
                                                       skip_runtime_bounds_check_because="first and last are windows")
                                j = w + off
                                eng.wait_ge(s_win, j + 1)
                                eng.wait_ge(s_mg, j * 3 + 3)
                                eng.copy(hcell[:, bass.ds(j & (CELLS - 1), 1), :].rearrange("p a d -> p (a d)"),
                                         psh[:, bass.ds((j & 1) * 512, ROW)]).then_inc(s_bank, 1)

                @block.vector
                def _(eng):
                    eng.engine_nop().then_inc(s_use, RING)
                    eng.engine_nop().then_inc(s_bank, 2)
                    eng.engine_nop().then_inc(s_sv, 5)
                    eng.engine_nop().then_inc(s_e1, 2)
                    eng.engine_nop().then_inc(s_mg, 3 * CELLS)
                    K = 15
                    eng.memset(ends[:, :, 0:1], -BIG).then_inc(s_st3, 1)
                    eng.memset(begs[:, :, C:C + 1], -BIG).then_inc(s_st3, 1)
                    eng.wait_ge(s_z, 2)
                    with eng.Fori(0, NC // 2) as i:
                        for b in range(2):
                            c = i * 2 + b
                            s0 = c * C
                            n = [0]

                            def step(ins, c=c, n=n):
                                ins.then_inc(s_st3, 1)
                                n[0] += 1

                            def done(c=c, n=n):
                                eng.wait_ge(s_st3, c * K + n[0] + 2)

                            info = eng.value_load(chunk_info[0:1, bass.ds(c, 1)], min_val=0, max_val=32767)
                            wl, wh, off = info & 31, (info >> 5) & 31, info >> 10
                            eng.wait_ge(s_gs[b], i * (C * 16) + C * 16)
                            step(eng.tensor_tensor(eraw[:, :, :], G[:, b * C:(b + 1) * C, D:ROW],
                                                   er_all[:, bass.ds(s0, C), :], ALU.add))
                            done()
                            eng.scalar_tensor_tensor(elog[:, :, :].rearrange("p h s -> p s h"), eraw[:, :, :], 0.2,
                                                     eraw[:, :, :], ALU.mult, ALU.max).then_inc(s_e1, 1)
                            eng.wait_ge(s_t1, c + 1)
                            eng.wait_ge(s_bf, c * 2 + 2)
                            bk = bkc
                            step(eng.tensor_tensor_scan(fw[:, :], bk[:, 0:P], psE[0:HC, 0:P], -BIG, ALU.add, ALU.max))
                            eng.tensor_tensor_scan(bw[:, ::-1], bk[:, P:0:-1], psE[0:HC, P - 1::-1], -BIG,
                                                   ALU.add, ALU.max).then_inc(s_e2, 1)
                            eng.wait_ge(s_t2, c + 1)
                            fl = [flc[:, m, :] for m in range(4)]
                            for h in range(H):
                                step(eng.tensor_tensor_scan(ends[:, h, 1:C + 1], fl[1], psR[0:1, h * C:(h + 1) * C],
                                                            ends[:, h, 0:1], ALU.add, ALU.max))
                                step(eng.tensor_tensor_scan(begs[:, h, C - 1::-1], fl[2][:, ::-1],
                                                            psR[0:1, P + h * C:P + (h + 1) * C][:, ::-1], -BIG,
                                                            ALU.add, ALU.max))
                            done()
                            step(eng.tensor_tensor(down[:, :], ends[:, :, 0], begs[:, :, 0], ALU.max))
                            step(eng.tensor_tensor(incr[:, 0, :, :], ends[:, :, 0:C],
                                                   fl[0].unsqueeze(1).to_broadcast([1, H, C]), ALU.add))
                            step(eng.tensor_tensor(incr[:, 1, :, :], begs[:, :, 1:C + 1],
                                                   fl[3].unsqueeze(1).to_broadcast([1, H, C]), ALU.add))
                            done()
                            eng.tensor_tensor(down[:, :], ends[:, :, 0], down[:, :], ALU.subtract).then_inc(s_e3, 1)
                            eng.wait_ge(s_e3, c + 1)
                            step(eng.tensor_copy(ends[:, :, 0:1], ends[:, :, C:C + 1]))
                            eng.wait_ge(s_t3, c + 1)
                            step(eng.tensor_copy(inc[:, :], psI[0:HC, 0:2]))
                            done()
                            eng.tensor_scalar(resc[:, :], psI[:, 2:2 + H], 1.0, cross[:, bass.ds(c, 1)],
                                              ALU.subtract, ALU.mult).then_inc(s_sv, 1)
                            eng.tensor_tensor_scan(fw[:, :], bk[:, 0:P], psE[0:HC, 0:P], inc[:, 0:1],
                                                   ALU.add, ALU.max).then_inc(s_sv, 1)
                            eng.tensor_tensor_scan(bw[:, ::-1], bk[:, P:0:-1], psE[0:HC, P - 1::-1], inc[:, 1:2],
                                                   ALU.add, ALU.max).then_inc(s_sv, 1)
                            eng.wait_ge(s_sv, c * 5 + 8)
                            eng.tensor_scalar(resc[:, :], resc[:, :], 1.0, None, ALU.add).then_inc(s_sv, 1)
                            eng.tensor_tensor(fw[:, :], fw[:, :], bw[:, :], ALU.max).then_inc(s_sv, 1)
                            eng.wait_ge(s_sv, c * 5 + 10)
                            eng.tensor_tensor(wrow[:, :], psE[0:HC, 0:P], fw[:, :], ALU.subtract).then_inc(s_e4, 1)
                            assert n[0] == K, n
                            eng.wait_ge(s_x3, c + 1)
                            for q in range(C // 4):
                                j = b * C + 4 * q
                                g = G[:, j:j + 4, 0:D].rearrange("p s (h d) -> p s h d", h=H)
                                eng.tensor_tensor(g, g, G[:, j:j + 4, D:ROW].unsqueeze(3).to_broadcast([P, 4, H, HD]),
                                                  ALU.mult).then_inc(s_g, 1)
                                eng.wait_ge(s_use, s0 + 4 * q + 4 + RING - C)
                                eng.wait_ge(s_g, c * (C // 4) + q + 1)
                                eng.tensor_tensor(OH[:, 4 * q:4 * q + 4, :],
                                                  iota_f[:, :].unsqueeze(1).to_broadcast([P, 4, P]),
                                                  dloc[:, bass.ds(s0 + 4 * q, 4)].unsqueeze(2).to_broadcast([P, 4, P]),
                                                  ALU.is_equal).then_inc(s_wt, 1)
                            with eng.Fori(wl, wh + 1) as wv:
                                w = nc.s_assert_within(wv, 0, NW - 1,
                                                       skip_runtime_bounds_check_because="first and last are windows")
                                j = w + off
                                eng.wait_ge(s_bank, j + 3)
                                acc_d = hacc[:, bass.ds(w, 1), 0:D].rearrange("p a (h d) -> p (a h) d", h=H)
                                acc_s = hacc[:, bass.ds(w, 1), D:ROW].rearrange("p a h -> p (a h)")
                                acc_w = hacc[:, bass.ds(w, 1), :]
                                eng.tensor_tensor(acc_d, acc_d, resc[:, :].unsqueeze(2).to_broadcast([P, H, HD]),
                                                  ALU.mult).then_inc(s_mg, 1)
                                eng.tensor_tensor(acc_s, acc_s, resc[:, :], ALU.mult).then_inc(s_mg, 1)
                                eng.wait_ge(s_mg, j * 3 + 2 + 3 * CELLS)
                                eng.tensor_tensor(acc_w, acc_w, hcell[:, bass.ds(j & (CELLS - 1), 1), :], ALU.add).then_inc(s_mg, 1)
                                eng.wait_ge(s_mg, j * 3 + 3 + 3 * CELLS)
                    eng.wait_ge(s_g, SLOTS // 4)

        w1s = sb("w1s", [P, KD, X, D], F32)
        w2s = sb("w2s", [P, KD, X, D], F32)
        b1s = sb("b1s", [P, X, KD], F32)
        b2s = sb("b2s", [X, D], F32)
        rws = sb("rws", [P, KD, X], F32)
        s_fw = sem("expert_weights_loaded")
        with nc.Block() as block:
            @block.sync
            def _(eng):
                with nc.allow_non_contiguous_dma(reason="small transposed loads"):
                    eng.dma_start(b1s[:, :, :], b1.rearrange("e (k p) -> p e k", p=P)).then_inc(s_fw, 16)
                    for k in range(KD):
                        eng.dma_start(rws[:, k, :], router_w[:, k * P:(k + 1) * P].rearrange("e p -> p e"))\
                           .then_inc(s_fw, 16)
                eng.dma_start(b2s[:, :], b2).then_inc(s_fw, 16)
                for k in range(KD):
                    eng.dma_start(w1s[:, k, :, :], w1[:, k * P:(k + 1) * P, :].rearrange("e p d -> p e d"))\
                       .then_inc(s_fw, 16)
                    eng.dma_start(w2s[:, k, :, :], w2[:, k * P:(k + 1) * P, :].rearrange("e p d -> p e d"))\
                       .then_inc(s_fw, 16)
                eng.wait_ge(s_fw, 16 * (2 + 3 * KD))

        TG = 3
        GN = TG * P
        xt2 = sb("xt2", [P, KD, NP], F32)
        comb = sb("comb", [P, NW, X], F32)
        acc = xb
        with ExitStack() as c5:
            prob = sb("prob", [P, NW, X], F32, c5)
            mk = sb("mk", [P, NW, X], F32, c5)
            mk2 = sb("mk2", [P, NW, X], F32, c5)
            top = sb("top", [P, NW, 8], F32, c5)
            topi = sb("topi", [P, NW, 8], U32, c5)
            topf = sb("topf", [P, NW, 8], F32, c5)
            r1 = sb("r1", [P, NW], F32, c5)
            r2 = sb("r2", [P, NW], F32, c5)
            stat = sb("stat5", [P, NW, 6], F32, c5)
            mv = sb("mv5", [P, NW, 2], F32, c5)
            cT = sb("cT", [X, 2, P], F32, c5)
            pst = [pb(f"pt5{i}", c5) for i in range(4)]
            psl = pb("pl5", c5)
            psc = [pb(f"pc5{i}", c5) for i in range(2)]
            s_d5 = sem("vector_steps_5")
            s_var5 = sem("variance_ready_5")
            s_std5 = sem("std_ready_5")
            s_xn5 = sem("xn_ready_5")
            s_t5 = sem("transposes_done_5")
            s_c5 = sem("transposes_copied_5")
            s_lg = sem("router_logits_done")
            s_sh = sem("router_shifted")
            s_ex5 = sem("router_exp_done")
            s_cm = sem("combine_ready")
            s_ct = sem("combine_turned")
            s_cc = sem("combine_copied")
            s_b2 = sem("bias_rows_done")
            s_ba = sem("bias_rows_added")

            with nc.Block() as block:
                @block.vector
                def _(eng):
                    do = Chain(eng, s_d5)
                    dn = hacc[:, :, D:ROW]
                    do(eng.tensor_scalar(dn, dn, 0.5, None, ALU.max))
                    do(eng.reciprocal(dn, dn))
                    for t in range(NW):
                        g = hacc[:, t, 0:D].rearrange("p (h d) -> p h d", h=H)
                        do.put(eng.tensor_tensor(g, g, hacc[:, t, D:ROW].unsqueeze(2).to_broadcast([P, H, HD]),
                                                 ALU.mult))
                    do.sync()
                    do(eng.tensor_tensor(xb[:, :, :], xb[:, :, :], hacc[:, :, 0:D], ALU.add))
                    for t in range(NW):
                        do.put(eng.bn_stats(stat[:, t, :], xb[:, t, :]))
                    do.sync()
                    for t in range(NW):
                        do.put(eng.bn_aggr(mv[:, t, :], stat[:, t, :]))
                    do.sync()
                    eng.engine_nop().then_inc(s_var5, 1)
                    eng.wait_ge(s_std5, 1)
                    do(eng.reciprocal(r2[:, :], r1[:, :]))
                    for t in range(NW):
                        eng.tensor_scalar(hacc[:, t, 0:D], xb[:, t, :], mv[:, t, 0:1], r2[:, t:t + 1],
                                          ALU.subtract, ALU.mult).then_inc(s_xn5, 1)
                    eng.wait_ge(s_xn5, NW)
                    do(eng.tensor_tensor(acc[:, :, :], xb[:, :, :], hacc[:, :, 0:D], ALU.add))
                    eng.wait_ge(s_lg, 1)
                    do(eng.tensor_copy(prob[:, :, :].rearrange("p t e -> p (t e)"), psl[:, 0:NW * X]))
                    do(eng.tensor_reduce(r2[:, :], prob[:, :, :], AX, ALU.max))
                    do(eng.tensor_tensor(prob[:, :, :], prob[:, :, :],
                                         r2[:, :].unsqueeze(2).to_broadcast([P, NW, X]), ALU.subtract))
                    eng.engine_nop().then_inc(s_sh, 1)
                    eng.wait_ge(s_ex5, 1)
                    do(eng.tensor_reduce(r2[:, :], prob[:, :, :], AX, ALU.add))
                    do(eng.reciprocal(r2[:, :], r2[:, :]))
                    do(eng.tensor_tensor(prob[:, :, :], prob[:, :, :],
                                         r2[:, :].unsqueeze(2).to_broadcast([P, NW, X]), ALU.mult))
                    for t in range(NW):
                        do.put(eng.max(top[:, t, :], prob[:, t, :]))
                    do.sync()
                    for t in range(NW):
                        do.put(eng.max_index(topi[:, t, :], top[:, t, :], prob[:, t, :]))
                    do.sync()
                    do(eng.tensor_copy(topf[:, :, :], topi[:, :, :]))
                    lane = iota_f[:, 0:X].unsqueeze(1).to_broadcast([P, NW, X])
                    do.put(eng.tensor_tensor(mk[:, :, :], lane, topf[:, :, 0:1].to_broadcast([P, NW, X]),
                                             ALU.is_equal))
                    do.put(eng.tensor_tensor(mk2[:, :, :], lane, topf[:, :, 1:2].to_broadcast([P, NW, X]),
                                             ALU.is_equal))
                    do(eng.tensor_tensor(r2[:, :], top[:, :, 0], top[:, :, 1], ALU.add))
                    do.put(eng.tensor_tensor(mk[:, :, :], mk[:, :, :], mk2[:, :, :], ALU.add))
                    do(eng.tensor_scalar(r2[:, :], r2[:, :], 1e-12, None, ALU.max))
                    do.put(eng.reciprocal(r1[:, :], r2[:, :]))
                    do(eng.tensor_tensor(mk[:, :, :], mk[:, :, :], prob[:, :, :], ALU.mult))
                    do(eng.tensor_tensor(comb[:, :, :], mk[:, :, :],
                                         r1[:, :].unsqueeze(2).to_broadcast([P, NW, X]), ALU.mult))
                    eng.engine_nop().then_inc(s_cm, 1)
                    for t in range(NW):
                        eng.wait_ge(s_b2, t + 1)
                        eng.tensor_tensor(acc[:, t, :], acc[:, t, :], psc[t % 2][:, 0:D], ALU.add).then_inc(s_ba, 1)
                    eng.wait_ge(s_ba, NW)

                @block.scalar
                def _(eng):
                    eng.wait_ge(s_var5, 1)
                    eng.activation(r1[:, :], mv[:, :, 1], ACT.Sqrt, bias=epsv[:, 0:1]).then_inc(s_std5, 1)
                    for t in range(NW):
                        eng.wait_ge(s_t5, t + 1)
                        eng.copy(xt2[:, :, t * P:(t + 1) * P],
                                 pst[t % 4][:, 0:2 * P].rearrange("p (k n) -> p k n", k=KD)).then_inc(s_c5, 1)
                    eng.wait_ge(s_sh, 1)
                    eng.activation(prob[:, :, :], prob[:, :, :], ACT.Exp, bias=zrow[:, 0:1]).then_inc(s_ex5, 1)
                    for t in range(NW):
                        eng.wait_ge(s_ct, t + 1)
                        if t >= 2:
                            eng.wait_ge(s_b2, t - 1)
                        eng.copy(cT[:, t % 2, :], pst[t % 4][0:X, 0:P]).then_inc(s_cc, 1)

                @block.tensor
                def _(eng):
                    for t in range(NW):
                        eng.wait_ge(s_xn5, t + 1)
                        if t >= 4:
                            eng.wait_ge(s_c5, t - 3)
                        for k in range(KD):
                            tr = eng.transpose(pst[t % 4][:, k * P:(k + 1) * P], hacc[:, t, k * P:(k + 1) * P],
                                               ident[:, :])
                        tr.then_inc(s_t5, 1)
                    eng.wait_ge(s_c5, NW)
                    for t in range(NW):
                        for k in range(KD):
                            mm = eng.matmul(psl[:, t * X:(t + 1) * X], xt2[:, k, t * P:(t + 1) * P], rws[:, k, :],
                                            start=(k == 0), stop=(k == KD - 1))
                    mm.then_inc(s_lg, 1)
                    eng.wait_ge(s_cm, 1)
                    for t in range(NW + 1):
                        if t < NW:
                            if t >= 4:
                                eng.wait_ge(s_cc, t - 3)
                            eng.transpose(pst[t % 4][0:X, 0:P], comb[:, t, :], ident[:, :]).then_inc(s_ct, 1)
                        if t >= 1:
                            eng.wait_ge(s_cc, t)
                            if t >= 3:
                                eng.wait_ge(s_ba, t - 2)
                            eng.matmul(psc[(t - 1) % 2][:, 0:D], cT[:, (t - 1) % 2, :], b2s[:, :],
                                       start=True, stop=True).then_inc(s_b2, 1)

        with ExitStack() as c6:
            hT = sb("hT", [P, 2, KD, GN], F32, c6)
            ph = [[pb(f"ph{i}{j}", c6) for j in range(KD)] for i in range(2)]
            py = [pb(f"py{i}", c6) for i in range(4)]
            s_h = sem("hidden_done")
            s_ge = sem("hidden_activated")
            s_y = sem("expert_rows_done")
            s_ya = sem("expert_rows_added")
            s_out = sem("output_stored")
            NG = NW // TG
            HP = KD * X
            YP = TG * X

            with nc.Block() as block:
                @block.tensor
                def _(eng):
                    with eng.Fori(0, NG) as g:
                        def up(e):
                            for hh in range(KD):
                                eng.wait_ge(s_ge, g * HP + e * KD + hh + 1)
                                for k in range(KD):
                                    mm = eng.matmul(ph[e % 2][hh][:, 0:GN], w1s[:, k, e, hh * P:(hh + 1) * P],
                                                    xt2[:, k, bass.ds(g * GN, GN)],
                                                    start=(k == 0), stop=(k == KD - 1))
                                mm.then_inc(s_h, 1)

                        def down(e):
                            eng.wait_ge(s_ge, g * HP + (e + 1) * KD + 2 * KD)
                            for m in range(TG):
                                n = e * TG + m
                                eng.wait_ge(s_ya, g * YP + n + 1)
                                for hh in range(KD):
                                    mm = eng.matmul(py[n % 4][:, 0:D], hT[:, e % 2, hh, m * P:(m + 1) * P],
                                                    w2s[:, hh, e, :], start=(hh == 0), stop=(hh == KD - 1))
                                mm.then_inc(s_y, 1)

                        up(0)
                        for e in range(X):
                            if e + 1 < X:
                                up(e + 1)
                            down(e)

                @block.scalar
                def _(eng):
                    with eng.Fori(0, NG) as g:
                        for e in range(X):
                            eng.wait_ge(s_y, g * YP + e * TG + TG)
                            for hh in range(KD):
                                eng.wait_ge(s_h, g * HP + e * KD + hh + 1)
                                eng.activation(hT[:, e % 2, hh, :], ph[e % 2][hh][:, 0:GN], ACT.Gelu,
                                               bias=b1s[:, e, hh:hh + 1]).then_inc(s_ge, 1)

                @block.vector
                def _(eng):
                    eng.engine_nop().then_inc(s_ge, 2 * KD)
                    eng.engine_nop().then_inc(s_y, 2 * TG)
                    eng.engine_nop().then_inc(s_ya, 4)
                    with eng.Fori(0, NG) as g:
                        for e in range(X):
                            for m in range(TG):
                                n = e * TG + m
                                eng.wait_ge(s_y, g * YP + n + 1 + 2 * TG)
                                if e:
                                    eng.wait_ge(s_ya, g * YP + n - TG + 1 + 4)
                                a = acc[:, bass.ds(g * TG + m, 1), :].rearrange("p a d -> p (a d)")
                                eng.scalar_tensor_tensor(a, py[n % 4][:, 0:D],
                                                         comb[:, bass.ds(g * TG + m, 1), e], a,
                                                         ALU.mult, ALU.add).then_inc(s_ya, 1)

                @block.sync
                def _(eng):
                    for g in range(NG):
                        eng.wait_ge(s_ya, (g + 1) * YP + 4)
                        for t in range(g * TG, (g + 1) * TG):
                            if t < FULL:
                                eng.dma_start(out[t * P:(t + 1) * P, :], acc[:, t, :]).then_inc(s_out, 16)
                            else:
                                eng.dma_start(out[t * P:N, :], acc[0:REST, t, :]).then_inc(s_out, 16)
                    eng.wait_ge(s_out, 16 * NW)


_INS = ['x', 'src', 'dst', 'edge_type_8', 'L0_gnn_conv_weights', 'L0_gnn_attn_l', 'L0_gnn_attn_r', 'L0_gnn_h_bias',
        'L0_ffn_router_w', 'L0_ffn_w1', 'L0_ffn_b1', 'L0_ffn_w2', 'L0_ffn_b2']
_OUTS = [((3750, 256), 'float32')]


def kernel(**inputs):
    import numpy as _np
    import concourse.bacc as _bacc
    from concourse import mybir as _mybir
    from concourse.bass_utils import run_bass_kernel_spmd as _run

    nc = _bacc.Bacc("TRN2", target_bir_lowering=False, num_devices=1)
    arrays, args = {}, []
    for name in _INS:
        a = _np.ascontiguousarray(inputs[name])
        arrays[f"in_{name}_dram"] = a
        args.append(nc.dram_tensor(f"in_{name}_dram", a.shape, _mybir.dt.from_np(a.dtype), kind="ExternalInput").ap())
    for i, (shape, dtype) in enumerate(_OUTS):
        dt = _mybir.dt.from_np(_np.dtype(dtype))
        args.append(nc.dram_tensor(f"out_{i}_dram", shape, dt, kind="ExternalOutput").ap())
    gnn_moe(nc, *args)
    r = _run(nc, [arrays], core_ids=[0])
    got = tuple(r.results[0][f"out_{i}_dram"] for i in range(len(_OUTS)))
    return got[0]
```

```python
from contextlib import ExitStack

import numpy as np

import concourse.bass as bass
from concourse import mybir

F32, BF16, I32, U32 = mybir.dt.float32, mybir.dt.bfloat16, mybir.dt.int32, mybir.dt.uint32
ALU = mybir.AluOpType
ACT = mybir.ActivationFunctionType
AX = mybir.AxisListType.X

P = 128
BIG = 1.0e30


class Chain:

    def __init__(self, eng, sem):
        self.eng, self.sem, self.n = eng, sem, 0

    def __call__(self, ins):
        ins.then_inc(self.sem, 1)
        self.n += 1
        self.eng.wait_ge(self.sem, self.n)

    def put(self, ins):
        ins.then_inc(self.sem, 1)
        self.n += 1

    def sync(self):
        self.eng.wait_ge(self.sem, self.n)


def gnn_moe(nc, x, src, dst, etype, conv_w, attn_l, attn_r, h_bias, router_w, w1, b1, w2, b2, out):
    N, D = x.shape
    E = src.shape[0]
    R, H, _, HD = conv_w.shape
    RH = R * H
    X = router_w.shape[0]
    KD = D // P
    NW = -(-N // P)
    NP = NW * P
    FULL = N // P
    REST = N - FULL * P
    T = -(-E // P)
    TF = E // P
    TREST = E - TF * P
    PAD_TILE = T
    PAIRS = (T + NW - 1 + NW) // 2
    HALF = 12
    QUADS = 4
    C = 2 * HALF
    RING = 2 * C
    SLOTS = -(-2 * PAIRS // RING) * RING
    PAIRS = SLOTS // 2
    NC = SLOTS // C
    CP2 = C // 2
    EG = 16
    NEG = SLOTS // EG
    HC = H * C
    SB = -(-SLOTS // P)
    ROW = D + H
    CP = 120
    assert NW < 32 and NC < 32 and P == 128 and E % CP == 0 and D == 2 * P and NW % 6 == 0 and SLOTS % (3 * EG) == 0
    EPS = 1e-5
    NCONST = 12 + CP2

    edges = nc.dram_tensor("edge_tiles", [T + 1, 3 * P], I32, kind="Internal").ap()
    feat = nc.dram_tensor("node_rows", [NP, R * ROW], F32, kind="Internal").ap()
    feat_rows = feat.rearrange("n (r d) -> (n r) d", r=R)
    dloc_rows = nc.dram_tensor("slot_targets", [SB * P, P], BF16, kind="Internal").ap()
    brk_rows = nc.dram_tensor("segment_breaks", [SB * P, P + 1], F32, kind="Internal").ap()
    col = lambda a: a.rearrange("(a d) -> a d", a=1)

    with ExitStack() as ctx:
        def sb(name, shape, dt, c=ctx):
            return c.enter_context(nc.sbuf_tensor(name, shape, dt))

        def pb(name, c, shape=(P, 512), dt=F32):
            return c.enter_context(nc.psum_tensor(name, list(shape), dt))

        def sem(name):
            return ctx.enter_context(nc.semaphore(name))

        ident = sb("ident", [P, P], F32)
        iota_f = sb("iota_f", [P, P], F32)
        xbp = sb("xbp", [P, NW + 1, D], F32)
        xb = xbp[:, 1:NW + 1, :]
        el_idx = sb("el_idx", [P, SB * P], I32)
        etyp = sb("etyp", [P, SB * P], F32)
        dloc = sb("dloc", [P, SB * P], F32)
        er_all = sb("er_all", [P, SLOTS, H], F32)
        brkt = sb("brkt", [HC, NC, P + 1], F32)
        flag = sb("flag", [1, 4, SLOTS], F32)
        cross = sb("cross", [P, NC], F32)
        new_in_group = sb("new_in_group", [1, NEG], I32)
        chunk_cells = sb("chunk_cells", [1, NC], I32)
        chunk_info = sb("chunk_info", [1, NC], I32)
        iota_p = sb("iota_p", [P, 1], F32)
        zero_i = sb("zero_i", [P, HALF], I32)
        zero16 = sb("zero16", [1, ROW], BF16)
        zrow = sb("zrow", [P, 1], F32)
        epsv = sb("epsv", [P, 1], F32)

        G_first = sb("G_first", [P, C, ROW], F32)
        ir2 = sb("ir2", [P, QUADS, HALF], I32)
        s_gs = [sem(f"rows_gathered{j}") for j in range(2)]
        s_ir2 = sem("index_ring")

        st1 = ExitStack()
        with st1:
            xt = xb
            xn = sb("xn", [P, 6, D], F32, st1)
            xnT = sb("xnT", [P, KD, NP + P], F32, st1)
            wsb = sb("wsb", [P, KD, R, D], F32, st1)
            wa = sb("wa", [P, KD, 2, RH], F32, st1)
            lts = sb("lts", [P, NW, 2, RH], F32, st1)
            er3 = sb("er3", [P, NW, 3, RH], BF16, st1)
            with ExitStack() as c1:
                keys = sb("keys", [P, SB, P], F32, c1)
                brk = sb("brk", [P, SB, P + 1], F32, c1)
                summ = sb("summ", [P, SB, 4], F32, c1)
                rows = sb("rows", [1, 4, SB * P], F32, c1)
                dlb16 = sb("dlb16", [P, SB, P], BF16, c1)
                crow = sb("crow", [1, 4, NC], F32, c1)
                winrow = sb("winrow", [1, SB * P], F32, c1)
                newp = sb("newp", [1, PAIRS], F32, c1)
                nprod = sb("nprod", [1, PAIRS], F32, c1)
                pow2 = sb("pow2", [1, CP2], F32, c1)
                dst_i = sb("dst_i", [CP, E // CP], I32, c1)
                dst_w = sb("dst_w", [CP, E // CP], BF16, c1)
                cmp = sb("cmp", [CP, 4, E // CP], BF16, c1)
                cnt = sb("cnt", [CP, NW - 1], F32, c1)
                ones = sb("ones", [P, P], F32, c1)
                sti = sb("sti", [P, 4, NW + 1], I32, c1)
                stf = sb("stf", [P, 6, NW + 1], F32, c1)
                slot_id = sb("slot_id", [P, SB, 1], F32, c1)
                ge = sb("ge", [P, SB, NW - 1], F32, c1)
                ged = sb("ged", [P, SB, NW - 1], F32, c1)
                win = sb("win", [P, SB], F32, c1)
                tile_f = sb("tile_f", [P, SB], F32, c1)
                tile_i = sb("tile_i", [P, SB], I32, c1)
                wtmp = er_all[:, :, :].rearrange("p s h -> p (s h)")[:, 0:R * D]
                space = G_first[:, :, :].rearrange("p s x -> p (s x)")
                att = space[:, 0:R * D]
                padr = sb("padr", [2, 3 * P], I32, c1)
                eg = sb("eg", [P, SB, 3 * P], I32, c1)
                ert = eg[:, :, :].rearrange("p k e -> p (k e)").bitcast(F32)\
                    .rearrange("p (n t c) -> p n t c", n=2, t=NW)
                ef, ix = [space[:, R * D + n * SB * 3 * P:R * D + (n + 1) * SB * 3 * P]
                          .rearrange("p (k n e) -> p k n e", k=SB, n=3) for n in range(2)]
                stat = sb("stat", [P, NW, 6], F32, c1)
                mv = sb("mv", [P, NW, 2], F32, c1)
                rstd = sb("rstd", [P, NW], F32, c1)
                std = sb("std", [P, NW], F32, c1)
                shift = sb("shift", [P, NW], F32, c1)
                hb = sb("hb", [P, D], F32, c1)
                psc = pb("psc", c1)
                pst = [pb(f"pst{i}", c1) for i in range(4)]
                psl = [pb(f"psl{i}", c1) for i in range(2)]
                psx = pb("psx", c1)

                s_const = sem("constants_ready")
                s_ident = sem("identity_ready")
                s_dst = sem("dst_loaded")
                s_x = sem("x_loaded")
                s_w = sem("weights_loaded")
                s_att = sem("attention_loaded")
                s_pad = sem("pad_rows_ready")
                s_et = sem("edge_tiles_stored")
                s_dv = sem("vector_steps_1")
                s_cnt = sem("counts_ready")
                s_cntp = sem("counts_summed")
                s_tile = sem("slot_tiles_ready")
                s_eg = sem("slot_edges_gathered")
                s_ix = sem("slot_indices_ready")
                s_tp = sem("transposes_done_1")
                s_te = sem("transposes_copied_1")
                s_var = sem("variance_ready")
                s_std = sem("std_ready")
                s_xn = sem("xn_ready")
                s_wa = sem("attention_folded")
                s_lt = sem("logits_done")
                s_le = sem("logits_copied")
                s_ls = sem("logit_tables_stored")
                s_rstd = sem("inverse_std_ready")
                s_wl = sem("source_vectors_folded")
                s_hb = sem("bias_loaded")
                s_wr = sem("slot_windows_turned")
                s_br = sem("segment_breaks_ready")
                s_sm = sem("row_summaries_ready")
                s_cr = sem("crossing_rows_ready")

                with nc.Block() as block:
                    @block.sync
                    def _(eng):
                        eng.dma_start(dst_i[:, :], dst.rearrange("(p f) -> p f", p=CP)).then_inc(s_dst, 16)
                        eng.wait_ge(s_const, 1)
                        eng.dma_start(xt[:, 0:FULL, :],
                                      x[0:FULL * P, :].rearrange("(t p) f -> p t f", p=P)).then_inc(s_x, 16)
                        eng.dma_start(xt[0:REST, FULL, :], x[FULL * P:N, :]).then_inc(s_x, 16)
                        eng.dma_start(hb[:, :], h_bias.partition_broadcast(P)).then_inc(s_hb, 16)
                        for n, a in enumerate((attn_l, attn_r)):
                            if n:
                                eng.wait_ge(s_wl, 1)
                            eng.dma_start(att, a.rearrange("r h d -> (r h d)").partition_broadcast(P))\
                               .then_inc(s_att, 16)
                        eng.wait_ge(s_br, 1)
                        eng.dma_start(dloc_rows.rearrange("(k s) e -> s k e", s=P), dlb16[:, :, :]).then_inc(s_ls, 16)
                        eng.dma_start(brk_rows.rearrange("(k s) e -> s k e", s=P), brk[:, :, :]).then_inc(s_ls, 16)
                        eng.wait_ge(s_ls, 32)
                        for h in range(H):
                            eng.dma_start(brkt[h * C:(h + 1) * C, :, :],
                                          brk_rows[0:SLOTS, :].rearrange("(c s) e -> s c e", s=C)).then_inc(s_ls, 16)
                        eng.wait_ge(s_ls, 16 * (2 + H))

                    @block.gpsimd
                    def _(eng):
                        eng.memset(xt[:, FULL, :], 0.0).then_inc(s_const, 1)
                        eng.memset(xbp[:, 0, :], 0.0).then_inc(s_const, 1)
                        eng.memset(ident[:, :], 0.0).then_inc(s_const, 1)
                        eng.memset(zero16[:, :], 0.0).then_inc(s_const, 1)
                        eng.memset(zero_i[:, :], 0).then_inc(s_const, 1)
                        eng.memset(zrow[:, :], 0.0).then_inc(s_const, 1)
                        eng.memset(epsv[:, :], EPS).then_inc(s_const, 1)
                        eng.memset(ones[:, :], 1.0).then_inc(s_const, 1)
                        eng.iota(iota_f[:, :], pattern=[[1, P]], base=0, channel_multiplier=0,
                                 allow_small_or_imprecise_dtypes=True).then_inc(s_const, 1)
                        eng.iota(iota_p[:, :], pattern=[[0, 1]], base=0, channel_multiplier=1,
                                 allow_small_or_imprecise_dtypes=True).then_inc(s_const, 1)
                        eng.memset(xnT[:, :, NP:NP + P], 0.0).then_inc(s_const, 1)
                        eng.iota(slot_id[:, :, :], pattern=[[P, SB], [1, 1]], base=0, channel_multiplier=1,
                                 allow_small_or_imprecise_dtypes=True).then_inc(s_const, 1)
                        for n in range(CP2):
                            eng.memset(pow2[:, n:n + 1], float(2 ** n)).then_inc(s_const, 1)
                        eng.memset(padr[:, 0:2 * P], 0).then_inc(s_pad, 1)
                        eng.memset(padr[:, 2 * P:3 * P], -1).then_inc(s_pad, 1)
                        eng.wait_ge(s_const, NCONST)
                        eng.affine_select(out=ident[:, :], in_=ident[:, :], compare_op=ALU.not_equal, fill=1.0,
                                          base=0, pattern=[[-1, P]], channel_multiplier=1).then_inc(s_ident, 1)
                        eng.wait_ge(s_tile, 1)
                        eng.wait_ge(s_et, 8 * 16)
                        for k in range(SB):
                            eng.indirect_dma_start(eg[:, k, :], None, edges[:, :],
                                                   bass.IndirectOffsetOnAxis(ap=tile_i[:, k:k + 1], axis=0))\
                               .then_inc(s_eg, 16)
                        eng.wait_ge(s_xn, NW)
                        eng.wait_ge(s_hb, 16)
                        eng.tensor_tensor(xb[:, :, :], xt[:, :, :],
                                          hb[:, :].unsqueeze(1).to_broadcast([P, NW, D]), ALU.add).then_inc(s_xn, 1)
                        eng.wait_ge(s_xn, NW + 1)
                        eng.wait_ge(s_eg, 16 * SB)

                    @block.scalar
                    def _(eng):
                        for n, a in enumerate((src, etype, dst)):
                            eng.dma_start(edges[0:TF, n * P:(n + 1) * P],
                                          a[0:TF * P].rearrange("(t e) -> t e", e=P)).then_inc(s_et, 16)
                            eng.dma_start(edges[TF:TF + 1, n * P:n * P + TREST],
                                          col(a[TF * P:E])).then_inc(s_et, 16)
                        eng.wait_ge(s_pad, 2)
                        eng.dma_start(edges[TF:TF + 1, :].rearrange("a (n e) -> a n e", e=P)[:, :, TREST:P],
                                      padr[0:1, :].rearrange("a (n e) -> a n e", e=P)[:, :, TREST:P])\
                           .then_inc(s_et, 16)
                        eng.dma_start(edges[T:T + 1, :], padr[1:2, :]).then_inc(s_et, 16)
                        for kh in range(KD):
                            for r in range(R):
                                eng.dma_start(wsb[:, kh, r, :].rearrange("p (h d) -> p h d", h=H),
                                              conv_w[r, :, kh * P:(kh + 1) * P, :].rearrange("h k d -> k h d"))\
                                   .then_inc(s_w, 16)
                        eng.wait_ge(s_var, 1)
                        eng.activation(std[:, :], mv[:, :, 1], ACT.Sqrt, bias=epsv[:, 0:1]).then_inc(s_std, 1)
                        eng.wait_ge(s_rstd, 1)
                        for t in range(NW + 2):
                            if t < NW:
                                if t >= 6:
                                    eng.wait_ge(s_tp, t - 5)
                                eng.activation(xn[:, t % 6, :], xt[:, t, :], ACT.Identity, scale=rstd[:, t:t + 1],
                                               bias=shift[:, t:t + 1]).then_inc(s_xn, 1)
                            if t < 2:
                                continue
                            t = t - 2
                            eng.wait_ge(s_tp, t + 1)
                            eng.copy(xnT[:, :, t * P:(t + 1) * P],
                                     pst[t % 4][:, 0:2 * P].rearrange("p (k n) -> p k n", k=KD)).then_inc(s_te, 1)
                        def logits(t):
                            eng.wait_ge(s_lt, t + 1)
                            eng.copy(lts[:, t, :, :].rearrange("p n c -> p (n c)"),
                                     psl[t % 2][:, 0:2 * RH]).then_inc(s_le, 1)

                        for t in range(NW // 2):
                            logits(t)
                        for k in range(SB):
                            eng.wait_ge(s_tp, NW + k + 1)
                            b = pst[(NW + k) % 4]
                            eng.copy(el_idx[:, k * P:(k + 1) * P], b[:, 0:P])
                            eng.copy(etyp[:, k * P:(k + 1) * P], b[:, P:2 * P])
                            eng.copy(dloc[:, k * P:(k + 1) * P], b[:, 2 * P:3 * P]).then_inc(s_te, 1)
                        for k in range(SB):
                            eng.wait_ge(s_tp, NW + SB + k + 1)
                            eng.copy(rows[:, :, k * P:(k + 1) * P],
                                     pst[(NW + SB + k) % 4][0:1, :].rearrange("p (n s) -> p n s", n=4)).then_inc(s_te, 1)
                        for t in range(NW // 2, NW):
                            logits(t)
                        eng.wait_ge(s_et, 8 * 16)
                        eng.wait_ge(s_w, 16 * KD * R)
                        eng.wait_ge(s_te, NW + 2 * SB)

                    @block.tensor
                    def _(eng):
                        eng.wait_ge(s_const, NCONST)
                        eng.wait_ge(s_cnt, 1)
                        eng.matmul(psc[:, 0:NW - 1], ones[0:CP, :], cnt[:, :], start=True, stop=True)\
                           .then_inc(s_cntp, 1)
                        eng.wait_ge(s_ident, 1)
                        eng.wait_ge(s_tile, 1)
                        for k in range(SB):
                            tr = eng.transpose((psx if k < 4 else psc)[0:1, (k % 4) * P:(k % 4 + 1) * P], win[:, k:k + 1],
                                               ident[:, :])
                        tr.then_inc(s_wr, 1)
                        for t in range(NW):
                            eng.wait_ge(s_xn, t + 1)
                            if t >= 4:
                                eng.wait_ge(s_te, t - 3)
                            for k in range(KD):
                                tr = eng.transpose(pst[t % 4][:, k * P:(k + 1) * P],
                                                   xn[:, t % 6, k * P:(k + 1) * P], ident[:, :])
                            tr.then_inc(s_tp, 1)
                        def logits(t):
                            eng.wait_ge(s_te, t + 1)
                            if t >= 2:
                                eng.wait_ge(s_le, t - 1)
                            for k in range(KD):
                                mm = eng.matmul(psl[t % 2][:, 0:2 * RH], xnT[:, k, t * P:(t + 1) * P],
                                                wa[:, k, :, :].rearrange("p a c -> p (a c)"),
                                                start=(k == 0), stop=(k == KD - 1))
                            mm.then_inc(s_lt, 1)

                        eng.wait_ge(s_wa, 1)
                        for t in range(NW // 2):
                            logits(t)
                        eng.wait_ge(s_ix, 1)
                        for k in range(SB):
                            eng.wait_ge(s_te, NW + k - 3)
                            for n in range(3):
                                tr = eng.transpose(pst[(NW + k) % 4][:, n * P:(n + 1) * P], ix[:, k, n, :],
                                                   ident[:, :])
                            tr.then_inc(s_tp, 1)
                        eng.wait_ge(s_sm, 1)
                        for k in range(SB):
                            eng.wait_ge(s_te, NW + SB + k - 3)
                            for n in range(4):
                                tr = eng.transpose(pst[(NW + SB + k) % 4][0:1, n * P:(n + 1) * P], summ[:, k, n:n + 1],
                                                   ident[:, :])
                            tr.then_inc(s_tp, 1)
                        for t in range(NW // 2, NW):
                            logits(t)
                        eng.wait_ge(s_cr, 1)
                        eng.matmul(psx[:, 0:NC], ones[0:1, :], crow[:, 0, :], start=True, stop=True)\
                           .then_inc(s_cntp, 1)

                    @block.vector
                    def _(eng):
                        do = Chain(eng, s_dv)
                        eng.wait_ge(s_dst, 16)
                        do(eng.tensor_scalar(dst_i[:, :], dst_i[:, :], 7, None, ALU.arith_shift_right))
                        do(eng.tensor_copy(dst_w[:, :], dst_i[:, :]))
                        for w in range(1, NW):
                            do.put(eng.tensor_scalar(cmp[:, w % 4, :], dst_w[:, :], float(w), 0.0, ALU.is_lt, ALU.add,
                                                     accum_out=cnt[:, w - 1:w]))
                            if w % 4 == 3:
                                do.sync()
                        do.sync()
                        eng.engine_nop().then_inc(s_cnt, 1)
                        eng.wait_ge(s_x, 32)
                        for t in range(NW):
                            do.put(eng.bn_stats(stat[:, t, :], xt[:, t, :]))
                        do.sync()
                        for t in range(NW):
                            do.put(eng.bn_aggr(mv[:, t, :], stat[:, t, :]))
                        do.sync()
                        eng.engine_nop().then_inc(s_var, 1)
                        eng.wait_ge(s_cntp, 1)
                        do.put(eng.memset(stf[:, 0, 0:1], 0.0))
                        do.put(eng.memset(stf[:, 0, NW:NW + 1], float(E)))
                        do(eng.tensor_copy(stf[:, 0, 1:NW], psc[:, 0:NW - 1]))
                        do(eng.tensor_scalar(stf[:, 1, :], stf[:, 0, :], 1.0, None, ALU.subtract))
                        do.put(eng.tensor_copy(sti[:, 0, :], stf[:, 0, :]))
                        do(eng.tensor_copy(sti[:, 1, :], stf[:, 1, :]))
                        do(eng.tensor_scalar(sti[:, 2:4, :], sti[:, 0:2, :], 7, None, ALU.arith_shift_right))
                        do(eng.tensor_copy(stf[:, 2:4, :], sti[:, 2:4, :]))
                        do(eng.tensor_tensor(stf[:, 4, 0:NW], stf[:, 3, 1:NW + 1], stf[:, 2, 0:NW], ALU.subtract))
                        do(eng.tensor_scalar(stf[:, 4, 0:NW], stf[:, 4, 0:NW], 0.0, 2.0, ALU.max, ALU.add))
                        do(eng.tensor_copy(sti[:, 0, 0:NW], stf[:, 4, 0:NW]))
                        do(eng.tensor_scalar(sti[:, 0, 0:NW], sti[:, 0, 0:NW], 1, None, ALU.arith_shift_right))
                        do(eng.tensor_copy(stf[:, 4, 0:NW], sti[:, 0, 0:NW]))
                        do(eng.memset(stf[:, 5, :], 0.0))
                        do(eng.tensor_tensor_scan(stf[:, 1, 0:NW], stf[:, 4, 0:NW], stf[:, 5, 0:NW], 0.0,
                                                  ALU.add, ALU.add))
                        do(eng.tensor_copy(stf[:, 5, 1:NW], stf[:, 1, 0:NW - 1]))
                        do(eng.memset(stf[:, 5, NW:NW + 1], float(PAIRS)))
                        do(eng.tensor_scalar(stf[:, 5, :], stf[:, 5, :], 2.0, None, ALU.mult))
                        do(eng.tensor_tensor(stf[:, 4, :], stf[:, 2, :], stf[:, 5, :], ALU.subtract))
                        do(eng.tensor_tensor(stf[:, 3, 1:NW], stf[:, 4, 1:NW], stf[:, 4, 0:NW - 1], ALU.subtract))
                        do(eng.tensor_tensor(ge[:, :, :], slot_id[:, :, :].to_broadcast([P, SB, NW - 1]),
                                             stf[:, 5:6, 1:NW].to_broadcast([P, SB, NW - 1]), ALU.is_ge))
                        do.put(eng.tensor_reduce(win[:, :], ge[:, :, :], AX, ALU.add))
                        do(eng.tensor_tensor(ged[:, :, :], ge[:, :, :],
                                             stf[:, 3:4, 1:NW].to_broadcast([P, SB, NW - 1]), ALU.mult))
                        do(eng.tensor_reduce(tile_f[:, :], ged[:, :, :], AX, ALU.add))
                        do(eng.tensor_tensor(tile_f[:, :], tile_f[:, :], slot_id[:, :, 0], ALU.add))
                        do.put(eng.tensor_scalar(tile_f[:, :], tile_f[:, :], float(PAD_TILE), 0.0, ALU.min, ALU.max))
                        do(eng.tensor_scalar(win[:, :], win[:, :], float(P), None, ALU.mult))
                        do(eng.tensor_copy(tile_i[:, :], tile_f[:, :]))
                        eng.engine_nop().then_inc(s_tile, 1)
                        eng.wait_ge(s_std, 1)
                        do(eng.reciprocal(rstd[:, :], std[:, :]))
                        do(eng.scalar_tensor_tensor(shift[:, :], mv[:, :, 0], -1.0, rstd[:, :], ALU.mult, ALU.mult))
                        eng.engine_nop().then_inc(s_rstd, 1)
                        def fold(n):
                            eng.wait_ge(s_att, 16 * (n + 1))
                            for k in range(KD):
                                do(eng.tensor_tensor(wtmp, wsb[:, k, :, :].rearrange("p r d -> p (r d)"),
                                                     att, ALU.mult))
                                do(eng.tensor_reduce(wa[:, k, n, :], wtmp.rearrange("p (c d) -> p c d", d=HD),
                                                     AX, ALU.add))

                        eng.wait_ge(s_w, 16 * KD * R)
                        fold(0)
                        eng.engine_nop().then_inc(s_wl, 1)
                        eng.wait_ge(s_wr, 1)
                        do.put(eng.tensor_copy(winrow[:, 0:4 * P], psx[0:1, :]))
                        do(eng.tensor_copy(winrow[:, 4 * P:5 * P], psc[0:1, 0:P]))
                        do(eng.tensor_scalar(winrow[:, :], winrow[:, :], 1.0 / P, None, ALU.mult))
                        do.put(eng.memset(newp[:, 0:1], 0.0))
                        do(eng.tensor_tensor(newp[:, 1:PAIRS], winrow[:, 2:2 * PAIRS:2], winrow[:, 0:2 * PAIRS - 2:2],
                                             ALU.subtract))
                        do(eng.tensor_tensor(nprod[:, :].rearrange("p (g n) -> p g n", n=EG // 2),
                                             newp[:, :].rearrange("p (g n) -> p g n", n=EG // 2),
                                             pow2[:, 0:EG // 2].unsqueeze(1).to_broadcast([1, NEG, EG // 2]), ALU.mult))
                        do(eng.tensor_reduce(nprod[:, 0:NEG],
                                             nprod[:, :].rearrange("p (g n) -> p g n", n=EG // 2), AX, ALU.add))
                        do(eng.tensor_copy(new_in_group[:, :], nprod[:, 0:NEG]))
                        do(eng.memset(crow[:, 1, :], 0.0))
                        do(eng.tensor_tensor_scan(crow[:, 2, :], newp[:, 0:PAIRS:CP2], crow[:, 1, :], 0.0,
                                                  ALU.add, ALU.add))
                        do(eng.tensor_tensor(crow[:, 2, :], iota_f[0:1, 0:NC], crow[:, 2, :], ALU.subtract))
                        do(eng.scalar_tensor_tensor(crow[:, 3, :], crow[:, 2, :], 32.0, winrow[:, C - 2:SLOTS:C],
                                                    ALU.mult, ALU.add))
                        do(eng.scalar_tensor_tensor(crow[:, 3, :], crow[:, 3, :], 32.0, winrow[:, 0:SLOTS:C],
                                                    ALU.mult, ALU.add))
                        do(eng.tensor_copy(chunk_info[:, :], crow[:, 3, :]))
                        do(eng.tensor_tensor(nprod[:, :].rearrange("p (g n) -> p g n", n=CP2),
                                             newp[:, :].rearrange("p (g n) -> p g n", n=CP2),
                                             pow2[:, :].unsqueeze(1).to_broadcast([1, NC, CP2]), ALU.mult))
                        do(eng.tensor_reduce(nprod[:, 0:NC],
                                             nprod[:, :].rearrange("p (g n) -> p g n", n=CP2), AX, ALU.add))
                        do(eng.scalar_tensor_tensor(nprod[:, 0:NC], nprod[:, 0:NC], 32.0, winrow[:, 0:SLOTS:C],
                                                    ALU.mult, ALU.add))
                        do(eng.tensor_copy(chunk_cells[:, :], nprod[:, 0:NC]))
                        fold(1)
                        eng.engine_nop().then_inc(s_wa, 1)
                        eng.wait_ge(s_eg, 16 * SB)
                        do(eng.tensor_copy(ef[:, :, :, :], eg[:, :, :].rearrange("p k (n e) -> p k n e", n=3)))
                        do.put(eng.scalar_tensor_tensor(ix[:, :, 0, :], ef[:, :, 0, :], float(R), ef[:, :, 1, :],
                                                        ALU.mult, ALU.add))
                        do.put(eng.tensor_copy(ix[:, :, 1, :], ef[:, :, 1, :]))
                        do(eng.tensor_tensor(ix[:, :, 2, :], ef[:, :, 2, :],
                                             win[:, :].unsqueeze(2).to_broadcast([P, SB, P]), ALU.subtract))
                        eng.engine_nop().then_inc(s_ix, 1)
                        do.put(eng.tensor_copy(dlb16[:, :, :], ix[:, :, 2, :]))
                        do.put(eng.tensor_scalar(ef[:, :, 0, :], ix[:, :, 2, :], 0.0, None, ALU.is_ge))
                        do(eng.tensor_scalar(ef[:, :, 1, :], ix[:, :, 2, :], float(P), None, ALU.is_lt))
                        do(eng.tensor_tensor(ef[:, :, 0, :], ef[:, :, 0, :], ef[:, :, 1, :], ALU.mult))
                        do(eng.scalar_tensor_tensor(keys[:, :, :], ef[:, :, 2, :], 1.0, ef[:, :, 0, :],
                                                    ALU.add, ALU.mult))
                        do.put(eng.memset(brk[:, :, 0:1], 0.0))
                        do.put(eng.memset(brk[:, :, P:P + 1], 0.0))
                        do(eng.tensor_tensor(brk[:, :, 1:P], keys[:, :, 1:P], keys[:, :, 0:P - 1], ALU.not_equal))
                        do(eng.tensor_scalar(brk[:, :, 1:P], brk[:, :, 1:P], -BIG, None, ALU.mult))
                        eng.engine_nop().then_inc(s_br, 1)
                        do.put(eng.tensor_reduce(summ[:, :, 1], keys[:, :, :], AX, ALU.min))
                        do(eng.tensor_reduce(summ[:, :, 2], keys[:, :, :], AX, ALU.max))
                        do(eng.tensor_tensor(summ[:, :, 0], summ[:, :, 1], summ[:, :, 2], ALU.is_equal))
                        do.put(eng.tensor_copy(summ[:, :, 1], keys[:, :, 0]))
                        do.put(eng.tensor_copy(summ[:, :, 2], keys[:, :, P - 1]))
                        do(eng.tensor_copy(summ[:, :, 3], ix[:, :, 2, 0]))
                        eng.engine_nop().then_inc(s_sm, 1)
                        eng.wait_ge(s_te, NW + 2 * SB)
                        S = SLOTS
                        do.put(eng.memset(flag[:, :, 0:1], 0.0))
                        do(eng.memset(flag[:, :, S - 1:S], 0.0))
                        do(eng.tensor_tensor(flag[:, 0, 1:S], rows[:, 1, 1:S], rows[:, 2, 0:S - 1], ALU.is_equal))
                        do.put(eng.tensor_tensor(flag[:, 1, :], flag[:, 0, :], rows[:, 0, 0:S], ALU.mult))
                        do.put(eng.tensor_tensor(flag[:, 2, 0:S - 1], flag[:, 0, 1:S], rows[:, 0, 0:S - 1], ALU.mult))
                        do(eng.tensor_copy(flag[:, 3, 0:S - 1], flag[:, 0, 1:S]))
                        do(eng.tensor_scalar(rows[:, 1, :], rows[:, 1, :], 0.0, None, ALU.is_gt))
                        do(eng.tensor_tensor(rows[:, 1, 0:S], rows[:, 1, 0:S], flag[:, 0, :], ALU.mult))
                        do(eng.scalar_tensor_tensor(rows[:, 3, :], rows[:, 3, :], 1.0, rows[:, 1, :],
                                                    ALU.add, ALU.mult))
                        do(eng.tensor_scalar(crow[:, 0, :], rows[:, 3, 0:SLOTS:C], 1.0, None, ALU.subtract))
                        eng.engine_nop().then_inc(s_cr, 1)
                        do(eng.tensor_scalar(flag[:, :, :], flag[:, :, :], 1.0, BIG, ALU.subtract, ALU.mult))
                        eng.wait_ge(s_cntp, 2)
                        do(eng.tensor_scalar(cross[:, :], psx[:, 0:NC], iota_p[:, 0:1], None, ALU.is_equal))
                        eng.wait_ge(s_le, NW)
                        do(eng.tensor_copy(er3[:, :, 0, :], lts[:, :, 1, :]))
                        do(eng.tensor_copy(ert[:, 0, :, :], er3[:, :, 0, :]))
                        do(eng.tensor_tensor(ert[:, 1, :, :], lts[:, :, 1, :], ert[:, 0, :, :], ALU.subtract))
                        do(eng.tensor_copy(er3[:, :, 1, :], ert[:, 1, :, :]))
                        do(eng.tensor_copy(ert[:, 0, :, :], er3[:, :, 1, :]))
                        do(eng.tensor_tensor(er3[:, :, 2, :], ert[:, 1, :, :], ert[:, 0, :, :], ALU.subtract))
            fsb = sb("fsb", [P, 2, R, ROW], F32, st1)
            stg = sb("stg", [P, 2, KD, P], F32, st1)
            dlb = sb("dlb", [P, 3, EG * P], BF16, st1)
            sel = sb("sel", [P, 3 * EG * P], BF16, st1)
            EH = EG // 2
            tmask = sb("tmask", [P, EH, 3, R], F32, st1)
            tprod = sb("tprod", [P, EH, 3 * R, H], F32, st1)
            with ExitStack() as c2:
                psf = [pb(f"psf{i}", c2) for i in range(4)]
                pse = pb("pse2", c2, (P, EG * P))
                s_stg = sem("node_tile_staged")
                s_f = sem("features_done")
                s_fa = sem("features_copied")
                s_fl = sem("source_logits_copied")
                s_fs = [sem(f"features_stored{i}") for i in range(2)]
                s_dl = [sem(f"targets_spread{i}") for i in range(3)]
                s_st = sem("selectors_ready")
                s_eu = sem("slots_looked_up")
                s_ev = sem("lookups_copied")
                s_tm = sem("lookup_steps")

                with nc.Block() as block:
                    @block.tensor
                    def _(eng):
                        wreg = eng.alloc_register("lookup_window")
                        eng.reg_mov(wreg, 0)

                        def tile(w, b):
                            eng.wait_ge(s_stg, w + 1)
                            for c in range(4):
                                eng.wait_ge(s_fa, w * 4 + c + 1)
                                for k in range(KD):
                                    mm = eng.matmul(psf[c][:, :], stg[:, b, k, :],
                                                    wsb[:, k, 2 * c:2 * c + 2, :].rearrange("p r d -> p (r d)"),
                                                    start=(k == 0), stop=(k == KD - 1))
                                mm.then_inc(s_f, 1)

                        def lookups(n, u):
                            fresh = eng.value_load(new_in_group[0:1, bass.ds(n, 1)], min_val=0, max_val=255)
                            eng.wait_ge(s_st, n + 3)
                            for q in range(EG // 2):
                                if q % (EH // 2) == 0:
                                    eng.wait_ge(s_ev, n * 2 + q // (EH // 2) + 1)
                                eng.reg_add(wreg, wreg, (fresh >> q) & 1)
                                w = eng.snap(wreg, min_val=0, max_val=NW - 1)
                                for s in range(2 * q, 2 * q + 2):
                                    mm = eng.matmul(pse[:, s * P:s * P + 3 * RH],
                                                    sel[:, (u * EG + s) * P:(u * EG + s + 1) * P],
                                                    er3[:, bass.ds(w, 1), :, :].rearrange("p a m c -> p (a m c)"),
                                                    start=True, stop=True)
                                if q % (EH // 2) == EH // 2 - 1:
                                    mm.then_inc(s_eu, 1)

                        with eng.Fori(0, NEG // 6) as i:
                            for u in range(6):
                                tile(i * 6 + u, u % 2)
                                lookups(i * 6 + u, u % 3)
                        for n in range(NEG // 6 * 6, NEG):
                            lookups(n, n % 3)

                    @block.gpsimd
                    def _(eng):
                        for q in range(3):
                            eng.tensor_copy(ir2[:, q, :], el_idx[:, q * HALF:(q + 1) * HALF]).then_inc(s_ir2, 1)
                        eng.wait_ge(s_ir2, 3)
                        for b in range(2):
                            eng.wait_ge(s_fs[b], 16 * (NW // 2))
                        for j in range(C):
                            eng.indirect_dma_start(G_first[:, j, :], None, feat_rows,
                                                   bass.IndirectOffsetOnAxis(ap=ir2[:, j // HALF, j % HALF:j % HALF + 1],
                                                                             axis=0)).then_inc(s_gs[0], 16)

                    @block.scalar
                    def _(eng):
                        eng.copy(stg[:, 0, :, :], xnT[:, :, 0:P]).then_inc(s_stg, 1)
                        with eng.Fori(0, NW // 2) as v:
                            for b in range(2):
                                w = v * 2 + b
                                eng.copy(stg[:, 1 - b, :, :], xnT[:, :, bass.ds(w * P + P, P)]).then_inc(s_stg, 1)
                                eng.copy(fsb[:, b, :, D:ROW], lts[:, bass.ds(w, 1), 0, :]
                                         .rearrange("p a (r h) -> p (a r) h", r=R)).then_inc(s_fl, 1)
                                for c in range(4):
                                    eng.wait_ge(s_f, w * 4 + c + 1)
                                    eng.copy(fsb[:, b, 2 * c:2 * c + 2, 0:D],
                                             psf[c][:, :].rearrange("p (r d) -> p r d", r=2)).then_inc(s_fa, 1)
                                eng.wait_ge(s_fl, w + 1)
                                eng.wait_ge(s_fa, w * 4 + 8)
                                eng.dma_start(feat[bass.ds(w * P, P), :],
                                              fsb[:, b, :, :].rearrange("p r d -> p (r d)")).then_inc(s_fs[b], 16)
                            for b in range(2):
                                eng.wait_ge(s_fs[b], v * 16 + 16)

                    @block.sync
                    def _(eng):
                        def load(rows_ap, u):
                            eng.dma_start(dlb[:, u, :], rows_ap.rearrange("s e -> (s e)").partition_broadcast(P))\
                               .then_inc(s_dl[u], 16)

                        load(dloc_rows[0:EG, :], 0)
                        with eng.Fori(0, NEG // 3) as i:
                            for u in range(3):
                                n = i * 3 + u
                                eng.wait_ge(s_st, n + 1)
                                load(dloc_rows[bass.ds(n * EG + EG, EG), :], (u + 1) % 3)
                        for u in range(3):
                            eng.wait_ge(s_dl[u], 16 * (NEG // 3) + (16 if u == 0 else 0))

                    @block.vector
                    def _(eng):
                        eng.engine_nop().then_inc(s_fa, 4)
                        eng.engine_nop().then_inc(s_st, 2)
                        eng.engine_nop().then_inc(s_ev, 2)
                        eng.engine_nop().then_inc(s_eu, 6)

                        def selectors(u):
                            eng.tensor_scalar(sel[:, u * EG * P:(u + 1) * EG * P], dlb[:, u, :], iota_p[:, 0:1], None,
                                              ALU.is_equal).then_inc(s_st, 1)

                        eng.wait_ge(s_dl[0], 16)
                        selectors(0)
                        with eng.Fori(0, NEG // 3) as i:
                            for u in range(3):
                                n = i * 3 + u
                                eng.wait_ge(s_dl[(u + 1) % 3], i * 16 + (32 if u == 2 else 16))
                                eng.wait_ge(s_eu, n * 2 + 4)
                                selectors((u + 1) % 3)
                                for half in range(2):
                                    g = n * 2 + half
                                    eng.tensor_tensor(tmask[:, :, :, :],
                                                      iota_f[:, 0:R].unsqueeze(1).unsqueeze(1)
                                                      .to_broadcast([P, EH, 3, R]),
                                                      etyp[:, bass.ds(g * EH, EH)].unsqueeze(2).unsqueeze(3)
                                                      .to_broadcast([P, EH, 3, R]), ALU.is_equal).then_inc(s_tm, 1)
                                    eng.wait_ge(s_tm, g * 2 + 1)
                                    eng.wait_ge(s_eu, g + 7)
                                    eng.tensor_tensor(tprod[:, :, :, :],
                                                      pse[:, half * EH * P:(half + 1) * EH * P]
                                                      .rearrange("p (s x) -> p s x", s=EH)[:, :, 0:3 * RH]
                                                      .rearrange("p s (m h) -> p s m h", h=H),
                                                      tmask[:, :, :, :].rearrange("p s m r -> p s (m r)")
                                                      .unsqueeze(3).to_broadcast([P, EH, 3 * R, H]),
                                                      ALU.mult).then_inc(s_tm, 1)
                                    eng.wait_ge(s_tm, g * 2 + 2)
                                    eng.tensor_reduce(er_all[:, bass.ds(g * EH, EH), :],
                                                      tprod[:, :, :, :].rearrange("p s m h -> p s h m"),
                                                      AX, ALU.add).then_inc(s_ev, 1)
                        eng.wait_ge(s_ev, 2 * NEG + 2)

        STAGE = NW + 1
        hacc = sb("hacc", [P, NW + 2, ROW], F32)
        comb = sb("comb", [P, NW + 1, X], F32)
        w1s = sb("w1s", [P, KD, X, D], F32)
        w2s = sb("w2s", [P, KD, X, D], F32)
        b1s = sb("b1s", [P, X, KD], F32)
        b2s = sb("b2s", [X, D], F32)
        rws = sb("rws", [P, KD, X], F32)
        with ExitStack() as c4:
            G = [G_first, sb("G_second", [P, C, ROW], F32, c4)]
            OH = sb("OH", [P, C, P], F32, c4)
            onesr = sb("onesr", [1, P], F32, c4)
            eraw = sb("eraw", [P, C, H], F32, c4)
            elog = sb("elog", [P, H, C], F32, c4)
            bkc = sb("bkc", [HC, P + 1], F32, c4)
            flc = sb("flc", [1, 4, C], F32, c4)
            fw = sb("fw", [HC, P], F32, c4)
            bw = sb("bw", [HC, P], F32, c4)
            ends = sb("ends", [1, H, C + 1], F32, c4)
            begs = sb("begs", [1, H, C + 1], F32, c4)
            incr = sb("incr", [1, 2, H, C], F32, c4)
            inc = sb("inc", [HC, 2], F32, c4)
            down_m = sb("down_m", [1, H], F32, c4)
            downe = sb("downe", [1, H], F32, c4)
            resc = sb("resc", [P, 2, H], F32, c4)
            wrow = sb("wrow", [HC, P], F32, c4)
            den = sb("den", [P, H], F32, c4)
            xr = sb("xr", [P, D], F32, c4)
            xn2 = sb("xn2", [P, D], F32, c4)
            stat2 = sb("stat2", [P, 6], F32, c4)
            mv2 = sb("mv2", [P, 2], F32, c4)
            ve = sb("ve", [P, 1], F32, c4)
            guess = sb("guess", [P, 1], I32, c4)
            rs = sb("rs", [P, 1], F32, c4)
            rq = sb("rq", [P, 1], F32, c4)
            xts = sb("xts", [P, KD, P], F32, c4)
            prob = sb("prob", [P, X], F32, c4)
            pm = sb("pm", [P, 1], F32, c4)
            top = sb("top", [P, 8], F32, c4)
            topi = sb("topi", [P, 8], U32, c4)
            topf = sb("topf", [P, 8], F32, c4)
            mk = sb("mk", [P, 2, X], F32, c4)
            combs = sb("combs", [P, X], F32, c4)
            warm = sb("warm", [1, 1], F32, c4)
            cT = sb("cT", [X, P], F32, c4)
            hT = sb("hT", [P, 2, KD, P], F32, c4)
            psh = pb("psh", c4, (P, 1024))
            psS = pb("psS", c4)
            psE, psR, psI, psX = psS[:, 0:P], psS[:, P:P + 2 * HC], psS[:, 320:326], psS[:, 328:328 + HC]
            psW = pb("psW", c4)
            psT, psL, psC, psB = psW[:, 0:2 * P], psW[:, 2 * P:2 * P + X], psW[0:X, 3 * P:4 * P], psW[:, 0:D]
            ph = [pb(f"ph{e}", c4) for e in range(2)]
            py = [pb(f"py{e}", c4) for e in range(2)]
            s_use = sem("slots_summed")
            s_bank = sem("cell_banks_free")
            s_wt = sem("slots_selected")
            s_g = sem("rows_weighted")
            s_warm = sem("table_loads")
            s_ga = sem("rows_weighted_by_scalar")
            s_win = sem("cells_summed")
            s_z = sem("window_sums_cleared")
            s_st3 = sem("chunk_steps")
            s_t1 = sem("logits_turned")
            s_t2 = sem("segment_ends_turned")
            s_t3 = sem("carries_turned")
            s_t4 = sem("weights_turned")
            s_e1 = sem("logits_ready")
            s_e2 = sem("segment_ends_ready")
            s_e3 = sem("carries_ready")
            s_e4 = sem("maxima_subtracted")
            s_x1 = sem("rescale_exp_done")
            s_x2 = sem("weights_exp_done")
            s_x3 = sem("weights_placed")
            s_bf = sem("breaks_and_flags_ready")
            s_sv = sem("second_scan_steps")
            s_mg = sem("merge_steps")
            s_pv = sem("window_steps")
            s_xn2 = sem("window_normalized")
            s_pt = sem("window_turned")
            s_xt = sem("window_turned_copied")
            s_lg = sem("router_logits_done")
            s_sh = sem("router_shifted")
            s_ex = sem("router_exp_done")
            s_cm = sem("combine_ready")
            s_ct = sem("combine_turned")
            s_cc = sem("combine_copied")
            s_b2 = sem("bias_rows_done")
            s_h = sem("hidden_done")
            s_ge = sem("hidden_activated")
            s_y = sem("expert_rows_done")
            s_ya = sem("expert_rows_added")
            s_fw = sem("expert_weights_loaded")
            s_out = sem("output_stored")
            FW = 16 * (2 + 3 * KD)
            KW = 32
            PAIR = NC // 2 - 1
            WV = 4

            def windows(eng, done, hi, body):
                lo = eng.snap(done, min_val=0, max_val=NW - 1)
                with eng.If(lo < hi):
                    with eng.Fori(lo, hi) as wv:
                        body(nc.s_assert_within(wv, 0, NW - 2,
                                                skip_runtime_bounds_check_because="the last window comes later"))

                eng.reg_mov(done, hi)

            def last_windows(eng, done, body):
                with eng.Fori(eng.snap(done, min_val=0, max_val=NW - 1), NW) as wv:
                    body(nc.s_assert_within(wv, 0, NW - 1, skip_runtime_bounds_check_because="a window"))

            with nc.Block() as block:
                @block.gpsimd
                def _(eng):
                    eng.memset(comb[:, 0, :], 0.0).then_inc(s_z, 1)
                    eng.memset(combs[:, :], 0.0).then_inc(s_z, 1)
                    eng.memset(onesr[:, :], 1.0).then_inc(s_z, 1)

                    def quarter(i, q):
                        m = i * QUADS + q
                        eng.wait_ge(s_ir2, m + 1)
                        eng.wait_ge(s_use, m * HALF + HALF)
                        eng.wait_ge(s_e1, i * 2 + q // 2 + q % 2 + 1)
                        eng.tensor_tensor(ir2[:, (q + 1) % QUADS, :], el_idx[:, bass.ds((m + 1) * HALF, HALF)],
                                          zero_i[:, :], ALU.add).then_inc(s_ir2, 1)
                        for j in range(HALF):
                            eng.indirect_dma_start(G[q // 2][:, q % 2 * HALF + j, :], None, feat_rows,
                                                   bass.IndirectOffsetOnAxis(ap=ir2[:, q, j:j + 1], axis=0))\
                               .then_inc(s_gs[q // 2], 16)

                    for q in range(2, QUADS):
                        quarter(0, q)
                    with eng.Fori(1, NC // 2) as i:
                        for q in range(QUADS):
                            quarter(i, q)
                    for b in range(2):
                        eng.wait_ge(s_gs[b], (NC // 2) * C * 16)

                @block.sync
                def _(eng):
                    with nc.allow_non_contiguous_dma(reason="small transposed loads"):
                        eng.dma_start(b1s[:, :, :], b1.rearrange("e (k p) -> p e k", p=P)).then_inc(s_fw, 16)
                        for k in range(KD):
                            eng.dma_start(rws[:, k, :], router_w[:, k * P:(k + 1) * P].rearrange("e p -> p e"))\
                               .then_inc(s_fw, 16)
                    eng.dma_start(b2s[:, :], b2).then_inc(s_fw, 16)
                    for k in range(KD):
                        eng.dma_start(w1s[:, k, :, :], w1[:, k * P:(k + 1) * P, :].rearrange("e p d -> p e d"))\
                           .then_inc(s_fw, 16)
                        eng.dma_start(w2s[:, k, :, :], w2[:, k * P:(k + 1) * P, :].rearrange("e p d -> p e d"))\
                           .then_inc(s_fw, 16)
                    with eng.Fori(0, FULL) as w:
                        eng.wait_ge(s_ya, w * (X + 1) + 2 * (X + 1) + 2)
                        eng.dma_start(out[bass.ds(w * P, P), :], xbp[:, bass.ds(w + 1, 1), :]
                                      .rearrange("p a d -> p (a d)")).then_inc(s_out, 16)
                    eng.wait_ge(s_ya, (FULL + 2) * (X + 1) + 2)
                    eng.dma_start(out[FULL * P:N, :], xbp[0:REST, FULL + 1, :]).then_inc(s_out, 16)
                    eng.wait_ge(s_out, 16 * NW)

                @block.tensor
                def _(eng):
                    eng.wait_ge(s_z, 4)
                    cell = eng.alloc_register("open_cell")
                    done = eng.alloc_register("windows_done")
                    packed = eng.alloc_register("chunk_cells")
                    eng.reg_mov(cell, 0)
                    eng.reg_mov(done, 0)

                    def load_cells(c):
                        eng.reg_mov(packed, eng.value_load(chunk_cells[0:1, bass.ds(c, 1)], min_val=0,
                                                           max_val=2 ** (CP2 + 5) - 1))

                    def bank_of(at):
                        return psh[:, bass.ds((at & 1) * 512, ROW)]

                    def open_cell():
                        at = eng.snap(cell, min_val=0, max_val=NW + NC)
                        eng.wait_ge(s_bank, at + 1)
                        eng.matmul(bank_of(at), zero16[0:1, 0:P], zero16[0:1, :], start=True, stop=False)

                    def close_cell():
                        at = eng.snap(cell, min_val=0, max_val=NW + NC)
                        eng.matmul(bank_of(at), zero16[0:1, 0:P], zero16[0:1, :], start=False, stop=True)\
                           .then_inc(s_win, 1)
                        eng.reg_add(cell, cell, 1)

                    def turn_logits(c):
                        eng.wait_ge(s_e1, c + 3)
                        eng.transpose(psE[0:HC, :], elog[:, :, :].rearrange("p h s -> p (h s)"), ident[:, :])\
                           .then_inc(s_t1, 1)

                    def turn_ends(c):
                        eng.wait_ge(s_e2, c + 1)
                        eng.transpose(psR[0:1, 0:HC], fw[:, P - 1:P], ident[0:HC, 0:HC])
                        eng.transpose(psR[0:1, HC:2 * HC], bw[:, 0:1], ident[0:HC, 0:HC]).then_inc(s_t2, 1)

                    def turn_carries(c):
                        eng.wait_ge(s_e3, c + 1)
                        eng.wait_ge(s_x1, c + 1)
                        eng.matmul(psI[:, 2:2 + H], onesr[:, :], downe[:, :], start=True, stop=True)
                        for n in range(2):
                            tr = eng.transpose(psI[0:HC, n:n + 1], incr[:, n, :, :].rearrange("p h s -> p (h s)"),
                                               ident[0:1, 0:1])
                        tr.then_inc(s_t3, 1)

                    def turn_weights(c):
                        eng.wait_ge(s_x2, c + 1)
                        eng.transpose(psX, wrow[:, :], ident[0:HC, 0:HC]).then_inc(s_t4, 1)

                    steps = [turn_logits, turn_ends, turn_carries, turn_weights]

                    def window(r, w=None):
                        def up(e):
                            eng.wait_ge(s_ge, r * (2 * X) + 2 * e + 2)
                            for hh in range(KD):
                                for k in range(KD):
                                    mm = eng.matmul(ph[e % 2][:, hh * P:(hh + 1) * P],
                                                    w1s[:, k, e, hh * P:(hh + 1) * P],
                                                    hacc[:, bass.ds(r, 1), k * P:(k + 1) * P]
                                                    .rearrange("p a d -> p (a d)"),
                                                    start=(k == 0), stop=(k == KD - 1))
                            mm.then_inc(s_h, 1)

                        def down(e):
                            eng.wait_ge(s_ya, r * (X + 1) + e + (e > 3) + 1)
                            for hh in range(KD):
                                eng.wait_ge(s_ge, r * (2 * X) + 2 * e + hh + 5)
                                mm = eng.matmul(py[e % 2][:, 0:D], hT[:, e % 2, hh, :],
                                                w2s[:, hh, e, :], start=(hh == 0), stop=(hh == KD - 1))
                            mm.then_inc(s_y, 1)

                        up(0)
                        for e in range(X):
                            if e + 1 < X:
                                up(e + 1)
                            down(e)
                            if e == 0:
                                eng.wait_ge(s_cm, r + 1)
                                eng.transpose(psC, combs[:, :], ident[:, :]).then_inc(s_ct, 1)
                            if e == 1:
                                eng.wait_ge(s_cc, r + 1)
                                eng.matmul(psB, cT[:, :], b2s[:, :], start=True, stop=True).then_inc(s_b2, 1)
                            if w is None:
                                continue
                            if e == 4:
                                eng.wait_ge(s_xn2, w + 1)
                                for k in range(KD):
                                    tr = eng.transpose(psT[:, k * P:(k + 1) * P], xn2[:, k * P:(k + 1) * P],
                                                       ident[:, :])
                                tr.then_inc(s_pt, 1)
                            if e == 6:
                                eng.wait_ge(s_xt, w * 2 + 2)
                                for k in range(KD):
                                    mm = eng.matmul(psL, xts[:, k, :], rws[:, k, :],
                                                    start=(k == 0), stop=(k == KD - 1))
                                mm.then_inc(s_lg, 1)

                    def chunk(c, b, last=False):
                        now = eng.snap(packed, min_val=0, max_val=2 ** (CP2 + 5) - 1)
                        fresh = now >> 5
                        open_cell()
                        for q in range(CP2):
                            if q > 0:
                                with eng.If((fresh >> q) & 1):
                                    close_cell()
                                    open_cell()
                            at = eng.snap(cell, min_val=0, max_val=NW + NC)
                            if q % 2 == 0:
                                eng.wait_ge(s_wt, c * (CP2 // 2) + q // 2 + 1)
                                if q // 2 < WV:
                                    eng.wait_ge(s_g, c * WV + q // 2 + 1)
                                else:
                                    eng.wait_ge(s_ga, c * (C // 4 - WV) + q // 2 - WV + 1)
                            for u in range(2):
                                j = 2 * q + u
                                eng.matmul(bank_of(at), OH[:, j, :], G[b][:, j, :], start=False, stop=False)\
                                   .then_inc(s_use, 1)
                            if q == 9 and not last:
                                load_cells(c + 1)
                            if q >= 5 and q % 2 and not last:
                                steps[(q - 5) // 2](c + 1)
                        close_cell()
                        windows(eng, done, now & 31, lambda w: window(w, w))

                    load_cells(0)
                    for st in steps:
                        st(0)
                    eng.wait_ge(s_fw, FW)
                    with eng.Fori(0, PAIR) as i:
                        for b in range(2):
                            chunk(i * 2 + b, b)
                    chunk(NC - 2, 0)
                    chunk(NC - 1, 1, True)
                    last_windows(eng, done, lambda w: window(w, w))
                    window(NW)

                @block.scalar
                def _(eng):
                    eng.wait_ge(s_z, 4)
                    cell = eng.alloc_register("copied_cell")
                    win_of = eng.alloc_register("copied_window")
                    to = eng.alloc_register("copied_to")
                    done = eng.alloc_register("windows_done")
                    eng.reg_mov(done, 0)
                    eng.reg_mov(cell, 0)
                    eng.reg_mov(win_of, 0)

                    def copy_cell():
                        at = eng.snap(cell, min_val=0, max_val=NW + NC)
                        place = eng.snap(to, min_val=0, max_val=NW + 1)
                        eng.wait_ge(s_win, at + 1)
                        eng.copy(hacc[:, bass.ds(place, 1), :].rearrange("p a d -> p (a d)"),
                                 psh[:, bass.ds((at & 1) * 512, ROW)]).then_inc(s_bank, 1)
                        eng.reg_add(cell, cell, 1)

                    def breaks(c):
                        eng.wait_ge(s_sv, c * 5 + 5)
                        eng.copy(bkc[:, :], brkt[:, bass.ds(c, 1), :].rearrange("p a e -> p (a e)"))\
                           .then_inc(s_bf, 1)
                        eng.copy(flc[:, :, :], flag[:, :, bass.ds(c * C, C)]).then_inc(s_bf, 1)

                    def rescale(c):
                        eng.wait_ge(s_e3, c + 1)
                        eng.activation(downe[:, :], down_m[:, :], ACT.Exp, bias=zrow[0:1, 0:1]).then_inc(s_x1, 1)

                    def weights(c, b):
                        eng.wait_ge(s_e4, c + 1)
                        eng.activation(wrow[:, :], wrow[:, :], ACT.Exp, bias=zrow[0:HC, 0:1]).then_inc(s_x2, 1)
                        eng.wait_ge(s_t4, c + 1)
                        eng.copy(G[b][:, :, D:ROW].rearrange("p s h -> p h s"),
                                 psX.rearrange("p (h s) -> p h s", h=H)).then_inc(s_x3, 1)

                    def load_gelu():
                        eng.activation(warm[:, :], zrow[0:1, 0:1], ACT.Gelu, bias=zrow[0:1, 0:1]).then_inc(s_warm, 1)

                    def window(r, w=None):
                        load_gelu()
                        for e in range(X):
                            eng.wait_ge(s_y, r * X + e + 1)
                            eng.wait_ge(s_h, r * X + e + 1)
                            for hh in range(KD):
                                eng.activation(hT[:, e % 2, hh, :],
                                               ph[e % 2][:, hh * P:(hh + 1) * P],
                                               ACT.Gelu, bias=b1s[:, e, hh:hh + 1]).then_inc(s_ge, 1)
                            if e == 1:
                                eng.wait_ge(s_ct, r + 1)
                                eng.copy(cT[:, :], psC).then_inc(s_cc, 1)
                            if w is None:
                                continue
                            if e == 5:
                                eng.wait_ge(s_pt, w + 1)
                                turned = psT.rearrange("p (k n) -> p k n", k=KD)
                                eng.copy(xts[:, :, :], turned).then_inc(s_xt, 1)
                                eng.copy(hacc[:, bass.ds(w + 1, 1), 0:D].rearrange("p a (k n) -> p (a k) n", k=KD),
                                         turned).then_inc(s_xt, 1)
                            if e == 7:
                                eng.wait_ge(s_sh, w + 1)
                                eng.activation(prob[:, :], prob[:, :], ACT.Exp, bias=zrow[:, 0:1]).then_inc(s_ex, 1)

                    def chunk(c, b, last=False):
                        now = eng.value_load(chunk_cells[0:1, bass.ds(c, 1)], min_val=0, max_val=2 ** (CP2 + 5) - 1)
                        fresh = now >> 5
                        eng.reg_add(win_of, win_of, fresh & 1)
                        eng.reg_mov(to, STAGE)
                        eng.wait_ge(s_mg, c * 3 + 3)
                        if not last:
                            breaks(c + 1)
                        eng.wait_ge(s_x3, c + 1)
                        for j in range(4 * WV, C):
                            for h in range(H):
                                ws = eng.activation(G[b][:, j, h * HD:(h + 1) * HD], G[b][:, j, h * HD:(h + 1) * HD],
                                                    ACT.Copy, scale=G[b][:, j, D + h:D + h + 1])
                            if j % 4 == 3:
                                ws.then_inc(s_ga, 1)
                        for q in range(CP2):
                            if q > 0:
                                with eng.If((fresh >> q) & 1):
                                    copy_cell()
                                    eng.reg_add(win_of, win_of, 1)
                                    eng.reg_add(to, win_of, 1)
                            if last:
                                continue
                            if q == 9:
                                rescale(c + 1)
                            if q == 11:
                                weights(c + 1, 1 - b)
                        copy_cell()
                        windows(eng, done, now & 31, lambda w: window(w, w))

                    breaks(0)
                    rescale(0)
                    weights(0, 0)
                    with eng.Fori(0, PAIR) as i:
                        for b in range(2):
                            chunk(i * 2 + b, b)
                    chunk(NC - 2, 0)
                    chunk(NC - 1, 1, True)
                    last_windows(eng, done, lambda w: window(w, w))
                    window(NW)

                @block.vector
                def _(eng):
                    eng.engine_nop().then_inc(s_use, RING)
                    eng.engine_nop().then_inc(s_bank, 2)
                    eng.engine_nop().then_inc(s_e1, 2)
                    eng.engine_nop().then_inc(s_mg, 3)
                    eng.engine_nop().then_inc(s_sv, 5)
                    eng.engine_nop().then_inc(s_cm, 1)
                    eng.engine_nop().then_inc(s_ge, 4)
                    eng.engine_nop().then_inc(s_y, 2)
                    eng.engine_nop().then_inc(s_ya, 2)
                    eng.memset(hacc[:, :, :], 0.0).then_inc(s_z, 1)
                    done = eng.alloc_register("windows_done")
                    eng.reg_mov(done, 0)
                    K = 15
                    eng.memset(ends[:, :, 0:1], -BIG).then_inc(s_st3, 1)
                    eng.memset(begs[:, :, C:C + 1], -BIG).then_inc(s_st3, 1)
                    eng.wait_ge(s_z, 4)

                    n = [0]

                    def step(ins):
                        ins.then_inc(s_st3, 1)
                        n[0] += 1

                    def logits(c, b, i):
                        n[0] = 0
                        eng.wait_ge(s_gs[b], i * (C * 16) + C * 16)
                        step(eng.tensor_tensor(eraw[:, :, :], G[b][:, :, D:ROW],
                                               er_all[:, bass.ds(c * C, C), :], ALU.add))
                        eng.wait_ge(s_st3, c * K + n[0] + 2)
                        eng.scalar_tensor_tensor(elog[:, :, :].rearrange("p h s -> p s h"), eraw[:, :, :], 0.2,
                                                 eraw[:, :, :], ALU.mult, ALU.max).then_inc(s_e1, 1)

                    def row_maxima(c, b, i):
                        eng.wait_ge(s_bf, c * 2 + 2)
                        eng.wait_ge(s_t1, c + 1)
                        step(eng.tensor_tensor_scan(fw[:, :], bkc[:, 0:P], psE[0:HC, :], -BIG, ALU.add, ALU.max))
                        eng.tensor_tensor_scan(bw[:, ::-1], bkc[:, P:0:-1], psE[0:HC, ::-1], -BIG,
                                               ALU.add, ALU.max).then_inc(s_e2, 1)

                    def carries(c, b, i):
                        eng.wait_ge(s_t2, c + 1)
                        for h in range(H):
                            step(eng.tensor_tensor_scan(ends[:, h, 1:C + 1], flc[:, 1, :], psR[0:1, h * C:(h + 1) * C],
                                                        ends[:, h, 0:1], ALU.add, ALU.max))
                            step(eng.tensor_tensor_scan(begs[:, h, C - 1::-1], flc[:, 2, ::-1],
                                                        psR[0:1, HC + h * C:HC + (h + 1) * C][:, ::-1], -BIG,
                                                        ALU.add, ALU.max))
                        eng.wait_ge(s_st3, c * K + n[0] + 2)
                        step(eng.tensor_tensor(down_m[:, :], ends[:, :, 0], begs[:, :, 0], ALU.max))
                        step(eng.tensor_tensor(incr[:, 0, :, :], ends[:, :, 0:C],
                                               flc[:, 0:1, :].to_broadcast([1, H, C]), ALU.add))
                        step(eng.tensor_tensor(incr[:, 1, :, :], begs[:, :, 1:C + 1],
                                               flc[:, 3:4, :].to_broadcast([1, H, C]), ALU.add))
                        eng.wait_ge(s_st3, c * K + n[0] + 2)
                        eng.tensor_tensor(down_m[:, :], ends[:, :, 0], down_m[:, :], ALU.subtract).then_inc(s_e3, 1)
                        eng.wait_ge(s_e3, c + 1)
                        step(eng.tensor_copy(ends[:, :, 0:1], ends[:, :, C:C + 1]))

                    def shifted(c, b, i):
                        eng.wait_ge(s_t3, c + 1)
                        step(eng.tensor_copy(inc[:, :], psI[0:HC, 0:2]))
                        assert n[0] == K, n
                        eng.wait_ge(s_st3, c * K + n[0] + 2)
                        eng.tensor_scalar(resc[:, b, :], psI[:, 2:2 + H], 1.0, cross[:, bass.ds(c, 1)],
                                          ALU.subtract, ALU.mult).then_inc(s_sv, 1)
                        eng.tensor_tensor_scan(fw[:, :], bkc[:, 0:P], psE[0:HC, :], inc[:, 0:1],
                                               ALU.add, ALU.max).then_inc(s_sv, 1)
                        eng.tensor_tensor_scan(bw[:, ::-1], bkc[:, P:0:-1], psE[0:HC, ::-1], inc[:, 1:2],
                                               ALU.add, ALU.max).then_inc(s_sv, 1)
                        eng.wait_ge(s_sv, c * 5 + 8)
                        eng.tensor_scalar(resc[:, b, :], resc[:, b, :], 1.0, None, ALU.add).then_inc(s_sv, 1)
                        eng.tensor_tensor(fw[:, :], fw[:, :], bw[:, :], ALU.max).then_inc(s_sv, 1)
                        eng.wait_ge(s_sv, c * 5 + 10)
                        eng.tensor_tensor(wrow[:, :], psE[0:HC, :], fw[:, :], ALU.subtract).then_inc(s_e4, 1)

                    steps = [logits, row_maxima, carries, shifted]

                    def places(c, q):
                        eng.wait_ge(s_use, c * C + 4 * q + 4 + RING - C)
                        eng.tensor_tensor(OH[:, 4 * q:4 * q + 4, :],
                                          iota_f[:, :].unsqueeze(1).to_broadcast([P, 4, P]),
                                          dloc[:, bass.ds(c * C + 4 * q, 4)].unsqueeze(2).to_broadcast([P, 4, P]),
                                          ALU.is_equal).then_inc(s_wt, 1)

                    def weigh(c, b, q):
                        eng.wait_ge(s_x3, c + 1)
                        j = 4 * q
                        g = G[b][:, j:j + 4, 0:D].rearrange("p s (h d) -> p s h d", h=H)
                        eng.tensor_tensor(g, g, G[b][:, j:j + 4, D:ROW].unsqueeze(3).to_broadcast([P, 4, H, HD]),
                                          ALU.mult).then_inc(s_g, 1)

                    def window(r, w=None):
                        m = [0]

                        def do(ins, last=True):
                            ins.then_inc(s_pv, 1)
                            m[0] += 1
                            if last:
                                eng.wait_ge(s_pv, w * KW + m[0])

                        def add(e):
                            acc = xbp[:, bass.ds(r, 1), :].rearrange("p a d -> p (a d)")
                            eng.wait_ge(s_y, r * X + e + 3)
                            eng.wait_ge(s_ya, r * (X + 1) + e + (e > 1) + 2)
                            eng.scalar_tensor_tensor(acc, py[e % 2][:, 0:D],
                                                     comb[:, bass.ds(r, 1), e], acc,
                                                     ALU.mult, ALU.add).then_inc(s_ya, 1)

                        def add_biases():
                            acc = xbp[:, bass.ds(r, 1), :].rearrange("p a d -> p (a d)")
                            eng.wait_ge(s_b2, r + 1)
                            eng.wait_ge(s_ya, r * (X + 1) + 4)
                            eng.tensor_tensor(acc, acc, psB, ALU.add).then_inc(s_ya, 1)

                        if w is None:
                            for e in range(X):
                                add(e)
                                if e == 1:
                                    add_biases()
                            return
                        res = xbp[:, bass.ds(w + 1, 1), :].rearrange("p a d -> p (a d)")
                        add(0)
                        do(eng.tensor_scalar(den[:, :], hacc[:, bass.ds(w + 1, 1), D:ROW]
                                             .rearrange("p a h -> p (a h)"), 0.5, None, ALU.max))
                        do(eng.reciprocal(den[:, :], den[:, :]))
                        do(eng.tensor_tensor(xr[:, :].rearrange("p (h d) -> p h d", h=H),
                                             hacc[:, bass.ds(w + 1, 1), 0:D].rearrange("p a (h d) -> p (a h) d", h=H),
                                             den[:, :].unsqueeze(2).to_broadcast([P, H, HD]), ALU.mult))
                        do(eng.tensor_tensor(xr[:, :], xr[:, :], res, ALU.add))
                        do(eng.bn_stats(stat2[:, :], xr[:, :]))
                        eng.memset(rq[:, :], 0.0)
                        do(eng.bn_aggr(mv2[:, :], stat2[:, :]))
                        add(1)
                        do(eng.tensor_scalar(ve[:, :], mv2[:, 1:2], EPS, None, ALU.add))
                        do(eng.tensor_scalar(guess[:, :], ve[:, :].bitcast(I32), -0.5, float(0x5f3759df),
                                             ALU.mult, ALU.add))
                        y = guess[:, :].bitcast(F32)
                        for it in range(3):
                            if it == 1:
                                add_biases()
                                add(2)
                            do(eng.scalar_tensor_tensor(rq[:, :], y, y, ve[:, :], ALU.mult, ALU.mult))
                            do(eng.tensor_scalar(rq[:, :], rq[:, :], -0.5, 1.5, ALU.mult, ALU.add))
                            do(eng.tensor_tensor(rs[:, :], y, rq[:, :], ALU.mult))
                            y = rs[:, :]
                        eng.tensor_scalar(xn2[:, :], xr[:, :], mv2[:, 0:1], rs[:, 0:1], ALU.subtract, ALU.mult)\
                           .then_inc(s_xn2, 1)
                        eng.wait_ge(s_xn2, w + 1)
                        add(3)
                        do(eng.tensor_tensor(res, xr[:, :], xn2[:, :], ALU.add))
                        for e in range(4, 7):
                            add(e)
                        eng.wait_ge(s_lg, w + 1)
                        do(eng.tensor_reduce(pm[:, :], psL, AX, ALU.max))
                        eng.tensor_scalar(prob[:, :], psL, pm[:, 0:1], None, ALU.subtract).then_inc(s_sh, 1)
                        add(7)
                        eng.wait_ge(s_ex, w + 1)
                        do(eng.tensor_reduce(pm[:, :], prob[:, :], AX, ALU.add))
                        do(eng.reciprocal(pm[:, :], pm[:, :]))
                        do(eng.tensor_scalar(prob[:, :], prob[:, :], pm[:, 0:1], None, ALU.mult))
                        eng.memset(rq[:, :], 0.0)
                        do(eng.max(top[:, :], prob[:, :]))
                        eng.memset(rq[:, :], 0.0)
                        do(eng.max_index(topi[:, :], top[:, :], prob[:, :]))
                        do(eng.tensor_copy(topf[:, :], topi[:, :]))
                        do(eng.tensor_tensor(mk[:, :, :], iota_f[:, 0:X].unsqueeze(1).to_broadcast([P, 2, X]),
                                             topf[:, 0:2].unsqueeze(2).to_broadcast([P, 2, X]), ALU.is_equal), False)
                        do(eng.tensor_tensor(pm[:, :], top[:, 0:1], top[:, 1:2], ALU.add))
                        do(eng.tensor_tensor(mk[:, 0, :], mk[:, 0, :], mk[:, 1, :], ALU.add), False)
                        do(eng.tensor_scalar(pm[:, :], pm[:, :], 1e-12, None, ALU.max))
                        do(eng.reciprocal(pm[:, :], pm[:, :]), False)
                        do(eng.tensor_tensor(mk[:, 0, :], mk[:, 0, :], prob[:, :], ALU.mult))
                        eng.tensor_scalar(combs[:, :], mk[:, 0, :], pm[:, 0:1], None, ALU.mult).then_inc(s_cm, 1)
                        eng.wait_ge(s_cm, w + 2)
                        do(eng.tensor_copy(comb[:, bass.ds(w + 1, 1), :].rearrange("p a e -> p (a e)"), combs[:, :]))
                        assert m[0] == KW, m

                    def chunk(c, b, i, last=False):
                        for q in range(C // 4):
                            if q == 0:
                                places(c, 2)
                                weigh(c, b, 3)
                            if q == 5:
                                info = eng.value_load(chunk_info[0:1, bass.ds(c, 1)], min_val=0, max_val=2 ** 15 - 1)
                            if q >= 2 and not last:
                                steps[q - 2](c + 1, 1 - b, i + b)
                            if 2 <= q < 5:
                                places(c, q + 1)
                        if not last:
                            for q in range(2):
                                places(c + 1, q)
                            weigh(c + 1, 1 - b, 0)
                        first = nc.s_assert_within(info & 31, 0, NW - 1,
                                                   skip_runtime_bounds_check_because="a window")
                        acc = hacc[:, bass.ds(first + 1, 1), :]
                        eng.wait_ge(s_bank, ((info >> 5) & 31) + (info >> 10) + 3)
                        eng.tensor_tensor(acc[:, :, 0:D].rearrange("p a (h d) -> p (a h) d", h=H),
                                          acc[:, :, 0:D].rearrange("p a (h d) -> p (a h) d", h=H),
                                          resc[:, b, :].unsqueeze(2).to_broadcast([P, H, HD]),
                                          ALU.mult).then_inc(s_mg, 1)
                        eng.tensor_tensor(acc[:, :, D:ROW].rearrange("p a h -> p (a h)"),
                                          acc[:, :, D:ROW].rearrange("p a h -> p (a h)"), resc[:, b, :],
                                          ALU.mult).then_inc(s_mg, 1)
                        eng.wait_ge(s_mg, c * 3 + 5)
                        eng.tensor_tensor(acc, acc, hacc[:, STAGE:STAGE + 1, :], ALU.add).then_inc(s_mg, 1)
                        eng.wait_ge(s_mg, c * 3 + 6)
                        if not last:
                            for q in range(1, 3):
                                weigh(c + 1, 1 - b, q)
                        windows(eng, done, info & 31, lambda w: window(w, w))

                    for q in range(2):
                        places(0, q)
                    for st in steps:
                        st(0, 0, 0)
                    for q in range(3):
                        weigh(0, 0, q)
                    with eng.Fori(0, PAIR) as i:
                        for b in range(2):
                            chunk(i * 2 + b, b, i)
                    chunk(NC - 2, 0, PAIR)
                    chunk(NC - 1, 1, PAIR, True)
                    last_windows(eng, done, lambda w: window(w, w))
                    window(NW)
                    eng.wait_ge(s_g, NC * WV)
                    eng.wait_ge(s_ya, (NW + 1) * (X + 1) + 2)


_INS = ['x', 'src', 'dst', 'edge_type_8', 'L0_gnn_conv_weights', 'L0_gnn_attn_l', 'L0_gnn_attn_r', 'L0_gnn_h_bias',
        'L0_ffn_router_w', 'L0_ffn_w1', 'L0_ffn_b1', 'L0_ffn_w2', 'L0_ffn_b2']
_OUTS = [((3750, 256), 'float32')]


def kernel(**inputs):
    import numpy as _np
    import concourse.bacc as _bacc
    from concourse import mybir as _mybir
    from concourse.bass_utils import run_bass_kernel_spmd as _run

    nc = _bacc.Bacc("TRN2", target_bir_lowering=False, num_devices=1)
    arrays, args = {}, []
    for name in _INS:
        a = _np.ascontiguousarray(inputs[name])
        arrays[f"in_{name}_dram"] = a
        args.append(nc.dram_tensor(f"in_{name}_dram", a.shape, _mybir.dt.from_np(a.dtype), kind="ExternalInput").ap())
    for i, (shape, dtype) in enumerate(_OUTS):
        dt = _mybir.dt.from_np(_np.dtype(dtype))
        args.append(nc.dram_tensor(f"out_{i}_dram", shape, dt, kind="ExternalOutput").ap())
    gnn_moe(nc, *args)
    r = _run(nc, [arrays], core_ids=[0])
    got = tuple(r.results[0][f"out_{i}_dram"] for i in range(len(_OUTS)))
    return got[0]
```
